# Optimizing a Trainium2 kernel written in Bass

```python
import numpy as np
import jax
import jax.numpy as jnp

def _softmax(x, axis=-1):
    return jax.nn.softmax(x, axis=axis)

def _gelu(x):
    return jax.nn.gelu(x, approximate=True)

def _silu(x):
    return jax.nn.silu(x)

def _sigmoid(x):
    return jax.nn.sigmoid(x)

def _layernorm(x, axis=-1, eps=1e-05):
    m = jnp.mean(x, axis=axis, keepdims=True)
    v = jnp.var(x, axis=axis, keepdims=True)
    return (x - m) / jnp.sqrt(v + eps)

def _scatter_add(tgt, idx, src, axis=0):
    return tgt.at[idx].add(src)

def _segment_sum(src, seg, n):
    return jax.ops.segment_sum(src, seg, n)
kernel_name = 'mk_gnn_ffn_d4_gnn_r16_82cfac'

def setup_inputs(seed: int=0):
    np.random.seed(seed)
    _w = jnp.asarray

    def _rec_inputs():
        import jax
        import jax.numpy as jnp
        _gk = jax.random.key(seed)
        x = -0.0003713 + 1 * jax.random.normal(jax.random.fold_in(_gk, 1), (3125, 256), jnp.float32)
        src = jax.random.randint(jax.random.fold_in(_gk, 2), (100000,), 0, 3125, jnp.int32)
        dst = jax.random.randint(jax.random.fold_in(_gk, 3), (100000,), 0, 3125, jnp.int32)
        _o = jnp.argsort(dst, stable=True)
        src = src[_o]
        dst = dst[_o]
        edge_weight = -0.000423496 + 0.100023 * jax.random.normal(jax.random.fold_in(_gk, 13), (100000,), jnp.float32)
        return (x, src, dst, edge_weight)
    x, src, dst, edge_weight = _rec_inputs()

    def _L0_gnn_setup():
        import jax, jax.numpy as jnp
        import numpy as np
        N_NODES = 3125
        D = 256
        L = 2
        N_EDGES = 50000
        NEG_SLOPE = 0.2

        def _gat_conv(h, W_l, al, ar, b, src, dst, n):
            hp = h @ W_l
            el = hp @ al
            er = hp @ ar
            e = jax.nn.leaky_relu(el[src] + er[dst], NEG_SLOPE)
            emax = jax.ops.segment_max(e, dst, num_segments=n)
            ex = jnp.exp(e - emax[dst])
            denom = jax.ops.segment_sum(ex, dst, num_segments=n)
            alpha = ex / denom[dst]
            out = jax.ops.segment_sum(hp[src] * alpha[:, None], dst, num_segments=n)
            return out + b
        key = jax.random.key(seed)
        ks = jax.random.split(key, 8)
        x = jax.random.normal(ks[0], (N_NODES, D), dtype=jnp.float32)
        W = jax.random.normal(ks[1], (L, D, D), dtype=jnp.float32) * (1.0 / np.sqrt(D))
        attn_l = jax.random.normal(ks[2], (L, D), dtype=jnp.float32) * (1.0 / np.sqrt(D))
        attn_r = jax.random.normal(ks[3], (L, D), dtype=jnp.float32) * (1.0 / np.sqrt(D))
        bias = jnp.zeros((L, D), dtype=jnp.float32)
        src = jax.random.randint(ks[4], (N_EDGES,), 0, N_NODES, dtype=jnp.int32)
        dst = jax.random.randint(ks[5], (N_EDGES,), 0, N_NODES, dtype=jnp.int32)
        return {'x': x, 'W': W, 'attn_l': attn_l, 'attn_r': attn_r, 'bias': bias, 'src': src, 'dst': dst}
    _L0_gnn_all = _L0_gnn_setup()
    _L0_gnn_in = {k: v for k, v in _L0_gnn_all.items() if k in ('W', 'attn_l', 'attn_r', 'bias')}
    del _L0_gnn_all

    def _L0_ffn_setup():
        import jax, jax.numpy as jnp
        import numpy as np
        B, S, D, E, H, K = (4, 256, 256, 8, 512, 2)
        key = jax.random.key(seed)
        ks = jax.random.split(key, 6)
        x = jax.random.normal(ks[0], (B, S, D), jnp.float32)
        Wg = jax.random.normal(ks[1], (D, E), jnp.float32) * 0.02
        bg = jnp.zeros((E,), jnp.float32)
        W1 = jax.random.normal(ks[2], (E, D, H), jnp.float32) * 0.02
        b1 = jnp.zeros((E, H), jnp.float32)
        W2 = jax.random.normal(ks[3], (E, H, D), jnp.float32) * 0.02
        b2 = jnp.zeros((E, D), jnp.float32)
        return {'x': x, 'Wg': Wg, 'bg': bg, 'W1': W1, 'b1': b1, 'W2': W2, 'b2': b2}
    _L0_ffn_all = _L0_ffn_setup()
    _L0_ffn_in = {k: v for k, v in _L0_ffn_all.items() if k in ('Wg', 'bg', 'W1', 'b1', 'W2', 'b2')}
    del _L0_ffn_all

    def _L1_gnn_setup():
        import jax, jax.numpy as jnp
        import numpy as np
        BLOCK_DIMS = [8] * 32

        def _mask_indices():
            d = sum(BLOCK_DIMS)
            mask = np.ones((d, d), dtype=np.int8)
            off = 0
            for b in BLOCK_DIMS:
                mask[off:off + b, off:off + b] = 0
                off += b
            rows, cols = np.nonzero(mask)
            return (d, rows.astype(np.int32), cols.astype(np.int32))
        key = jax.random.key(seed)
        k1, k2 = jax.random.split(key)
        d, rows, cols = _mask_indices()
        N = 31250
        X = jax.random.normal(k1, (N, d), dtype=jnp.float32)
        w_est = 0.1 * jax.random.normal(k2, (rows.shape[0],), dtype=jnp.float32)
        return {'X': X, 'w_est': w_est, 'rows': jnp.asarray(rows), 'cols': jnp.asarray(cols)}
    _L1_gnn_all = _L1_gnn_setup()
    _L1_gnn_in = {k: v for k, v in _L1_gnn_all.items() if k in ()}
    del _L1_gnn_all

    def _L1_ffn_setup():
        import jax, jax.numpy as jnp
        import numpy as np
        B, N, D = (16, 256, 256)
        NUM_EXPERTS, TOP_K, HEADS = (4, 2, 4)
        N_EDGES = 65536
        LN_EPS = 1e-05

        def _layernorm(x, g, b):
            mu = x.mean(-1, keepdims=True)
            var = ((x - mu) ** 2).mean(-1, keepdims=True)
            return (x - mu) * jax.lax.rsqrt(var + LN_EPS) * g + b

        def _forward(x, edge_index, W_gat, att_src, att_dst, b_gat, ln_gamma, ln_beta, W1, b1, W2, b2):
            Bc, Nc, Dc = x.shape
            M = Bc * Nc
            x_flat = x.reshape(M, Dc)
            h = (x_flat @ W_gat).reshape(M, HEADS, NUM_EXPERTS)
            loops = jnp.arange(M, dtype=edge_index.dtype)
            src = jnp.concatenate([edge_index[0], loops])
            dst = jnp.concatenate([edge_index[1], loops])
            a_src = (h * att_src).sum(-1)
            a_dst = (h * att_dst).sum(-1)
            e = jax.nn.leaky_relu(a_src[src] + a_dst[dst], negative_slope=0.2)
            e_max = jax.ops.segment_max(e, dst, num_segments=M)
            ee = jnp.exp(e - e_max[dst])
            denom = jax.ops.segment_sum(ee, dst, num_segments=M)
            alpha = ee / (denom[dst] + 1e-16)
            msg = h[src] * alpha[:, :, None]
            agg = jax.ops.segment_sum(msg, dst, num_segments=M).reshape(M, HEADS * NUM_EXPERTS) + b_gat
            scores = _layernorm(agg, ln_gamma, ln_beta).reshape(M, HEADS, NUM_EXPERTS).mean(1)
            scores = scores.reshape(Bc, Nc, NUM_EXPERTS)
            topk_s, topk_i = jax.lax.top_k(scores, TOP_K)
            w = jax.nn.softmax(topk_s, axis=-1)
            out = jnp.zeros_like(x)
            for ei in range(NUM_EXPERTS):
                g = jnp.where(topk_i == ei, w, 0.0).sum(-1)
                hh = jax.nn.gelu(x @ W1[ei] + b1[ei], approximate=False)
                out = out + g[..., None] * (hh @ W2[ei] + b2[ei])
            return out
        key = jax.random.key(seed)
        ks = jax.random.split(key, 8)
        s = 0.05
        return {'x': jax.random.normal(ks[0], (B, N, D), jnp.float32), 'W_gat': jax.random.normal(ks[1], (D, HEADS * NUM_EXPERTS), jnp.float32) * s, 'att_src': jax.random.normal(ks[2], (HEADS, NUM_EXPERTS), jnp.float32) * s, 'att_dst': jax.random.normal(ks[3], (HEADS, NUM_EXPERTS), jnp.float32) * s, 'b_gat': jnp.zeros((HEADS * NUM_EXPERTS,), jnp.float32), 'ln_gamma': jnp.ones((HEADS * NUM_EXPERTS,), jnp.float32), 'ln_beta': jnp.zeros((HEADS * NUM_EXPERTS,), jnp.float32), 'W1': jax.random.normal(ks[4], (NUM_EXPERTS, D, 2 * D), jnp.float32) * s, 'b1': jnp.zeros((NUM_EXPERTS, 2 * D), jnp.float32), 'W2': jax.random.normal(ks[5], (NUM_EXPERTS, 2 * D, D), jnp.float32) * s, 'b2': jnp.zeros((NUM_EXPERTS, D), jnp.float32), 'edge_index': jax.random.randint(ks[6], (2, N_EDGES), 0, B * N, jnp.int32)}
    _L1_ffn_all = _L1_ffn_setup()
    _L1_ffn_in = {k: v for k, v in _L1_ffn_all.items() if k in ('W_gat', 'att_src', 'att_dst', 'b_gat', 'ln_gamma', 'ln_beta', 'W1', 'b1', 'W2', 'b2', 'edge_index')}
    del _L1_ffn_all

    def _L2_gnn_setup():
        import jax, jax.numpy as jnp
        import numpy as np
        N_NODES = 1250
        N_EDGES = 20000
        EMB = 256
        key = jax.random.key(seed)
        k_h, k_s, k_d, k_w1, k_w2, k_b1, k_b2 = jax.random.split(key, 7)
        h = jax.random.normal(k_h, (N_NODES, EMB), dtype=jnp.float32)
        src = jax.random.randint(k_s, (N_EDGES,), 0, N_NODES, dtype=jnp.int32)
        dst = jax.random.randint(k_d, (N_EDGES,), 0, N_NODES, dtype=jnp.int32)
        gain = float(np.sqrt(2.0))
        std = gain * float(np.sqrt(2.0 / (EMB + EMB)))
        W_nb = jax.random.normal(k_w1, (EMB, EMB), dtype=jnp.float32) * std
        W_self = jax.random.normal(k_w2, (EMB, EMB), dtype=jnp.float32) * std
        b_nb = jax.random.uniform(k_b1, (EMB,), dtype=jnp.float32, minval=-0.06, maxval=0.06)
        b_self = jax.random.uniform(k_b2, (EMB,), dtype=jnp.float32, minval=-0.06, maxval=0.06)
        return {'h': h, 'W_nb': W_nb, 'b_nb': b_nb, 'W_self': W_self, 'b_self': b_self, 'src': src, 'dst': dst}
    _L2_gnn_all = _L2_gnn_setup()
    _L2_gnn_in = {k: v for k, v in _L2_gnn_all.items() if k in ('W_nb', 'b_nb', 'W_self', 'b_self')}
    del _L2_gnn_all

    def _L2_ffn_setup():
        import jax, jax.numpy as jnp
        import numpy as np
        E, D, H, TOP_K = (6, 256, 256, 2)
        ROUTER_H = D // 2
        key = jax.random.key(seed)
        ks = jax.random.split(key, 12)
        s = 1.0 / np.sqrt(D)
        sh = 1.0 / np.sqrt(H)
        sr = 1.0 / np.sqrt(ROUTER_H)
        return {'features': jax.random.normal(ks[0], (8, 256, D), dtype=jnp.float32), 'router_w1': jax.random.uniform(ks[1], (D, ROUTER_H), jnp.float32, -s, s), 'router_b1': jnp.zeros((ROUTER_H,), jnp.float32), 'router_w2': jax.random.uniform(ks[2], (ROUTER_H, E), jnp.float32, -sr, sr), 'router_b2': jnp.zeros((E,), jnp.float32), 'expert_w1': jax.random.uniform(ks[3], (E, D, H), jnp.float32, -s, s), 'expert_b1': jnp.zeros((E, H), jnp.float32), 'expert_w2': jax.random.uniform(ks[4], (E, H, H), jnp.float32, -sh, sh), 'expert_b2': jnp.zeros((E, H), jnp.float32), 'expert_w3': jax.random.uniform(ks[5], (E, H, D), jnp.float32, -sh, sh), 'expert_b3': jnp.zeros((E, D), jnp.float32)}
    _L2_ffn_all = _L2_ffn_setup()
    _L2_ffn_in = {k: v for k, v in _L2_ffn_all.items() if k in ('router_w1', 'router_b1', 'router_w2', 'router_b2', 'expert_w1', 'expert_b1', 'expert_w2', 'expert_b2', 'expert_w3', 'expert_b3')}
    del _L2_ffn_all

    def _L3_gnn_setup():
        import jax, jax.numpy as jnp
        import numpy as np
        N_NODES = 3125
        N_EDGES = 100000
        H_SIZE = 256
        HEADS = 8
        HEAD_DIM = H_SIZE // HEADS
        NEG_SLOPE = 0.2
        key = jax.random.key(seed)
        k_x, k_e, k_w, k_as, k_ad, k_b = jax.random.split(key, 6)
        x = jax.random.normal(k_x, (N_NODES, H_SIZE), dtype=jnp.float32)
        edge_index = jax.random.randint(k_e, (2, N_EDGES), 0, N_NODES, dtype=jnp.int64)
        scale = 1.0 / np.sqrt(H_SIZE)
        W = jax.random.normal(k_w, (H_SIZE, HEADS, HEAD_DIM), dtype=jnp.float32) * scale
        att_src = jax.random.normal(k_as, (HEADS, HEAD_DIM), dtype=jnp.float32) * scale
        att_dst = jax.random.normal(k_ad, (HEADS, HEAD_DIM), dtype=jnp.float32) * scale
        bias = jnp.zeros((H_SIZE,), dtype=jnp.float32)
        return {'x': x, 'edge_index': edge_index, 'W': W, 'att_src': att_src, 'att_dst': att_dst, 'bias': bias}
    _L3_gnn_all = _L3_gnn_setup()
    _L3_gnn_in = {k: v for k, v in _L3_gnn_all.items() if k in ('W', 'att_src', 'att_dst', 'bias')}
    del _L3_gnn_all

    def _L3_ffn_setup():
        import jax, jax.numpy as jnp
        import numpy as np
        NUM_EXPERTS = 8
        TOP_K = 2
        B, S, D = (8, 512, 256)

        def _moe(tokens, router_w, w1, b1, w2, b2):
            N = tokens.shape[0]
            E = router_w.shape[0]
            logits = tokens.astype(jnp.float32) @ router_w.astype(jnp.float32).T
            probs = jax.nn.softmax(logits, axis=-1)
            rw, re = jax.lax.top_k(probs, TOP_K)
            if TOP_K > 1:
                rw = rw / jnp.maximum(rw.sum(-1, keepdims=True), 1e-12)
            rw = rw.astype(tokens.dtype)
            combine = jnp.zeros((N, E), tokens.dtype).at[jnp.arange(N)[:, None], re].set(rw)
            out = tokens
            for e in range(E):
                h = jax.nn.gelu(tokens @ w1[e] + b1[e], approximate=False)
                y = h @ w2[e] + b2[e]
                out = out + combine[:, e:e + 1] * y
            return out
        key = jax.random.key(seed)
        ks = jax.random.split(key, 4)
        scale = 1.0 / np.sqrt(D).astype(np.float32)
        return {'input_embeddings': jax.random.normal(ks[0], (B, S, D), jnp.float32), 'router_w': jax.random.normal(ks[1], (NUM_EXPERTS, D), jnp.float32) * scale, 'w1': jax.random.normal(ks[2], (NUM_EXPERTS, D, D), jnp.float32) * scale, 'b1': jnp.zeros((NUM_EXPERTS, D), jnp.float32), 'w2': jax.random.normal(ks[3], (NUM_EXPERTS, D, D), jnp.float32) * scale, 'b2': jnp.zeros((NUM_EXPERTS, D), jnp.float32)}
    _L3_ffn_all = _L3_ffn_setup()
    _L3_ffn_in = {k: v for k, v in _L3_ffn_all.items() if k in ('router_w', 'w1', 'b1', 'w2', 'b2')}
    del _L3_ffn_all
    return {'x': x, 'src': src, 'dst': dst, 'edge_weight': edge_weight, 'L0_gnn_W': _L0_gnn_in['W'], 'L0_gnn_attn_l': _L0_gnn_in['attn_l'], 'L0_gnn_attn_r': _L0_gnn_in['attn_r'], 'L0_gnn_bias': _L0_gnn_in['bias'], 'L0_ffn_Wg': _L0_ffn_in['Wg'], 'L0_ffn_bg': _L0_ffn_in['bg'], 'L0_ffn_W1': _L0_ffn_in['W1'], 'L0_ffn_b1': _L0_ffn_in['b1'], 'L0_ffn_W2': _L0_ffn_in['W2'], 'L0_ffn_b2': _L0_ffn_in['b2'], 'L1_ffn_W_gat': _L1_ffn_in['W_gat'], 'L1_ffn_att_src': _L1_ffn_in['att_src'], 'L1_ffn_att_dst': _L1_ffn_in['att_dst'], 'L1_ffn_b_gat': _L1_ffn_in['b_gat'], 'L1_ffn_ln_gamma': _L1_ffn_in['ln_gamma'], 'L1_ffn_ln_beta': _L1_ffn_in['ln_beta'], 'L1_ffn_W1': _L1_ffn_in['W1'], 'L1_ffn_b1': _L1_ffn_in['b1'], 'L1_ffn_W2': _L1_ffn_in['W2'], 'L1_ffn_b2': _L1_ffn_in['b2'], 'L1_ffn_edge_index': _L1_ffn_in['edge_index'], 'L2_gnn_W_nb': _L2_gnn_in['W_nb'], 'L2_gnn_b_nb': _L2_gnn_in['b_nb'], 'L2_gnn_W_self': _L2_gnn_in['W_self'], 'L2_gnn_b_self': _L2_gnn_in['b_self'], 'L2_ffn_router_w1': _L2_ffn_in['router_w1'], 'L2_ffn_router_b1': _L2_ffn_in['router_b1'], 'L2_ffn_router_w2': _L2_ffn_in['router_w2'], 'L2_ffn_router_b2': _L2_ffn_in['router_b2'], 'L2_ffn_expert_w1': _L2_ffn_in['expert_w1'], 'L2_ffn_expert_b1': _L2_ffn_in['expert_b1'], 'L2_ffn_expert_w2': _L2_ffn_in['expert_w2'], 'L2_ffn_expert_b2': _L2_ffn_in['expert_b2'], 'L2_ffn_expert_w3': _L2_ffn_in['expert_w3'], 'L2_ffn_expert_b3': _L2_ffn_in['expert_b3'], 'L3_gnn_W': _L3_gnn_in['W'], 'L3_gnn_att_src': _L3_gnn_in['att_src'], 'L3_gnn_att_dst': _L3_gnn_in['att_dst'], 'L3_gnn_bias': _L3_gnn_in['bias'], 'L3_ffn_router_w': _L3_ffn_in['router_w'], 'L3_ffn_w1': _L3_ffn_in['w1'], 'L3_ffn_b1': _L3_ffn_in['b1'], 'L3_ffn_w2': _L3_ffn_in['w2'], 'L3_ffn_b2': _L3_ffn_in['b2']}

def reference(x, src, dst, edge_weight, L0_gnn_W, L0_gnn_attn_l, L0_gnn_attn_r, L0_gnn_bias, L0_ffn_Wg, L0_ffn_bg, L0_ffn_W1, L0_ffn_b1, L0_ffn_W2, L0_ffn_b2, L1_ffn_W_gat, L1_ffn_att_src, L1_ffn_att_dst, L1_ffn_b_gat, L1_ffn_ln_gamma, L1_ffn_ln_beta, L1_ffn_W1, L1_ffn_b1, L1_ffn_W2, L1_ffn_b2, L1_ffn_edge_index, L2_gnn_W_nb, L2_gnn_b_nb, L2_gnn_W_self, L2_gnn_b_self, L2_ffn_router_w1, L2_ffn_router_b1, L2_ffn_router_w2, L2_ffn_router_b2, L2_ffn_expert_w1, L2_ffn_expert_b1, L2_ffn_expert_w2, L2_ffn_expert_b2, L2_ffn_expert_w3, L2_ffn_expert_b3, L3_gnn_W, L3_gnn_att_src, L3_gnn_att_dst, L3_gnn_bias, L3_ffn_router_w, L3_ffn_w1, L3_ffn_b1, L3_ffn_w2, L3_ffn_b2):
    import jax
    import jax.numpy as jnp

    def _L0_gnn_ref(x, W, attn_l, attn_r, bias, src, dst):
        import jax, jax.numpy as jnp
        import numpy as np
        N_NODES = 3125
        D = 256
        L = 2
        N_EDGES = 50000
        NEG_SLOPE = 0.2

        def _gat_conv(h, W_l, al, ar, b, src, dst, n):
            hp = h @ W_l
            el = hp @ al
            er = hp @ ar
            e = jax.nn.leaky_relu(el[src] + er[dst], NEG_SLOPE)
            emax = jax.ops.segment_max(e, dst, num_segments=n)
            ex = jnp.exp(e - emax[dst])
            denom = jax.ops.segment_sum(ex, dst, num_segments=n)
            alpha = ex / denom[dst]
            out = jax.ops.segment_sum(hp[src] * alpha[:, None], dst, num_segments=n)
            return out + b
        n = x.shape[0]
        loops = jnp.arange(n, dtype=src.dtype)
        src_sl = jnp.concatenate([src, loops])
        dst_sl = jnp.concatenate([dst, loops])
        h = x
        n_layers = W.shape[0]
        for i in range(n_layers):
            h = _gat_conv(h, W[i], attn_l[i], attn_r[i], bias[i], src_sl, dst_sl, n)
            if i < n_layers - 1:
                h = jax.nn.relu(h)
        return h

    def _L0_ffn_ref(x, Wg, bg, W1, b1, W2, b2):
        import jax, jax.numpy as jnp
        import numpy as np
        B, S, D, E, H, K = (4, 256, 256, 8, 512, 2)
        Bv, Sv, Dv = x.shape
        gate_scores = x @ Wg + bg
        _, idx = jax.lax.top_k(gate_scores, K)
        mask = jax.nn.one_hot(idx, E, dtype=x.dtype).sum(axis=-2)
        xf = x.reshape(-1, Dv)
        mf = mask.reshape(-1, E)
        h = jax.nn.gelu(jnp.einsum('td,edh->teh', xf, W1) + b1[None], approximate=False)
        y = jnp.einsum('teh,ehd->ted', h, W2) + b2[None]
        out = jnp.einsum('ted,te->td', y, mf)
        return out.reshape(Bv, Sv, Dv)

    def _L1_gnn_ref(X, w_est, rows, cols):
        import jax, jax.numpy as jnp
        import numpy as np
        BLOCK_DIMS = [8] * 32

        def _mask_indices():
            d = sum(BLOCK_DIMS)
            mask = np.ones((d, d), dtype=np.int8)
            off = 0
            for b in BLOCK_DIMS:
                mask[off:off + b, off:off + b] = 0
                off += b
            rows, cols = np.nonzero(mask)
            return (d, rows.astype(np.int32), cols.astype(np.int32))
        d = X.shape[1]
        W = jnp.zeros((d, d), dtype=X.dtype).at[rows, cols].set(w_est)
        return X @ W

    def _L1_ffn_ref(x, W_gat, att_src, att_dst, b_gat, ln_gamma, ln_beta, W1, b1, W2, b2, edge_index):
        import jax, jax.numpy as jnp
        import numpy as np
        B, N, D = (16, 256, 256)
        NUM_EXPERTS, TOP_K, HEADS = (4, 2, 4)
        N_EDGES = 65536
        LN_EPS = 1e-05

        def _layernorm(x, g, b):
            mu = x.mean(-1, keepdims=True)
            var = ((x - mu) ** 2).mean(-1, keepdims=True)
            return (x - mu) * jax.lax.rsqrt(var + LN_EPS) * g + b

        def _forward(x, edge_index, W_gat, att_src, att_dst, b_gat, ln_gamma, ln_beta, W1, b1, W2, b2):
            Bc, Nc, Dc = x.shape
            M = Bc * Nc
            x_flat = x.reshape(M, Dc)
            h = (x_flat @ W_gat).reshape(M, HEADS, NUM_EXPERTS)
            loops = jnp.arange(M, dtype=edge_index.dtype)
            src = jnp.concatenate([edge_index[0], loops])
            dst = jnp.concatenate([edge_index[1], loops])
            a_src = (h * att_src).sum(-1)
            a_dst = (h * att_dst).sum(-1)
            e = jax.nn.leaky_relu(a_src[src] + a_dst[dst], negative_slope=0.2)
            e_max = jax.ops.segment_max(e, dst, num_segments=M)
            ee = jnp.exp(e - e_max[dst])
            denom = jax.ops.segment_sum(ee, dst, num_segments=M)
            alpha = ee / (denom[dst] + 1e-16)
            msg = h[src] * alpha[:, :, None]
            agg = jax.ops.segment_sum(msg, dst, num_segments=M).reshape(M, HEADS * NUM_EXPERTS) + b_gat
            scores = _layernorm(agg, ln_gamma, ln_beta).reshape(M, HEADS, NUM_EXPERTS).mean(1)
            scores = scores.reshape(Bc, Nc, NUM_EXPERTS)
            topk_s, topk_i = jax.lax.top_k(scores, TOP_K)
            w = jax.nn.softmax(topk_s, axis=-1)
            out = jnp.zeros_like(x)
            for ei in range(NUM_EXPERTS):
                g = jnp.where(topk_i == ei, w, 0.0).sum(-1)
                hh = jax.nn.gelu(x @ W1[ei] + b1[ei], approximate=False)
                out = out + g[..., None] * (hh @ W2[ei] + b2[ei])
            return out
        return _forward(x, edge_index, W_gat, att_src, att_dst, b_gat, ln_gamma, ln_beta, W1, b1, W2, b2)

    def _L2_gnn_ref(h, W_nb, b_nb, W_self, b_self, src, dst):
        import jax, jax.numpy as jnp
        import numpy as np
        N_NODES = 1250
        N_EDGES = 20000
        EMB = 256
        n = h.shape[0]
        neib_h = h @ W_nb.T + b_nb
        self_h = h @ W_self.T + b_self
        msg = self_h[src] + neib_h[dst]
        seg_max = jax.ops.segment_max(msg, dst, num_segments=n)
        e = jnp.exp(msg - seg_max[dst])
        seg_sum = jax.ops.segment_sum(e, dst, num_segments=n)
        alpha = e / seg_sum[dst]
        h_agg = jax.ops.segment_sum(alpha * h[src], dst, num_segments=n)
        deg = jax.ops.segment_sum(jnp.ones_like(dst, dtype=jnp.float32), dst, num_segments=n)
        return jnp.where((deg > 0)[:, None], h_agg, h)

    def _L2_ffn_ref(features, router_w1, router_b1, router_w2, router_b2, expert_w1, expert_b1, expert_w2, expert_b2, expert_w3, expert_b3):
        import jax, jax.numpy as jnp
        import numpy as np
        E, D, H, TOP_K = (6, 256, 256, 2)
        ROUTER_H = D // 2
        rh = jax.nn.relu(features @ router_w1 + router_b1)
        expert_logits = jax.nn.softmax(rh @ router_w2 + router_b2, axis=-1)
        top_w, top_i = jax.lax.top_k(expert_logits, TOP_K)
        routing_weights = jax.nn.softmax(top_w, axis=-1)
        h1 = jax.nn.relu(jnp.einsum('bsd,edh->bseh', features, expert_w1) + expert_b1)
        h2 = jax.nn.relu(jnp.einsum('bseh,ehf->bsef', h1, expert_w2) + expert_b2)
        expert_out = jnp.einsum('bsef,efo->bseo', h2, expert_w3) + expert_b3
        sel = jnp.take_along_axis(expert_out, top_i[:, :, :, None], axis=2)
        combined = jnp.sum(sel * routing_weights[..., None], axis=2)
        return combined

    def _L3_gnn_ref(x, edge_index, W, att_src, att_dst, bias):
        import jax, jax.numpy as jnp
        import numpy as np
        N_NODES = 3125
        N_EDGES = 100000
        H_SIZE = 256
        HEADS = 8
        HEAD_DIM = H_SIZE // HEADS
        NEG_SLOPE = 0.2
        'GATConv (concat heads) -> relu -> dropout(eval=identity).\n\n            x: [N, F]; edge_index: [2, E] with (src=row0, dst=row1) meaning message j->i.\n            '
        N = x.shape[0]
        h = jnp.einsum('nf,fhd->nhd', x, W)
        a_src = jnp.sum(h * att_src, axis=-1)
        a_dst = jnp.sum(h * att_dst, axis=-1)
        src = edge_index[0]
        dst = edge_index[1]
        e = jax.nn.leaky_relu(a_src[src] + a_dst[dst], NEG_SLOPE)
        e_max = jax.ops.segment_max(e, dst, num_segments=N)
        e_exp = jnp.exp(e - e_max[dst])
        denom = jax.ops.segment_sum(e_exp, dst, num_segments=N)
        alpha = e_exp / (denom[dst] + 1e-16)
        msg = h[src] * alpha[:, :, None]
        out = jax.ops.segment_sum(msg, dst, num_segments=N)
        out = out.reshape(N, -1) + bias
        return jax.nn.relu(out)

    def _L3_ffn_ref(input_embeddings, router_w, w1, b1, w2, b2):
        import jax, jax.numpy as jnp
        import numpy as np
        NUM_EXPERTS = 8
        TOP_K = 2
        B, S, D = (8, 512, 256)

        def _moe(tokens, router_w, w1, b1, w2, b2):
            N = tokens.shape[0]
            E = router_w.shape[0]
            logits = tokens.astype(jnp.float32) @ router_w.astype(jnp.float32).T
            probs = jax.nn.softmax(logits, axis=-1)
            rw, re = jax.lax.top_k(probs, TOP_K)
            if TOP_K > 1:
                rw = rw / jnp.maximum(rw.sum(-1, keepdims=True), 1e-12)
            rw = rw.astype(tokens.dtype)
            combine = jnp.zeros((N, E), tokens.dtype).at[jnp.arange(N)[:, None], re].set(rw)
            out = tokens
            for e in range(E):
                h = jax.nn.gelu(tokens @ w1[e] + b1[e], approximate=False)
                y = h @ w2[e] + b2[e]
                out = out + combine[:, e:e + 1] * y
            return out
        b, s, d = input_embeddings.shape
        tokens = input_embeddings.reshape(b * s, d)
        return _moe(tokens, router_w, w1, b1, w2, b2).reshape(b, s, d)
    edge_index = jnp.stack([src, dst])
    x = x + _L0_gnn_ref(_layernorm(x, axis=-1), L0_gnn_W, L0_gnn_attn_l, L0_gnn_attn_r, L0_gnn_bias, src, dst)
    x = x + _L0_ffn_ref(_layernorm(x, axis=-1)[None], L0_ffn_Wg, L0_ffn_bg, L0_ffn_W1, L0_ffn_b1, L0_ffn_W2, L0_ffn_b2)[0]
    x = x + _L1_gnn_ref(_layernorm(x, axis=-1), edge_weight, src, dst)
    x = x + _L1_ffn_ref(_layernorm(x, axis=-1)[None], L1_ffn_W_gat, L1_ffn_att_src, L1_ffn_att_dst, L1_ffn_b_gat, L1_ffn_ln_gamma, L1_ffn_ln_beta, L1_ffn_W1, L1_ffn_b1, L1_ffn_W2, L1_ffn_b2, L1_ffn_edge_index)[0]
    x = x + _L2_gnn_ref(_layernorm(x, axis=-1), L2_gnn_W_nb, L2_gnn_b_nb, L2_gnn_W_self, L2_gnn_b_self, src, dst)
    x = x + _L2_ffn_ref(_layernorm(x, axis=-1)[None], L2_ffn_router_w1, L2_ffn_router_b1, L2_ffn_router_w2, L2_ffn_router_b2, L2_ffn_expert_w1, L2_ffn_expert_b1, L2_ffn_expert_w2, L2_ffn_expert_b2, L2_ffn_expert_w3, L2_ffn_expert_b3)[0]
    x = x + _L3_gnn_ref(_layernorm(x, axis=-1), edge_index, L3_gnn_W, L3_gnn_att_src, L3_gnn_att_dst, L3_gnn_bias)
    x = x + _L3_ffn_ref(_layernorm(x, axis=-1)[None], L3_ffn_router_w, L3_ffn_w1, L3_ffn_b1, L3_ffn_w2, L3_ffn_b2)[0]
    return x

_drawn_inputs = setup_inputs


def setup_inputs(seed=0):
    import zlib

    import numpy as np

    out = dict(_drawn_inputs(seed))
    spreads = {'L0_gnn_bias': (0.0, 0.1),
     'L0_ffn_bg': (0.0, 0.1),
     'L0_ffn_b1': (0.0, 0.1),
     'L0_ffn_b2': (0.0, 0.1),
     'L1_ffn_b_gat': (0.0, 0.1),
     'L1_ffn_ln_gamma': (1.0, 0.2),
     'L1_ffn_ln_beta': (0.0, 0.1),
     'L1_ffn_b1': (0.0, 0.1),
     'L1_ffn_b2': (0.0, 0.1),
     'L2_ffn_router_b1': (0.0, 0.1),
     'L2_ffn_router_b2': (0.0, 0.1),
     'L2_ffn_expert_b1': (0.0, 0.462),
     'L2_ffn_expert_b2': (0.0, 0.1),
     'L2_ffn_expert_b3': (0.0, 0.1),
     'L3_gnn_bias': (0.0, 0.1),
     'L3_ffn_b1': (0.0, 0.372),
     'L3_ffn_b2': (0.0, 0.1)}
    factors = {'L2_gnn_W_nb': 8.0, 'L2_gnn_b_nb': 8.0, 'L2_gnn_b_self': 8.0, 'L3_gnn_att_dst': 3.64}
    for name, (base, spread) in spreads.items():
        noise = np.random.default_rng([zlib.crc32(name.encode()), seed]).standard_normal(out[name].shape)
        drawn = base * np.exp(spread * noise) if base else spread * noise
        out[name] = jnp.asarray(drawn.astype(out[name].dtype))
    for name, factor in factors.items():
        out[name] = (out[name] * factor).astype(out[name].dtype)
    return out
```

```python
from contextlib import ExitStack, contextmanager

import concourse.bass as bass
from concourse import mybir

ALU = mybir.AluOpType
ACT = mybir.ActivationFunctionType
F32 = mybir.dt.float32
I32 = mybir.dt.int32
U32 = mybir.dt.uint32
AX = mybir.AxisListType.X

P = 128
D = 256
KT = D // P
LN_EPS = 1e-5
SLOPE = 0.2
U = 5
HALF = 4
SLOTS = 8
NODE_BITS = 12
LO_BITS = 6
LO = 1 << LO_BITS
DROPPED = 4095
NOBODY = 8191
FLOOR = -1e30
START = -1e25


class Core:
    pass


class Stage:

    def __init__(self, nc, name):
        self.nc, self.name = nc, name
        self.stack = ExitStack()
        self.sems = []

    def sb(self, name, shape, dt=F32):
        return self.stack.enter_context(self.nc.sbuf_tensor(f"{self.name}_{name}", shape, dt))

    def sem(self, name):
        s = self.nc.alloc_semaphore(f"{self.name}_{name}")
        self.sems.append(s)
        return s


@contextmanager
def stage(nc, name):
    st = Stage(nc, name)
    yield st
    st.stack.close()
    nc.clear_and_free_semaphores(st.sems)
    nc.all_engine_barrier()


class Chain:

    def __init__(self, eng, sem):
        self.eng, self.sem, self.n = eng, sem, 0

    def __call__(self, ins):
        self.n += 1
        ins.then_inc(self.sem, 1)
        self.eng.wait_ge(self.sem, self.n)

    def add(self, ins):
        self.n += 1
        ins.then_inc(self.sem, 1)

    def join(self):
        self.eng.wait_ge(self.sem, self.n)

    def restart(self):
        self.eng.sem_clear(self.sem)
        self.n = 0


def when(eng, c, sem, value):
    eng.wait_ge(sem, value)
    eng.sem_inc(c.passed, 1)



def build_edge_table(nc, c, name, dst, src, weight, edges, half, table, base_row):
    NT = c.NT
    F = -(-edges // P)
    whole = edges // F
    rest = edges - whole * F
    turns = F // (2 * half)
    assert turns * 2 * half == F
    HI = 2 * NT
    rows = table.shape[0]
    sorted_lo = nc.dram_tensor(f"{name}_sorted_lo", (1 + P * F, 2), I32, kind="Internal").ap()

    with stage(nc, name) as st:
        sb, sem = st.sb, st.sem
        dst_i, src_i = sb("dst_i", [P, F], I32), sb("src_i", [P, F], I32)
        pay = sb("pay", [P, F, 2], I32)
        prev = sb("prev", [P, F, 2], I32)
        digit, other = sb("digit", [P, F]), sb("other", [P, F])
        eq, run, pos, keep = sb("eq", [P, F]), sb("run", [P, F]), sb("pos", [P, F]), sb("keep", [P, F])
        pos_i = sb("pos_i", [P, F], I32)
        tmp_i = sb("tmp_i", [P, F], I32)
        pay_s, pos_s = sb("pay_s", [P, 2, half, 2], I32), sb("pos_s", [P, 2, half], I32)
        cnt, base = sb("cnt", [P, LO]), sb("base", [P, LO])
        tot, cum = sb("tot", [P, LO]), sb("cum", [P, LO])
        last, allsame = sb("last", [P, LO]), sb("allsame", [P, LO])
        last_t, same_t, carry_t, peak_t = (sb(n, [LO, P]) for n in ("last_t", "same_t", "carry_t", "peak_t"))
        peak = sb("peak", [LO, 2])
        row, row2, row3 = sb("row", [1, LO]), sb("row2", [1, LO]), sb("row3", [1, LO])
        row_i = sb("row_i", [1, LO], I32)
        bases = sb("bases", [P, NT + 1])
        empty = sb("empty", [P, SLOTS, 2], I32)
        zrow = sb("zrow", [1, 2], I32)
        loaded, chain_sem, stored, counted = (sem(n) for n in ("loaded", "chain", "stored", "counted"))
        staged, sent = [sem("staged_a"), sem("staged_b")], [sem("sent_a"), sem("sent_b")]
        free = [sem("free_a"), sem("free_b")]
        reloaded, based, emptied, cleared, mm = sem("reloaded"), sem("based"), sem("emptied"), sem("cleared"), sem("mm")
        ps = c.psum

        with nc.Block() as block:

            @block.sync
            def _(sp):
                def rows_of(tile, ap):
                    sp.wait_ge(cleared, 2)
                    sp.dma_start(tile[0:whole, :], ap[0:whole * F].rearrange("(p f) -> p f", f=F)).then_inc(loaded, 16)
                    if rest:
                        sp.dma_start(tile[whole:whole + 1, 0:rest],
                                     ap[whole * F:edges].rearrange("(a f) -> a f", a=1)).then_inc(loaded, 16)

                rows_of(dst_i, dst)
                rows_of(src_i, src)
                rows_of(tmp_i, weight)
                sp.dma_start(sorted_lo[0:1, :], zrow[:, :]).then_inc(stored, 16)

                def relay(second):
                    with sp.Fori(0, turns) as i:
                        for a in range(2):
                            when(sp, c, sent[a], (i + (1 + second * turns)) * (16 * half))
                            sp.sem_inc(free[a], 1)

                for a in range(2):
                    sp.sem_inc(free[a], 1)
                relay(0)
                sp.wait_ge(stored, 16)
                sp.wait_ge(sent[0], 16 * half * turns)
                sp.wait_ge(sent[1], 16 * half * turns)
                sp.dma_start(pay[:, :, :], sorted_lo[1:1 + P * F, :].rearrange("(p f) w -> p f w", f=F)).then_inc(reloaded, 16)
                sp.dma_start(prev[:, :, :], sorted_lo[0:P * F, :].rearrange("(p f) w -> p f w", f=F)).then_inc(reloaded, 16)
                sp.wait_ge(based, 1)
                n = sp.value_load(base_row[0:1, NT:NT + 1], min_val=1, max_val=rows // (P * SLOTS) - 1)
                with sp.Fori(0, n + 1) as b:
                    sp.dma_start(table[bass.ds(b * (P * SLOTS), P * SLOTS), :].rearrange("(p s) w -> p s w", s=SLOTS),
                                 empty[:, :, :]).then_inc(stored, 16)
                sp.wait_ge(stored, n * 16 + 32)
                sp.sem_inc(emptied, 1)
                relay(1)

            @block.vector
            def _(dve):
                ch = Chain(dve, chain_sem)
                dve.memset(dst_i[:, :], DROPPED).then_inc(cleared, 1)
                dve.memset(src_i[:, :], 0)
                dve.memset(zrow[:, :], 0)
                dve.memset(empty[:, :, :], NOBODY)
                dve.memset(pos[:, :], 0.0)
                ch(dve.memset(tmp_i[:, :], 0))
                dve.sem_inc(cleared, 1)
                dve.wait_ge(loaded, (96 if rest else 48))
                ch(dve.tensor_scalar(other[:, :], src_i[:, :], float(c.N - 1), None, ALU.min))
                ch(dve.tensor_scalar(digit[:, :], dst_i[:, :], float(DROPPED), float(1 << NODE_BITS), ALU.min, ALU.mult))
                ch(dve.tensor_tensor(other[:, :], digit[:, :], other[:, :], ALU.add))
                ch.add(dve.tensor_copy(pay[:, :, 0], other[:, :]))
                ch.add(dve.tensor_copy(pay[:, :, 1], tmp_i[:, :]))
                ch(dve.tensor_scalar(digit[:, :], dst_i[:, :], float(DROPPED), None, ALU.min))
                ch(dve.tensor_copy(dst_i[:, :], digit[:, :]))
                ch(dve.tensor_scalar(src_i[:, :], dst_i[:, :], LO - 1, None, ALU.bitwise_and))
                ch(dve.tensor_copy(digit[:, :], src_i[:, :]))
                ch(dve.memset(keep[:, :], 1.0))
                with dve.Fori(0, LO) as b:
                    ch.restart()
                    ch(dve.tensor_scalar(eq[:, :], digit[:, :], c.iota[:, bass.ds(b, 1)], None, ALU.is_equal))
                    ch(dve.tensor_reduce(cnt[:, bass.ds(b, 1)], eq[:, :], AX, ALU.add))
                ch.restart()
                dve.sem_inc(counted, 1)
                dve.wait_ge(mm, 1)
                ch(dve.tensor_copy(tot[:, :], ps[:, 1, 0:LO]))
                ch(dve.tensor_tensor_scan(cum[:, :], keep[:, 0:LO], tot[:, :], 0.0, ALU.mult, ALU.add))
                ch(dve.tensor_tensor(cum[:, :], cum[:, :], tot[:, :], ALU.subtract))
                ch(dve.tensor_tensor(base[:, :], cum[:, :], ps[:, 0, 0:LO], ALU.add))

                def positions(n):
                    with dve.Fori(0, n) as b:
                        ch.restart()
                        ch(dve.tensor_scalar(eq[:, :], digit[:, :], c.iota[:, bass.ds(b, 1)], None, ALU.is_equal))
                        ch(dve.tensor_tensor_scan(run[:, :], keep[:, :], eq[:, :], base[:, bass.ds(b, 1)], ALU.mult, ALU.add))
                        ch.add(dve.tensor_reduce(cnt[:, bass.ds(b, 1)], run[:, :], AX, ALU.max))
                        ch.add(dve.copy_predicated(pos[:, :], eq[:, :].bitcast(I32), run[:, :]))
                        ch.join()
                    ch.restart()

                def stage_out(second):
                    with dve.Fori(0, turns) as i:
                        ch.restart()
                        for a in range(2):
                            when(dve, c, free[a], i + (1 + second * turns))
                            col = i * (2 * half) + a * half
                            ch.add(dve.tensor_copy(pay_s[:, a, :, :], pay[:, bass.ds(col, half), :]))
                            ch.add(dve.tensor_copy(pos_s[:, a, :], pos_i[:, bass.ds(col, half)]))
                            ch.join()
                            dve.sem_inc(staged[a], 1)
                    ch.restart()

                positions(LO)
                ch(dve.tensor_copy(pos_i[:, :], pos[:, :]))
                stage_out(0)
                dve.wait_ge(reloaded, 32)
                ch(dve.tensor_scalar(dst_i[:, :], pay[:, :, 0], NODE_BITS, LO - 1, ALU.logical_shift_right, ALU.bitwise_and))
                ch(dve.tensor_scalar(src_i[:, :], prev[:, :, 0], NODE_BITS, LO - 1, ALU.logical_shift_right, ALU.bitwise_and))
                ch(dve.tensor_copy(other[:, :], dst_i[:, :]))
                ch(dve.tensor_copy(eq[:, :], src_i[:, :]))
                ch(dve.tensor_tensor(keep[:, :], other[:, :], eq[:, :], ALU.is_equal))
                ch(dve.tensor_scalar(tmp_i[:, :], pay[:, :, 0], NODE_BITS + LO_BITS, None, ALU.logical_shift_right))
                ch(dve.tensor_copy(digit[:, :], tmp_i[:, :]))
                ch(dve.memset(last[:, :], 0.0))
                ch(dve.tensor_reduce(cum[:, 0:1], keep[:, :], AX, ALU.min))
                ch(dve.tensor_copy(allsame[:, :], cum[:, 0:1].broadcast_to([P, LO])))
                with dve.Fori(0, HI) as b:
                    ch.restart()
                    ch(dve.tensor_scalar(eq[:, :], digit[:, :], c.iota[:, bass.ds(b, 1)], None, ALU.is_equal))
                    ch(dve.tensor_tensor_scan(run[:, :], keep[:, :], eq[:, :], 0.0, ALU.mult, ALU.add))
                    ch(dve.tensor_copy(last[:, bass.ds(b, 1)], run[:, F - 1:F]))
                ch.restart()
                dve.sem_inc(counted, 1)
                dve.wait_ge(mm, 2)
                ch.add(dve.tensor_copy(last_t[:, :], ps[0:LO, 0, 0:P]))
                ch.add(dve.tensor_copy(same_t[:, :], ps[0:LO, 1, 0:P]))
                ch(dve.memset(carry_t[:, 0:1], 0.0))
                ch(dve.tensor_tensor_scan(carry_t[:, 1:P], same_t[:, 0:P - 1], last_t[:, 0:P - 1], 0.0, ALU.mult, ALU.add))
                dve.sem_inc(counted, 1)
                dve.wait_ge(mm, 3)
                ch(dve.tensor_copy(base[:, :], ps[:, 2, 0:LO]))
                ch(dve.memset(pos[:, :], 1.0))
                ch(dve.memset(cnt[:, :], 0.0))
                positions(HI)
                dve.sem_inc(counted, 1)
                dve.wait_ge(mm, 4)
                ch(dve.tensor_copy(peak_t[:, :], ps[0:LO, 3, 0:P]))
                ch(dve.tensor_reduce(peak[:, 0:1], peak_t[:, :], AX, ALU.max))
                dve.sem_inc(counted, 1)
                dve.wait_ge(mm, 5)
                ch(dve.tensor_copy(row[:, :], ps[0:1, 4, 0:LO]))
                pairs = row[:, 0:HI].rearrange("a (t two) -> a t two", two=2)
                ch(dve.tensor_tensor(row2[:, 0:NT], pairs[:, :, 0], pairs[:, :, 1], ALU.max))
                ch(dve.tensor_scalar(row2[:, 0:NT], row2[:, 0:NT], 1.0, float(SLOTS - 1), ALU.max, ALU.add))
                ch(dve.tensor_copy(row_i[:, 0:NT], row2[:, 0:NT]))
                ch(dve.tensor_scalar(row_i[:, 0:NT], row_i[:, 0:NT], SLOTS.bit_length() - 1, None, ALU.logical_shift_right))
                ch(dve.tensor_copy(row2[:, 0:NT], row_i[:, 0:NT]))
                ch(dve.memset(row3[:, 0:1], 0.0))
                ch(dve.memset(row[:, :], 1.0))
                ch(dve.tensor_tensor_scan(row3[:, 1:NT + 1], row[:, 0:NT], row2[:, 0:NT], 0.0, ALU.mult, ALU.add))
                ch(dve.tensor_copy(base_row[:, 0:NT + 1], row3[:, 0:NT + 1]))
                dve.sem_inc(counted, 1)
                dve.sem_inc(based, 1)
                dve.wait_ge(mm, 6)
                ch(dve.tensor_copy(bases[:, :], ps[:, 5, 0:NT + 1]))
                ch(dve.tensor_scalar(pos[:, :], pos[:, :], -1.0, None, ALU.add))
                ch(dve.tensor_copy(pos_i[:, :], pos[:, :]))
                ch(dve.tensor_scalar(tmp_i[:, :], pos_i[:, :], SLOTS - 1, None, ALU.bitwise_and))
                ch(dve.tensor_copy(run[:, :], tmp_i[:, :]))
                ch(dve.tensor_tensor(pos[:, :], pos[:, :], run[:, :], ALU.subtract))
                ch(dve.scalar_tensor_tensor(pos[:, :], pos[:, :], float(P), run[:, :], ALU.mult, ALU.add))
                ch(dve.tensor_scalar(tmp_i[:, :], pay[:, :, 0], NODE_BITS, P - 1, ALU.logical_shift_right, ALU.bitwise_and))
                ch(dve.tensor_copy(run[:, :], tmp_i[:, :]))
                ch(dve.scalar_tensor_tensor(pos[:, :], run[:, :], float(SLOTS), pos[:, :], ALU.mult, ALU.add))
                ch(dve.tensor_scalar(tmp_i[:, :], pay[:, :, 0], NODE_BITS + 7, None, ALU.logical_shift_right))
                ch(dve.tensor_copy(digit[:, :], tmp_i[:, :]))
                ch(dve.tensor_scalar(run[:, :], digit[:, :], float(NT), float(rows), ALU.is_ge, ALU.mult))
                ch(dve.tensor_tensor(pos[:, :], pos[:, :], run[:, :], ALU.add))
                with dve.Fori(0, NT) as b:
                    ch.restart()
                    ch(dve.tensor_scalar(run[:, :], digit[:, :], c.iota[:, bass.ds(b, 1)], bases[:, bass.ds(b, 1)], ALU.is_equal, ALU.mult))
                    ch(dve.scalar_tensor_tensor(pos[:, :], run[:, :], float(P * SLOTS), pos[:, :], ALU.mult, ALU.add))
                ch.restart()
                ch(dve.tensor_copy(pos_i[:, :], pos[:, :]))
                ch(dve.tensor_scalar(tmp_i[:, :], pay[:, :, 0], (1 << NODE_BITS) - 1, None, ALU.bitwise_and))
                ch(dve.tensor_copy(pay[:, :, 0], tmp_i[:, :]))
                stage_out(1)

            @block.tensor
            def _(pe):
                pe.wait_ge(counted, 1)
                pe.matmul(ps[:, 0, 0:LO], c.before[:, :], cnt[:, :], start=True, stop=True)
                pe.matmul(ps[:, 1, 0:LO], c.ones[:, :], cnt[:, :], start=True, stop=True).then_inc(mm, 1)
                pe.wait_ge(counted, 2)
                pe.transpose(ps[0:LO, 0, 0:P], last[:, :], c.ident[:, :])
                pe.transpose(ps[0:LO, 1, 0:P], allsame[:, :], c.ident[:, :]).then_inc(mm, 1)
                pe.wait_ge(counted, 3)
                pe.transpose(ps[:, 2, 0:LO], carry_t[:, :], c.ident[0:LO, 0:LO]).then_inc(mm, 1)
                pe.wait_ge(counted, 4)
                pe.transpose(ps[0:LO, 3, 0:P], cnt[:, :], c.ident[:, :]).then_inc(mm, 1)
                pe.wait_ge(counted, 5)
                pe.transpose(ps[0:1, 4, 0:LO], peak[:, 0:1], c.ident[0:LO, 0:LO]).then_inc(mm, 1)
                pe.wait_ge(counted, 6)
                pe.matmul(ps[:, 5, 0:NT + 1], c.ones[0:1, :], row3[:, 0:NT + 1], start=True, stop=True).then_inc(mm, 1)

            @block.gpsimd
            def _(pool):
                for second in range(2):
                    if second:
                        pool.wait_ge(emptied, 1)
                    with pool.Fori(0, turns) as i:
                        for a in range(2):
                            when(pool, c, staged[a], i + (1 + second * turns))
                            for k in range(half):
                                pool.indirect_dma_start(
                                    out=(table[:, :] if second else sorted_lo[:, :]),
                                    out_offset=bass.IndirectOffsetOnAxis(ap=pos_s[:, a, k:k + 1].bitcast(U32), axis=0),
                                    in_=pay_s[:, a, k, :], in_offset=None,
                                    bounds_check=rows - 1 if second else P * F, oob_is_err=False).then_inc(sent[a], 16)
                pool.wait_ge(sent[0], 16 * half * (2 * turns))
                pool.wait_ge(sent[1], 16 * half * (2 * turns))
                pool.sem_inc(c.passed, 1)



def normalise(dve, ch, c, src, i, stats, moments, rstd, xn, varied, rooted):
    for j in range(U):
        ch.add(dve.bn_stats(stats[:, j, :], src[:, bass.ds((i * U + j) * D, D)]))
    ch.join()
    for j in range(U):
        ch.add(dve.bn_aggr(moments[:, j, :], stats[:, j, :]))
    ch.join()
    ch(dve.tensor_scalar(rstd[:, :], moments[:, :, 1], LN_EPS, None, ALU.add))
    dve.sem_inc(varied, 1)
    when(dve, c, rooted, i + 1)
    ch(dve.reciprocal(rstd[:, :], rstd[:, :]))
    for j in range(U):
        ch.add(dve.tensor_scalar(xn[:, j, :], src[:, bass.ds((i * U + j) * D, D)], moments[:, j, 0:1], rstd[:, j:j + 1],
                                 ALU.subtract, ALU.mult))
    ch.join()


def prepare(nc, c, name, src, weights, width, norm=True, bias=None, attend=None, transposed=False,
            hidden=None, rows=None, xn_rows=False, scores=None, neighbours=None, keep_xt=False, add=False, ready=None, add_xn=False):
    NB = c.NT // U
    H = attend[0] if attend else 0
    N = width + 2 * H
    row_width = (width + H) if not xn_rows else 2 * D + 1
    with stage(nc, name) as st:
        sb, sem = st.sb, st.sem
        w = ready if ready is not None else sb("w", [P, KT, N])
        stats, moments, rstd = sb("stats", [P, U, 6]), sb("moments", [P, U, 2]), sb("rstd", [P, U])
        xn, xt = sb("xn", [P, U, D]), sb("xt", [P, U, D])
        out_rows = sb("rows", [P, U, row_width]) if rows is not None else None
        if attend:
            vec = sb("vec", [P, 2, width])
            prod = sb("prod", [P, width])
        if transposed:
            raw = sb("raw", [P, 2, KT, D])
        bias_row = sb("bias", [1, N]) if bias is not None else None
        if hidden:
            w1 = sb("w1", [P, KT, P])
            b1 = sb("b1", [P, 1])
            hid = sb("hid", [P, U, P])
        chain_sem, loaded, weighed, flipped_w = (sem(n) for n in ("chain", "loaded", "weighed", "flipped_w"))
        normed = sem("normed")
        flipped = sem("flipped")
        turned = sem("turned")
        kept = sem("kept")
        multiplied = sem("multiplied")
        taken = sem("taken")
        evacuated = sem("evacuated")
        filled = sem("filled")
        sent = sem("sent")
        stored = sem("stored")
        hidden_in, hidden_out = sem("hidden_in"), sem("hidden_out")
        varied, rooted = sem("varied"), sem("rooted")
        ps = c.psum
        loads = []
        if ready is None and not transposed:
            if hidden:
                loads.append((w[:, 0, 0:width], weights))
            else:
                loads += [(w[:, k, 0:width], weights[:, k, :]) for k in range(KT)]
        if transposed:
            for a in range(2):
                loads.append((raw[:, a, :, :], weights[a].rearrange("(k p) n -> p k n", p=P)))
        if attend:
            for a in range(2):
                loads.append((vec[:, a, :], attend[1 + a].rearrange("(o n) -> o n", o=1).broadcast_to([P, width])))
        if bias is not None:
            for off, b in bias:
                loads.append((bias_row[:, off:off + b.shape[0]], b.rearrange("(o n) -> o n", o=1)))
        if hidden:
            loads.append((w1[:, :, :], hidden[0].rearrange("(k p) n -> p k n", p=P)))
            loads.append((b1[:, :], hidden[1].rearrange("(p o) -> p o", o=1)))

        with nc.Block() as block:

            @block.sync
            def _(sp):
                with nc.allow_non_contiguous_dma(reason="small weights, loaded once"):
                    for tile, source in loads:
                        sp.dma_start(tile, source).then_inc(loaded, 16)
                if rows is not None:
                    sp.sem_inc(stored, 1)
                    with sp.Fori(0, NB) as i:
                        if xn_rows:
                            when(sp, c, filled, i + 1)
                        when(sp, c, evacuated, (i + 2) * U)
                        sp.dma_start(rows[bass.ds(i * (U * P), U * P), 0:row_width].rearrange("(j p) w -> p j w", p=P),
                                     out_rows[:, :, :]).then_inc(sent, 16)
                        when(sp, c, sent, (i + 1) * 16)
                        sp.sem_inc(stored, 1)

            @block.vector
            def _(dve):
                ch = Chain(dve, chain_sem)
                dve.sem_inc(taken, U)
                if loads:
                    dve.wait_ge(loaded, 16 * len(loads))
                if attend:
                    for a in range(2):
                        for k in range(KT):
                            ch(dve.tensor_tensor(prod[:, :], w[:, k, 0:width], vec[:, a, :], ALU.mult))
                            ch(dve.tensor_reduce(w[:, k, width + a * H:width + (a + 1) * H],
                                                 prod[:, :].rearrange("p (h d) -> p h d", h=H), AX, ALU.add))
                if transposed:
                    for a in range(2):
                        dve.wait_ge(flipped_w, a + 1)
                        for k in range(KT):
                            ch(dve.tensor_copy(w[:, k, a * D:(a + 1) * D], ps[:, 2 * a + k, 0:D]))
                if xn_rows:
                    ch(dve.memset(out_rows[:, :, 2 * D:2 * D + 1], 0.0))
                dve.sem_inc(weighed, 1)
                ch.restart()
                with dve.Fori(0, NB) as i:
                    ch.restart()
                    when(dve, c, flipped, i + 1)
                    if norm:
                        normalise(dve, ch, c, src, i, stats, moments, rstd, xn, varied, rooted)
                    else:
                        ch(dve.tensor_copy(xn[:, :, :].rearrange("p u d -> p (u d)"), src[:, bass.ds(i * (U * D), U * D)]))
                    dve.sem_inc(normed, 1)
                    if add_xn:
                        whole = c.x[:, bass.ds(i * (U * D), U * D)]
                        ch(dve.tensor_tensor(whole, whole, xn[:, :, :].rearrange("p u d -> p (u d)"), ALU.add))
                    if xn_rows:
                        when(dve, c, stored, i + 1)
                        ch(dve.tensor_copy(out_rows[:, :, D:2 * D], xn[:, :, :]))
                        dve.sem_inc(filled, 1)
                    for j in range(U):
                        t = i * U + j
                        when(dve, c, evacuated, t + U + 1) if rows is not None else when(dve, c, multiplied, t + 1)
                        if attend:
                            ch(dve.tensor_copy(c.er[:, bass.ds(t * 8, H)], ps[:, 3 + j, width + H:width + 2 * H]))
                        if neighbours is not None:
                            ch(dve.tensor_copy(neighbours[:, bass.ds(t * D, D)], ps[:, 3 + j, D:2 * D]))
                        if scores is not None:
                            ch(dve.tensor_copy(scores[:, bass.ds(t * 8, width)], ps[:, 3 + j, 0:width]))
                        if add:
                            ch(dve.tensor_tensor(c.x[:, bass.ds(t * D, D)], ps[:, 3 + j, 0:D], c.x[:, bass.ds(t * D, D)], ALU.add))
                        dve.sem_inc(taken, 1)
                ch.restart()

            @block.tensor
            def _(pe):
                pe.sem_inc(flipped, 1)
                if transposed:
                    pe.wait_ge(loaded, 16 * len(loads))
                    for a in range(2):
                        for k in range(KT):
                            for n in range(KT):
                                ins = pe.transpose(ps[:, 2 * a + k, n * P:(n + 1) * P], raw[:, a, n, k * P:(k + 1) * P], c.ident[:, :])
                        ins.then_inc(flipped_w, 1)
                pe.wait_ge(weighed, 1)
                with pe.Fori(0, NB) as i:
                    when(pe, c, normed, i + 1)
                    when(pe, c, turned, i + 1)
                    for j in range(U):
                        for k in range(KT):
                            ins = pe.transpose(ps[:, j // 2, (j % 2) * D + k * P:(j % 2) * D + (k + 1) * P],
                                               xn[:, j, k * P:(k + 1) * P], c.ident[:, :])
                    ins.then_inc(flipped, 1)
                    when(pe, c, turned, i + 2)
                    if hidden:
                        for j in range(U):
                            when(pe, c, taken, i * U + j + 1)
                            for k in range(KT):
                                ins = pe.matmul(ps[:, 3 + j, 0:P], w1[:, k, :], xt[:, j, k * P:(k + 1) * P],
                                                start=(k == 0), stop=(k == KT - 1))
                            ins.then_inc(hidden_in, 1)
                    for j in range(U):
                        t = i * U + j
                        if hidden:
                            when(pe, c, hidden_out, t + 1)
                            pe.matmul(ps[:, 3 + j, 0:N], hid[:, j, :], w[:, 0, 0:N], start=True, stop=False)
                        else:
                            when(pe, c, taken, t + 1)
                            if rows is not None:
                                when(pe, c, evacuated, t + 1)
                            for k in range(KT):
                                ins = pe.matmul(ps[:, 3 + j, 0:N], xt[:, j, k * P:(k + 1) * P], w[:, k, 0:N],
                                                start=(k == 0), stop=(k == KT - 1 and bias is None))
                        if bias is not None:
                            ins = pe.matmul(ps[:, 3 + j, 0:N], c.ones[0:1, :], bias_row[:, :], start=False, stop=True)
                        ins.then_inc(multiplied, 1)

            @block.scalar
            def _(act):
                act.sem_inc(turned, 1)
                if rows is not None:
                    act.sem_inc(evacuated, U)
                with act.Fori(0, NB) as i:
                    if norm:
                        when(act, c, varied, i + 1)
                        act.activation(rstd[:, :], rstd[:, :], ACT.Sqrt).then_inc(rooted, 1)
                    when(act, c, flipped, i + 2)
                    if keep_xt:
                        when(act, c, kept, i + 1)
                    for q in range(3):
                        n = min(2, U - 2 * q)
                        ins = act.activation(xt[:, 2 * q:2 * q + n, :].rearrange("p u d -> p (u d)"), ps[:, q, 0:n * D], ACT.Copy)
                    ins.then_inc(turned, 1)
                    if hidden:
                        for j in range(U):
                            when(act, c, hidden_in, i * U + j + 1)
                            act.activation(hid[:, j, :], ps[:, 3 + j, 0:P], ACT.Relu, bias=b1[:, :]).then_inc(hidden_out, 1)
                    if rows is not None:
                        when(act, c, stored, i + 1)
                        for j in range(U):
                            when(act, c, multiplied, i * U + j + 1)
                            n = D if xn_rows else width + H
                            act.activation(out_rows[:, j, 0:n], ps[:, 3 + j, 0:n], ACT.Copy).then_inc(evacuated, 1)

            @block.gpsimd
            def _(pool):
                if keep_xt:
                    pool.sem_inc(kept, 1)
                    with pool.Fori(0, NB) as i:
                        when(pool, c, turned, i + 2)
                        pool.tensor_copy(c.xt[:, bass.ds(i * (U * D), U * D)], xt[:, :, :].rearrange("p u d -> p (u d)")).then_inc(kept, 1)


def attend_edges(nc, c, name, table, base_row, rows, H, DH, slope=True, loops=False, tiny=0.0, bias=None, relu=False,
                 out=None, add=False, neighbours=None, fallback=False):
    VW = H * DH
    vector_scores = neighbours is not None
    SC = 2 * D if vector_scores else VW
    RW = SC + (1 if vector_scores else H)
    V0 = D if vector_scores else 0
    NS = 1 if vector_scores else H
    blocks = table.shape[0] // (P * SLOTS)
    with stage(nc, name) as st:
        sb, sem = st.sb, st.sem
        idx = sb("idx", [P, 2, HALF, 2], I32)
        got = sb("got", [P, 2, HALF, RW])
        self_row = sb("self_row", [P, RW])
        e = sb("e", [P, HALF + 1, H])
        d = sb("d", [P, HALF + 1, H])
        p = sb("p", [P, HALF + 1, H])
        top, den, rden = sb("top", [P, H]), sb("den", [P, H]), sb("rden", [P, H])
        v = sb("v", [P, HALF, VW])
        part, acc = sb("part", [P, VW]), sb("acc", [P, VW])
        bias_all = sb("bias", [P, VW]) if bias is not None else None
        chain_sem, loaded = sem("chain"), sem("loaded")
        self_in, self_free = sem("self_in"), sem("self_free")
        idx_in = [sem("idx_in_a"), sem("idx_in_b")]
        gathered = [sem("got_a"), sem("got_b")]
        freed = [sem("freed_a"), sem("freed_b")]
        shifted, weighed = sem("shifted"), sem("weighed")
        need_self = loops or fallback

        with nc.Block() as block:

            @block.sync
            def _(sp):
                if bias is not None:
                    sp.dma_start(bias_all[:, :], bias.rearrange("(o n) -> o n", o=1).broadcast_to([P, VW])).then_inc(loaded, 16)
                total = sp.value_load(base_row[0:1, c.NT:c.NT + 1], min_val=1, max_val=blocks - 1)

                def load(b, a):
                    src = table[bass.ds(b * (P * SLOTS), P * SLOTS), :].rearrange("(p s) w -> p s w", s=SLOTS)
                    sp.dma_start(idx[:, a, :, :], src[:, a * HALF:(a + 1) * HALF, :]).then_inc(idx_in[a], 16)

                for a in range(2):
                    load(0, a)
                with sp.Fori(0, total) as b:
                    for a in range(2):
                        when(sp, c, gathered[a], (b + 1) * (16 * HALF))
                        load(b + 1, a)
                for a in range(2):
                    sp.wait_ge(idx_in[a], (total + 1) * 16)
                    sp.sem_inc(c.passed, 1)

            @block.gpsimd
            def _(pool):
                with pool.Fori(0, c.NT) as t:
                    b0 = pool.value_load(base_row[0:1, bass.ds(t, 1)], min_val=0, max_val=blocks - 1)
                    b1 = pool.value_load(base_row[0:1, bass.ds(t + 1, 1)], min_val=1, max_val=blocks)
                    with pool.Fori(b0, b1) as b:
                        for a in range(2):
                            when(pool, c, idx_in[a], (b + 1) * 16)
                            when(pool, c, freed[a], b + 1)
                            for k in range(HALF):
                                pool.indirect_dma_start(
                                    out=got[:, a, k, :], out_offset=None, in_=rows[:, :],
                                    in_offset=bass.IndirectOffsetOnAxis(ap=idx[:, a, k, 0:1].bitcast(U32), axis=0),
                                    bounds_check=c.N - 1, oob_is_err=False).then_inc(gathered[a], 16)

            @block.scalar
            def _(act):
                with act.Fori(0, c.NT) as t:
                    if need_self:
                        when(act, c, self_free, t + 1)
                        act.dma_start(self_row[:, :], rows[bass.ds(t * P, P), 0:RW]).then_inc(self_in, 16)
                    b0 = act.value_load(base_row[0:1, bass.ds(t, 1)], min_val=0, max_val=blocks - 1)
                    b1 = act.value_load(base_row[0:1, bass.ds(t + 1, 1)], min_val=1, max_val=blocks)
                    with act.Fori(b0, b1) as b:
                        for a in range(2):
                            when(act, c, shifted, b * 2 + (a + 1))
                            act.activation(p[:, :, :], d[:, :, :], ACT.Exp).then_inc(weighed, 1)

            @block.vector
            def _(dve):
                ch = Chain(dve, chain_sem)
                ch(dve.memset(got[:, :, :, :], 0.0))
                ch(dve.memset(got[:, :, :, SC:RW], FLOOR))
                dve.sem_inc(self_free, 1)
                for a in range(2):
                    dve.sem_inc(freed[a], 1)
                if bias is not None:
                    dve.wait_ge(loaded, 16)
                ch.restart()
                by_head = lambda ap: ap.rearrange("p (h d) -> p h d", h=H)
                spread = lambda ap: ap.unsqueeze(2).broadcast_to([P, H, DH])
                with dve.Fori(0, c.NT) as t:
                    ch.restart()
                    if need_self:
                        when(dve, c, self_in, (t + 1) * 16)
                    if loops:
                        ch(dve.tensor_tensor(top[:, :], self_row[:, SC:RW], c.er[:, bass.ds(t * 8, H)], ALU.add))
                        ch(dve.scalar_tensor_tensor(e[:, HALF, :], top[:, :], SLOPE, top[:, :], ALU.mult, ALU.max))
                        ch.add(dve.memset(den[:, :], 1.0))
                        ch.add(dve.tensor_copy(acc[:, :], self_row[:, 0:VW]))
                    else:
                        ch.add(dve.memset(e[:, HALF, :], START))
                        ch.add(dve.memset(den[:, :], 0.0))
                        ch.add(dve.memset(acc[:, :], 0.0))
                    ch.join()
                    b0 = dve.value_load(base_row[0:1, bass.ds(t, 1)], min_val=0, max_val=blocks - 1)
                    b1 = dve.value_load(base_row[0:1, bass.ds(t + 1, 1)], min_val=1, max_val=blocks)
                    ch.restart()
                    with dve.Fori(b0, b1) as b:
                        ch.restart()
                        for a in range(2):
                            when(dve, c, gathered[a], (b + 1) * (16 * HALF))
                            if vector_scores:
                                for k in range(HALF):
                                    ch.add(dve.scalar_tensor_tensor(e[:, k, :], got[:, a, k, 0:D], got[:, a, k, SC:RW],
                                                                    neighbours[:, bass.ds(t * D, D)], ALU.add, ALU.add))
                                ch.join()
                            else:
                                er = c.er[:, bass.ds(t * 8, H)].unsqueeze(1).broadcast_to([P, HALF, H])
                                ch(dve.tensor_tensor(e[:, 0:HALF, :], got[:, a, :, SC:RW], er, ALU.add))
                                ch(dve.scalar_tensor_tensor(e[:, 0:HALF, :], e[:, 0:HALF, :], SLOPE, e[:, 0:HALF, :], ALU.mult, ALU.max))
                            ch(dve.tensor_reduce(top[:, :], e[:, :, :].rearrange("p s h -> p h s"), AX, ALU.max))
                            ch(dve.tensor_tensor(d[:, :, :], e[:, :, :], top[:, :].unsqueeze(1).broadcast_to([P, HALF + 1, H]), ALU.subtract))
                            dve.sem_inc(shifted, 1)
                            ch.add(dve.tensor_copy(e[:, HALF, :], top[:, :]))
                            ch.add(dve.memset(got[:, a, :, SC:RW], FLOOR))
                            ch.join()
                            when(dve, c, weighed, b * 2 + (a + 1))
                            if DH > 1:
                                ch.add(dve.tensor_tensor(
                                    v[:, :, :].rearrange("p s (h d) -> p s h d", h=H),
                                    got[:, a, :, V0:V0 + VW].rearrange("p s (h d) -> p s h d", h=H),
                                    p[:, 0:HALF, :].unsqueeze(3).broadcast_to([P, HALF, H, DH]), ALU.mult))
                                ch.add(dve.tensor_tensor(by_head(acc[:, :]), by_head(acc[:, :]), spread(p[:, HALF, :]), ALU.mult))
                            else:
                                ch.add(dve.tensor_tensor(v[:, :, :], got[:, a, :, V0:V0 + VW], p[:, 0:HALF, :], ALU.mult))
                                ch.add(dve.tensor_tensor(acc[:, :], acc[:, :], p[:, HALF, :], ALU.mult))
                            ch.join()
                            dve.sem_inc(freed[a], 1)
                            ch.add(dve.tensor_tensor(p[:, HALF, :], p[:, HALF, :], den[:, :], ALU.mult))
                            ch.add(dve.tensor_reduce(part[:, :], v[:, :, :].rearrange("p s w -> p w s"), AX, ALU.add))
                            ch.join()
                            ch.add(dve.tensor_reduce(den[:, :], p[:, :, :].rearrange("p s h -> p h s"), AX, ALU.add))
                            ch.add(dve.tensor_tensor(acc[:, :], acc[:, :], part[:, :], ALU.add))
                            ch.join()
                    ch.restart()
                    if fallback:
                        ch(dve.tensor_scalar(top[:, :], den[:, :], 0.0, None, ALU.is_equal))
                        ch(dve.tensor_tensor(den[:, :], den[:, :], top[:, :], ALU.add))
                        ch(dve.tensor_tensor(part[:, :], top[:, :], self_row[:, V0:V0 + VW], ALU.mult))
                        ch(dve.reciprocal(rden[:, :], den[:, :]))
                        ch(dve.tensor_tensor(acc[:, :], acc[:, :], rden[:, :], ALU.mult))
                        ch(dve.tensor_tensor(acc[:, :], acc[:, :], part[:, :], ALU.add))
                    else:
                        if tiny:
                            ch(dve.tensor_scalar(den[:, :], den[:, :], tiny, None, ALU.add))
                        ch(dve.reciprocal(rden[:, :], den[:, :]))
                        ch(dve.tensor_tensor(by_head(acc[:, :]), by_head(acc[:, :]), spread(rden[:, :]), ALU.mult))
                    if need_self:
                        dve.sem_inc(self_free, 1)
                    if bias is not None:
                        ch(dve.tensor_tensor(acc[:, :], acc[:, :], bias_all[:, :], ALU.add))
                    if relu:
                        ch(dve.tensor_scalar(acc[:, :], acc[:, :], 0.0, None, ALU.max))
                    target = out[:, bass.ds(t * VW, VW)]
                    if add:
                        ch(dve.tensor_tensor(target, target, acc[:, :], ALU.add))
                    else:
                        ch(dve.tensor_copy(target, acc[:, :]))
                ch.restart()


def set_weights(nc, c, name, edge_table, base_row, wmat):
    blocks = edge_table.shape[0] // (P * SLOTS)
    with stage(nc, name) as st:
        sb, sem = st.sb, st.sem
        blk = sb("blk", [P, SLOTS, 2], I32)
        src = sb("src", [P, SLOTS])
        mask = sb("mask", [P, D])
        wt = sb("wt", [P, KT, D])
        chain_sem, loaded, freed, filled, flipped = (sem(n) for n in ("chain", "loaded", "freed", "filled", "flipped"))
        ps = c.psum
        with nc.Block() as block:

            @block.sync
            def _(sp):
                with sp.Fori(0, KT) as t:
                    b0 = sp.value_load(base_row[0:1, bass.ds(t, 1)], min_val=0, max_val=blocks - 1)
                    b1 = sp.value_load(base_row[0:1, bass.ds(t + 1, 1)], min_val=1, max_val=blocks)
                    with sp.Fori(b0, b1) as b:
                        when(sp, c, freed, b + 1)
                        sp.dma_start(blk[:, :, :], edge_table[bass.ds(b * (P * SLOTS), P * SLOTS), :].rearrange(
                            "(p s) w -> p s w", s=SLOTS)).then_inc(loaded, 16)

            @block.vector
            def _(dve):
                ch = Chain(dve, chain_sem)
                dve.sem_inc(freed, 1)
                ch(dve.memset(wt[:, :, :], 0.0))
                ch.restart()
                for t in range(KT):
                    b0 = dve.value_load(base_row[0:1, t:t + 1], min_val=0, max_val=blocks - 1)
                    b1 = dve.value_load(base_row[0:1, t + 1:t + 2], min_val=1, max_val=blocks)
                    with dve.Fori(b0, b1) as b:
                        ch.restart()
                        when(dve, c, loaded, (b + 1) * 16)
                        ch(dve.tensor_copy(src[:, :], blk[:, :, 0]))
                        for k in range(SLOTS):
                            ch(dve.tensor_scalar(mask[:, :], c.iota[:, 0:D], src[:, k:k + 1], None, ALU.is_equal))
                            ch(dve.copy_predicated(wt[:, t, :], mask[:, :].bitcast(I32), blk[:, k, 1:2].bitcast(F32).broadcast_to([P, D])))
                        dve.sem_inc(freed, 1)
                    ch.restart()
                dve.sem_inc(filled, 1)
                dve.wait_ge(flipped, 1)
                for k in range(KT):
                    ch(dve.tensor_copy(wmat[:, k, :], ps[:, k, 0:D]))

            @block.tensor
            def _(pe):
                pe.wait_ge(filled, 1)
                for k in range(KT):
                    for n in range(KT):
                        ins = pe.transpose(ps[:, k, n * P:(n + 1) * P], wt[:, n, k * P:(k + 1) * P], c.ident[:, :])
                ins.then_inc(flipped, 1)


def gate(nc, c, name, E, mode, agg=None, gamma=None, beta=None):
    NT = c.NT
    with stage(nc, name) as st:
        sb, sem = st.sb, st.sem
        s, t1, oh1, oh2 = (sb(n, [P, NT, E]) for n in ("s", "t1", "oh1", "oh2"))
        m1, m2, i1, u, z, w1, w2 = (sb(n, [P, NT]) for n in ("m1", "m2", "i1", "u", "z", "w1", "w2"))
        chain_sem, shifted, exped, loaded = sem("chain"), sem("shifted"), sem("exped"), sem("loaded")
        if agg is not None:
            W = 16
            cen, sq = sb("cen", [P, NT, W]), sb("sq", [P, NT, W])
            gam, bet = sb("gam", [P, W]), sb("bet", [P, W])
        lg = c.lg[:, :].rearrange("p (t e) -> p t e", e=8)[:, :, 0:E]
        g = c.g[:, :].rearrange("p (t e) -> p t e", e=8)[:, :, 0:E]
        io = c.iota[:, 0:E].unsqueeze(1).broadcast_to([P, NT, E])
        sp3 = lambda ap: ap.unsqueeze(2).broadcast_to([P, NT, E])

        with nc.Block() as block:

            @block.sync
            def _(sp):
                if agg is not None:
                    for tile, v in ((gam, gamma), (bet, beta)):
                        sp.dma_start(tile[:, :], v.rearrange("(o n) -> o n", o=1).broadcast_to([P, 16])).then_inc(loaded, 16)

            @block.vector
            def _(dve):
                ch = Chain(dve, chain_sem)
                if agg is not None:
                    a3 = agg[:, :].rearrange("p (t w) -> p t w", w=16)
                    sp16 = lambda ap: ap.unsqueeze(2).broadcast_to([P, NT, 16])
                    across = lambda ap: ap.unsqueeze(1).broadcast_to([P, NT, 16])
                    ch(dve.tensor_reduce(u[:, :], a3, AX, ALU.add))
                    ch(dve.tensor_scalar(u[:, :], u[:, :], 1.0 / 16, None, ALU.mult))
                    ch(dve.tensor_tensor(cen[:, :, :], a3, sp16(u[:, :]), ALU.subtract))
                    ch(dve.tensor_tensor(sq[:, :, :], cen[:, :, :], cen[:, :, :], ALU.mult))
                    ch(dve.tensor_reduce(z[:, :], sq[:, :, :], AX, ALU.add))
                    ch(dve.tensor_scalar(z[:, :], z[:, :], 1.0 / 16, LN_EPS, ALU.mult, ALU.add))
                    dve.sem_inc(shifted, 1)
                    dve.wait_ge(exped, 1)
                    ch(dve.reciprocal(z[:, :], z[:, :]))
                    ch(dve.tensor_tensor(cen[:, :, :], cen[:, :, :], sp16(z[:, :]), ALU.mult))
                    dve.wait_ge(loaded, 32)
                    ch(dve.tensor_tensor(cen[:, :, :], cen[:, :, :], across(gam[:, :]), ALU.mult))
                    ch(dve.tensor_tensor(cen[:, :, :], cen[:, :, :], across(bet[:, :]), ALU.add))
                    v4 = cen[:, :, :].rearrange("p t (h e) -> p t e h", e=E)
                    ch(dve.tensor_reduce(s[:, :, :], v4, AX, ALU.add))
                    ch(dve.tensor_scalar(s[:, :, :], s[:, :, :], 0.25, None, ALU.mult))
                else:
                    ch(dve.tensor_copy(s[:, :, :], lg))
                if mode in ("softmax2", "normalised"):
                    ch(dve.tensor_reduce(m1[:, :], s[:, :, :], AX, ALU.max))
                    ch(dve.tensor_tensor(t1[:, :, :], s[:, :, :], sp3(m1[:, :]), ALU.subtract))
                    dve.sem_inc(shifted, 1)
                    dve.wait_ge(exped, 1)
                    ch(dve.tensor_reduce(u[:, :], t1[:, :, :], AX, ALU.add))
                    ch(dve.reciprocal(z[:, :], u[:, :]))
                    ch(dve.tensor_tensor(s[:, :, :], t1[:, :, :], sp3(z[:, :]), ALU.mult))

                def best(m, oh):
                    ch(dve.tensor_reduce(m[:, :], s[:, :, :], AX, ALU.max))
                    ch(dve.tensor_tensor(t1[:, :, :], s[:, :, :], sp3(m[:, :]), ALU.is_lt))
                    ch(dve.tensor_scalar(t1[:, :, :], t1[:, :, :], float(E), None, ALU.mult))
                    ch(dve.tensor_tensor(t1[:, :, :], t1[:, :, :], io, ALU.add))
                    ch(dve.tensor_reduce(i1[:, :], t1[:, :, :], AX, ALU.min))
                    ch(dve.tensor_tensor(oh[:, :, :], io, sp3(i1[:, :]), ALU.is_equal))

                best(m1, oh1)
                ch(dve.scalar_tensor_tensor(s[:, :, :].rearrange("p t e -> p (t e)"), oh1[:, :, :].rearrange("p t e -> p (t e)"), FLOOR,
                                            s[:, :, :].rearrange("p t e -> p (t e)"), ALU.mult, ALU.add))
                best(m2, oh2)
                if mode == "mask":
                    ch(dve.tensor_tensor(g, oh1[:, :, :], oh2[:, :, :], ALU.add))
                    return
                if mode in ("softmax", "softmax2"):
                    ch(dve.tensor_tensor(u[:, :], m2[:, :], m1[:, :], ALU.subtract))
                    dve.sem_inc(shifted, 1)
                    dve.wait_ge(exped, 2)
                    ch(dve.tensor_scalar(z[:, :], u[:, :], 1.0, None, ALU.add))
                    ch(dve.reciprocal(w1[:, :], z[:, :]))
                    ch(dve.tensor_tensor(w2[:, :], u[:, :], w1[:, :], ALU.mult))
                else:
                    ch(dve.tensor_tensor(u[:, :], m2[:, :], m1[:, :], ALU.add))
                    ch(dve.tensor_scalar(u[:, :], u[:, :], 1e-12, None, ALU.max))
                    ch(dve.reciprocal(z[:, :], u[:, :]))
                    ch(dve.tensor_tensor(w1[:, :], m1[:, :], z[:, :], ALU.mult))
                    ch(dve.tensor_tensor(w2[:, :], m2[:, :], z[:, :], ALU.mult))
                ch(dve.tensor_tensor(oh1[:, :, :], oh1[:, :, :], sp3(w1[:, :]), ALU.mult))
                ch(dve.tensor_tensor(oh2[:, :, :], oh2[:, :, :], sp3(w2[:, :]), ALU.mult))
                ch(dve.tensor_tensor(g, oh1[:, :, :], oh2[:, :, :], ALU.add))

            @block.scalar
            def _(act):
                n = 0
                if agg is not None:
                    n += 1
                    act.wait_ge(shifted, n)
                    act.activation(z[:, :], z[:, :], ACT.Sqrt).then_inc(exped, 1)
                if mode in ("softmax2", "normalised"):
                    n += 1
                    act.wait_ge(shifted, n)
                    act.activation(t1[:, :, :], t1[:, :, :], ACT.Exp).then_inc(exped, 1)
                if mode in ("softmax", "softmax2"):
                    n += 1
                    act.wait_ge(shifted, n)
                    act.activation(u[:, :], u[:, :], ACT.Exp).then_inc(exped, 1)


def experts(nc, c, name, E, func, layers):
    inner, (w_last, b_last) = layers[:-1], layers[-1]
    C = U
    HALVES = ((0, 3), (3, 5))
    turns = c.NT // C
    NL = len(inner)
    sizes = [w.shape[2] // P for w, _ in inner]
    HT = sizes[-1]
    with stage(nc, name) as st:
        sb, sem = st.sb, st.sem
        w = [sb(f"w{l}", [P, 2, wl.shape[1] // P, wl.shape[2]]) for l, (wl, _) in enumerate(inner)]
        wl_sb = sb("w_last", [P, 2, HT, D])
        b = [sb(f"b{l}", [P, 2, sizes[l]]) for l in range(NL)]
        b_sb = sb("b_last", [1, 2, 2, D])
        h = [sb(f"h{l}", [P, sizes[l] if l < NL - 1 else 2, C * P]) for l in range(NL)]
        loaded = [sem("loaded_a"), sem("loaded_b")]
        product = sem("product")
        hidden = sem("hidden")
        added = sem("added")
        used = sem("used")
        chain_sem = sem("chain")
        ps = c.psum
        per_turn = sum(sizes)
        credits = 2 * turns * HT
        n_loads = 2 * NL + 3
        xt = c.xt[:, :].rearrange("p (t k n) -> p t k n", k=KT, n=P)

        with nc.Block() as block:

            @block.sync
            def _(sp):
                with nc.allow_non_contiguous_dma(reason="biases, one column per block"), sp.Fori(0, E // 2) as pair:
                    for a in range(2):
                        e = pair * 2 + a
                        when(sp, c, used, (e + 1) * (turns * HT))
                        for l, (wl, bl) in enumerate(inner):
                            sp.dma_start(w[l][:, a, :, :], wl[bass.ds(e, 1), :, :].rearrange("o (k p) n -> p (o k) n", p=P)).then_inc(loaded[a], 16)
                            sp.dma_start(b[l][:, a, :], bl[bass.ds(e, 1), :].rearrange("o (k p) -> p (o k)", p=P)).then_inc(loaded[a], 16)
                        sp.dma_start(wl_sb[:, a, :, :], w_last[bass.ds(e, 1), :, :].rearrange("o (k p) n -> p (o k) n", p=P)).then_inc(loaded[a], 16)
                        for r in range(2):
                            sp.dma_start(b_sb[:, a, r, :], b_last[bass.ds(e, 1), :]).then_inc(loaded[a], 16)

            @block.tensor
            def _(pe):
                pe.sem_inc(used, credits)
                with pe.Fori(0, E // 2) as pair:
                    for a in range(2):
                        e = pair * 2 + a
                        when(pe, c, loaded[a], (pair + 1) * (16 * n_loads))
                        with pe.Fori(0, turns) as i:
                            turn = e * turns + i
                            q = 0

                            def outputs(m):
                                when(pe, c, hidden, turn * per_turn + (2 + per_turn - HT + m + 1))
                                if m == 0:
                                    when(pe, c, added, turn + 1)
                                    for y in range(3):
                                        n = min(2, C - 2 * y)
                                        pe.matmul(ps[:, 4 + y, 0:n * D], c.ones[0:1, :],
                                                  b_sb[:, a, 0:n, :].rearrange("o r d -> o (r d)"), start=True, stop=False,
                                                  skip_group_check=True)
                                for j in range(C):
                                    ins = pe.matmul(ps[:, 4 + j // 2, (j % 2) * D:(j % 2 + 1) * D],
                                                    h[-1][:, m % 2, j * P:(j + 1) * P], wl_sb[:, a, m, :],
                                                    start=False, stop=(m == HT - 1), skip_group_check=True)
                                ins.then_inc(used, 1)

                            for l in range(NL):
                                for m in range(sizes[l]):
                                    when(pe, c, hidden, turn * per_turn + (q + 1))
                                    if l:
                                        when(pe, c, hidden, turn * per_turn + (2 + sizes[0]) )
                                    kn = w[l].shape[2]
                                    for y, (lo, hi) in enumerate(HALVES):
                                        for k in range(kn):
                                            rhs = (xt[:, bass.ds(i * C + lo, hi - lo), k, :] if l == 0
                                                   else h[l - 1][:, k, lo * P:hi * P])
                                            ins = pe.matmul(ps[:, 2 * (q % 2) + y, 0:(hi - lo) * P], w[l][:, a, k, m * P:(m + 1) * P],
                                                            rhs, start=(k == 0), stop=(k == kn - 1))
                                    ins.then_inc(product, 1)
                                    q += 1
                                    if l == NL - 1 and m >= 1:
                                        outputs(m - 1)
                            outputs(HT - 1)

            @block.scalar
            def _(act):
                act.sem_inc(hidden, 2)
                with act.Fori(0, E // 2) as pair:
                    for a in range(2):
                        e = pair * 2 + a
                        with act.Fori(0, turns) as i:
                            turn = e * turns + i
                            q = 0
                            for l in range(NL):
                                for m in range(sizes[l]):
                                    when(act, c, product, turn * per_turn + (q + 1))
                                    if l == NL - 1:
                                        when(act, c, used, turn * HT + (credits + m - 1))
                                    for y, (lo, hi) in enumerate(HALVES):
                                        ins = act.activation(h[l][:, m % 2 if l == NL - 1 else m, lo * P:hi * P],
                                                             ps[:, 2 * (q % 2) + y, 0:(hi - lo) * P], func,
                                                             bias=b[l][:, a, m:m + 1])
                                    ins.then_inc(hidden, 1)
                                    q += 1

            @block.vector
            def _(dve):
                ch = Chain(dve, chain_sem)
                dve.sem_inc(added, 1)
                with dve.Fori(0, E // 2) as pair:
                    for a in range(2):
                        e = pair * 2 + a
                        with dve.Fori(0, turns) as i:
                            ch.restart()
                            when(dve, c, used, (e * turns + i + 1) * HT + credits)
                            for j in range(C):
                                t = i * C + j
                                target = c.x[:, bass.ds(t * D, D)]
                                ch.add(dve.scalar_tensor_tensor(target, ps[:, 4 + j // 2, (j % 2) * D:(j % 2 + 1) * D],
                                                                c.g[:, bass.ds(t * 8 + e, 1)], target, ALU.mult, ALU.add))
                            ch.join()
                            dve.sem_inc(added, 1)
                ch.restart()


def gnn_transformer_kernel(nc, a, out):
    c = Core()
    c.N = a["x"].shape[0]
    c.NT = -(-c.N // P)
    NT = c.NT
    tail = c.N - (NT - 1) * P
    rows_of = lambda w: nc.dram_tensor(f"rows_{w}_{nc.next_id()}", (NT * P, w), F32, kind="Internal").ap()

    def blocks_of(edges):
        return -(-edges // SLOTS) + NT + 1

    with ExitStack() as ctx:
        def sb(name, shape, dt=F32):
            return ctx.enter_context(nc.sbuf_tensor(name, shape, dt))

        c.x = sb("x", [P, NT * D])
        c.xt = sb("xt", [P, NT * D])
        c.er = sb("er", [P, NT * 8])
        c.lg = sb("lg", [P, NT * 8])
        c.g = sb("g", [P, NT * 8])
        agg = sb("agg", [P, NT * 16])
        wmat = sb("wmat", [P, KT, D])
        c.ident, c.before, c.ones = sb("ident", [P, P]), sb("before", [P, P]), sb("ones", [P, P])
        c.iota, iota_i = sb("iota", [P, D]), sb("iota_i", [P, D], I32)
        base_main, base_gate = sb("base_main", [1, NT + 1], I32), sb("base_gate", [1, NT + 1], I32)
        c.psum = ctx.enter_context(nc.psum_tensor("ps", [P, 8, 512], F32))
        c.passed = nc.alloc_semaphore("passed")
        E_main, E_gate = a["src"].shape[0], a["L1_ffn_edge_index"].shape[1]
        table_main = nc.dram_tensor("table_main", (blocks_of(E_main) * P * SLOTS, 2), I32, kind="Internal").ap()
        table_gate = nc.dram_tensor("table_gate", (blocks_of(E_gate) * P * SLOTS, 2), I32, kind="Internal").ap()

        with stage(nc, "begin") as st:
            loaded, counted, cleared, filled = (st.sem(n) for n in ("loaded", "counted", "cleared", "filled"))
            with nc.Block() as block:

                @block.sync
                def _(sp):
                    sp.dma_start(c.x[:, 0:(NT - 1) * D].rearrange("p (t d) -> p t d", d=D),
                                 a["x"][0:(NT - 1) * P, :].rearrange("(t p) d -> p t d", p=P)).then_inc(loaded, 16)
                    sp.wait_ge(cleared, 1)
                    sp.dma_start(c.x[0:tail, (NT - 1) * D:NT * D], a["x"][(NT - 1) * P:c.N, :]).then_inc(loaded, 16)
                    sp.wait_ge(loaded, 32)
                    sp.sem_inc(c.passed, 1)

                @block.vector
                def _(dve):
                    dve.memset(c.x[:, (NT - 1) * D:NT * D], 0.0).then_inc(cleared, 1)
                    dve.memset(c.ones[:, :], 1.0)
                    dve.wait_ge(counted, 1)
                    dve.tensor_copy(c.iota[:, :], iota_i[:, :])

                @block.gpsimd
                def _(pool):
                    pool.iota(iota_i[:, :], pattern=[[1, D]], base=0, channel_multiplier=0).then_inc(counted, 1)
                    pool.memset(c.ident[:, :], 0.0).then_inc(filled, 1)
                    pool.memset(c.before[:, :], 1.0).then_inc(filled, 1)
                    pool.wait_ge(filled, 2)
                    pool.affine_select(out=c.ident[:, :], in_=c.ident[:, :], compare_op=ALU.not_equal, fill=1.0,
                                       base=0, pattern=[[-1, P]], channel_multiplier=1)
                    pool.affine_select(out=c.before[:, :], in_=c.before[:, :], compare_op=ALU.is_gt, fill=0.0,
                                       base=0, pattern=[[1, P]], channel_multiplier=-1)

        build_edge_table(nc, c, "main", a["dst"], a["src"], a["edge_weight"].bitcast(I32), E_main, 17, table_main, base_main)
        gate_src, gate_dst = a["L1_ffn_edge_index"][0, :], a["L1_ffn_edge_index"][1, :]
        build_edge_table(nc, c, "gate", gate_dst, gate_src, gate_src, E_gate, 16, table_gate, base_gate)

        by_block = lambda w: w.rearrange("(k p) n -> p k n", p=P)

        for l in range(2):
            rows = rows_of(D + 1)
            prepare(nc, c, f"l0p{l}", c.xt if l else c.x, by_block(a["L0_gnn_W"][l]), D, norm=(l == 0),
                    attend=(1, a["L0_gnn_attn_l"][l], a["L0_gnn_attn_r"][l]), rows=rows)
            attend_edges(nc, c, f"l0a{l}", table_main, base_main, rows, 1, D, loops=True, bias=a["L0_gnn_bias"][l],
                         relu=(l == 0), out=c.x if l else c.xt, add=(l == 1))
        prepare(nc, c, "l0f", c.x, by_block(a["L0_ffn_Wg"]), 8, bias=[(0, a["L0_ffn_bg"])], scores=c.lg, keep_xt=True)
        gate(nc, c, "l0g", 8, "mask")
        experts(nc, c, "l0e", 8, ACT.Gelu, [(a["L0_ffn_W1"], a["L0_ffn_b1"]), (a["L0_ffn_W2"], a["L0_ffn_b2"])])

        set_weights(nc, c, "l1w", table_main, base_main, wmat)
        prepare(nc, c, "l1p", c.x, None, D, ready=wmat, add=True)
        rows = rows_of(16 + 4)
        flat = lambda v: v.rearrange("h d -> (h d)")
        prepare(nc, c, "l1f", c.x, by_block(a["L1_ffn_W_gat"]), 16,
                attend=(4, flat(a["L1_ffn_att_src"]), flat(a["L1_ffn_att_dst"])), rows=rows, keep_xt=True)
        attend_edges(nc, c, "l1a", table_gate, base_gate, rows, 4, 4, loops=True, tiny=1e-16, bias=a["L1_ffn_b_gat"], out=agg)
        gate(nc, c, "l1g", 4, "softmax", agg=agg, gamma=a["L1_ffn_ln_gamma"], beta=a["L1_ffn_ln_beta"])
        experts(nc, c, "l1e", 4, ACT.Gelu, [(a["L1_ffn_W1"], a["L1_ffn_b1"]), (a["L1_ffn_W2"], a["L1_ffn_b2"])])

        rows = rows_of(2 * D + 1)
        prepare(nc, c, "l2p", c.x, (a["L2_gnn_W_self"], a["L2_gnn_W_nb"]), 2 * D, transposed=True,
                bias=[(0, a["L2_gnn_b_self"]), (D, a["L2_gnn_b_nb"])], rows=rows, xn_rows=True, neighbours=c.xt)
        attend_edges(nc, c, "l2a", table_main, base_main, rows, D, 1, neighbours=c.xt, fallback=True, out=c.x, add=True)
        prepare(nc, c, "l2f", c.x, a["L2_ffn_router_w2"], 6, bias=[(0, a["L2_ffn_router_b2"])],
                hidden=(a["L2_ffn_router_w1"], a["L2_ffn_router_b1"]), scores=c.lg, keep_xt=True)
        gate(nc, c, "l2g", 6, "softmax2")
        experts(nc, c, "l2e", 6, ACT.Relu, [(a["L2_ffn_expert_w1"], a["L2_ffn_expert_b1"]),
                                            (a["L2_ffn_expert_w2"], a["L2_ffn_expert_b2"]),
                                            (a["L2_ffn_expert_w3"], a["L2_ffn_expert_b3"])])

        rows = rows_of(D + 8)
        prepare(nc, c, "l3p", c.x, a["L3_gnn_W"].rearrange("(k p) h d -> p k (h d)", p=P), D,
                attend=(8, flat(a["L3_gnn_att_src"]), flat(a["L3_gnn_att_dst"])), rows=rows)
        attend_edges(nc, c, "l3a", table_main, base_main, rows, 8, D // 8, tiny=1e-16, bias=a["L3_gnn_bias"], relu=True,
                     out=c.x, add=True)
        prepare(nc, c, "l3f", c.x, a["L3_ffn_router_w"].rearrange("e (k p) -> p k e", p=P), 8, scores=c.lg, keep_xt=True,
                add_xn=True)
        gate(nc, c, "l3g", 8, "normalised")
        experts(nc, c, "l3e", 8, ACT.Gelu, [(a["L3_ffn_w1"], a["L3_ffn_b1"]), (a["L3_ffn_w2"], a["L3_ffn_b2"])])

        with stage(nc, "end") as st:
            stored = st.sem("stored")
            with nc.Block() as block:

                @block.sync
                def _(sp):
                    sp.dma_start(out[0:(NT - 1) * P, :].rearrange("(t p) d -> p t d", p=P),
                                 c.x[:, 0:(NT - 1) * D].rearrange("p (t d) -> p t d", d=D)).then_inc(stored, 16)
                    sp.dma_start(out[(NT - 1) * P:c.N, :], c.x[0:tail, (NT - 1) * D:NT * D]).then_inc(stored, 16)
                    sp.wait_ge(stored, 32)


def kernel(**inputs):
    import numpy as _np
    import concourse.bacc as _bacc
    from concourse import mybir as _mybir
    from concourse.bass_utils import run_bass_kernel_spmd as _run

    nc = _bacc.Bacc("TRN2", target_bir_lowering=False, num_devices=1)
    arrays, args = {}, {}
    for name, value in inputs.items():
        v = _np.ascontiguousarray(value)
        arrays[f"in_{name}_dram"] = v
        args[name] = nc.dram_tensor(f"in_{name}_dram", v.shape, _mybir.dt.from_np(v.dtype), kind="ExternalInput").ap()
    out = nc.dram_tensor("out_0_dram", tuple(inputs["x"].shape), _mybir.dt.float32, kind="ExternalOutput").ap()
    gnn_transformer_kernel(nc, args, out)
    r = _run(nc, [arrays], core_ids=[0])
    return r.results[0]["out_0_dram"]
```

```python
from contextlib import ExitStack, contextmanager

import concourse.bass as bass
from concourse import mybir

ALU = mybir.AluOpType
ACT = mybir.ActivationFunctionType
F32 = mybir.dt.float32
I32 = mybir.dt.int32
U32 = mybir.dt.uint32
AX = mybir.AxisListType.X

P = 128
D = 256
KT = D // P
LN_EPS = 1e-5
SLOPE = 0.2
U = 5
SLOTS = 8
NODE_BITS = 12
LO_BITS = 6
LO = 1 << LO_BITS
DROPPED = 4095
NOBODY = 8191
FLOOR = -1e30
START = -1e25


class Core:
    pass


class Stage:

    def __init__(self, nc, name):
        self.nc, self.name = nc, name
        self.stack = ExitStack()
        self.sems = []

    def sb(self, name, shape, dt=F32):
        return self.stack.enter_context(self.nc.sbuf_tensor(f"{self.name}_{name}", shape, dt))

    def sem(self, name):
        s = self.nc.alloc_semaphore(f"{self.name}_{name}")
        self.sems.append(s)
        return s


@contextmanager
def stage(nc, name):
    st = Stage(nc, name)
    yield st
    st.stack.close()
    nc.clear_and_free_semaphores(st.sems)
    nc.all_engine_barrier()


class Chain:

    def __init__(self, eng, sem):
        self.eng, self.sem, self.n = eng, sem, 0

    def __call__(self, ins):
        self.n += 1
        ins.then_inc(self.sem, 1)
        self.eng.wait_ge(self.sem, self.n)

    def add(self, ins):
        self.n += 1
        ins.then_inc(self.sem, 1)

    def join(self):
        self.eng.wait_ge(self.sem, self.n)

    def restart(self):
        self.eng.sem_clear(self.sem)
        self.n = 0


def when(eng, c, sem, value):
    eng.wait_ge(sem, value)
    eng.sem_inc(c.passed, 1)



def build_edge_table(nc, c, name, dst, src, weight, edges, half, table, base_row):
    NT = c.NT
    F = -(-edges // P)
    whole = edges // F
    rest = edges - whole * F
    turns = F // (2 * half)
    assert turns * 2 * half == F
    HI = 2 * NT
    rows = table.shape[0]
    sorted_lo = nc.dram_tensor(f"{name}_sorted_lo", (1 + P * F, 2), I32, kind="Internal").ap()

    with stage(nc, name) as st:
        sb, sem = st.sb, st.sem
        dst_i, src_i = sb("dst_i", [P, F], I32), sb("src_i", [P, F], I32)
        pay = sb("pay", [P, F, 2], I32)
        prev = sb("prev", [P, F, 2], I32)
        digit, other = sb("digit", [P, F]), sb("other", [P, F])
        eq, run, pos, keep = sb("eq", [P, F]), sb("run", [P, F]), sb("pos", [P, F]), sb("keep", [P, F])
        pos_i = sb("pos_i", [P, F], I32)
        tmp_i = sb("tmp_i", [P, F], I32)
        pay_s, pos_s = sb("pay_s", [P, 2, half, 2], I32), sb("pos_s", [P, 2, half], I32)
        cnt, base = sb("cnt", [P, LO]), sb("base", [P, LO])
        tot, cum = sb("tot", [P, LO]), sb("cum", [P, LO])
        last, allsame = sb("last", [P, LO]), sb("allsame", [P, LO])
        last_t, same_t, carry_t, peak_t = (sb(n, [LO, P]) for n in ("last_t", "same_t", "carry_t", "peak_t"))
        peak = sb("peak", [LO, 2])
        row, row2, row3 = sb("row", [1, LO]), sb("row2", [1, LO]), sb("row3", [1, LO])
        row_i = sb("row_i", [1, LO], I32)
        bases = sb("bases", [P, NT + 1])
        empty = sb("empty", [P, SLOTS, 2], I32)
        zrow = sb("zrow", [1, 2], I32)
        loaded, chain_sem, stored, counted = (sem(n) for n in ("loaded", "chain", "stored", "counted"))
        staged, sent = [sem("staged_a"), sem("staged_b")], [sem("sent_a"), sem("sent_b")]
        free = [sem("free_a"), sem("free_b")]
        reloaded, based, emptied, cleared, mm = sem("reloaded"), sem("based"), sem("emptied"), sem("cleared"), sem("mm")
        ps = c.psum

        with nc.Block() as block:

            @block.sync
            def _(sp):
                def rows_of(tile, ap):
                    sp.wait_ge(cleared, 2)
                    sp.dma_start(tile[0:whole, :], ap[0:whole * F].rearrange("(p f) -> p f", f=F)).then_inc(loaded, 16)
                    if rest:
                        sp.dma_start(tile[whole:whole + 1, 0:rest],
                                     ap[whole * F:edges].rearrange("(a f) -> a f", a=1)).then_inc(loaded, 16)

                rows_of(dst_i, dst)
                rows_of(src_i, src)
                rows_of(tmp_i, weight)
                sp.dma_start(sorted_lo[0:1, :], zrow[:, :]).then_inc(stored, 16)

                def relay(second):
                    with sp.Fori(0, turns) as i:
                        for a in range(2):
                            when(sp, c, sent[a], (i + (1 + second * turns)) * (16 * half))
                            sp.sem_inc(free[a], 1)

                for a in range(2):
                    sp.sem_inc(free[a], 1)
                relay(0)
                sp.wait_ge(stored, 16)
                sp.wait_ge(sent[0], 16 * half * turns)
                sp.wait_ge(sent[1], 16 * half * turns)
                sp.dma_start(pay[:, :, :], sorted_lo[1:1 + P * F, :].rearrange("(p f) w -> p f w", f=F)).then_inc(reloaded, 16)
                sp.dma_start(prev[:, :, :], sorted_lo[0:P * F, :].rearrange("(p f) w -> p f w", f=F)).then_inc(reloaded, 16)
                sp.wait_ge(based, 1)
                n = sp.value_load(base_row[0:1, NT:NT + 1], min_val=1, max_val=rows // (P * SLOTS) - 4)
                with sp.Fori(0, n + 3) as b:
                    sp.dma_start(table[bass.ds(b * (P * SLOTS), P * SLOTS), :].rearrange("(p s) w -> p s w", s=SLOTS),
                                 empty[:, :, :]).then_inc(stored, 16)
                sp.wait_ge(stored, n * 16 + 64)
                sp.sem_inc(emptied, 1)
                relay(1)

            @block.vector
            def _(dve):
                ch = Chain(dve, chain_sem)
                dve.memset(dst_i[:, :], DROPPED).then_inc(cleared, 1)
                dve.memset(src_i[:, :], 0)
                dve.memset(zrow[:, :], 0)
                dve.memset(empty[:, :, :], NOBODY)
                dve.memset(pos[:, :], 0.0)
                ch(dve.memset(tmp_i[:, :], 0))
                dve.sem_inc(cleared, 1)
                dve.wait_ge(loaded, (96 if rest else 48))
                ch(dve.tensor_scalar(other[:, :], src_i[:, :], float(c.N - 1), None, ALU.min))
                ch(dve.tensor_scalar(digit[:, :], dst_i[:, :], float(DROPPED), float(1 << NODE_BITS), ALU.min, ALU.mult))
                ch(dve.tensor_tensor(other[:, :], digit[:, :], other[:, :], ALU.add))
                ch.add(dve.tensor_copy(pay[:, :, 0], other[:, :]))
                ch.add(dve.tensor_copy(pay[:, :, 1], tmp_i[:, :]))
                ch(dve.tensor_scalar(digit[:, :], dst_i[:, :], float(DROPPED), None, ALU.min))
                ch(dve.tensor_copy(dst_i[:, :], digit[:, :]))
                ch(dve.tensor_scalar(src_i[:, :], dst_i[:, :], LO - 1, None, ALU.bitwise_and))
                ch(dve.tensor_copy(digit[:, :], src_i[:, :]))
                ch(dve.memset(keep[:, :], 1.0))
                with dve.Fori(0, LO) as b:
                    ch.restart()
                    ch(dve.tensor_scalar(eq[:, :], digit[:, :], c.iota[:, bass.ds(b, 1)], None, ALU.is_equal))
                    ch(dve.tensor_reduce(cnt[:, bass.ds(b, 1)], eq[:, :], AX, ALU.add))
                ch.restart()
                dve.sem_inc(counted, 1)
                dve.wait_ge(mm, 1)
                ch(dve.tensor_copy(tot[:, :], ps[:, 1, 0:LO]))
                ch(dve.tensor_tensor_scan(cum[:, :], keep[:, 0:LO], tot[:, :], 0.0, ALU.mult, ALU.add))
                ch(dve.tensor_tensor(cum[:, :], cum[:, :], tot[:, :], ALU.subtract))
                ch(dve.tensor_tensor(base[:, :], cum[:, :], ps[:, 0, 0:LO], ALU.add))

                def positions(n):
                    with dve.Fori(0, n) as b:
                        ch.restart()
                        ch(dve.tensor_scalar(eq[:, :], digit[:, :], c.iota[:, bass.ds(b, 1)], None, ALU.is_equal))
                        ch(dve.tensor_tensor_scan(run[:, :], keep[:, :], eq[:, :], base[:, bass.ds(b, 1)], ALU.mult, ALU.add))
                        ch.add(dve.tensor_reduce(cnt[:, bass.ds(b, 1)], run[:, :], AX, ALU.max))
                        ch.add(dve.copy_predicated(pos[:, :], eq[:, :].bitcast(I32), run[:, :]))
                        ch.join()
                    ch.restart()

                def stage_out(second):
                    with dve.Fori(0, turns) as i:
                        ch.restart()
                        for a in range(2):
                            when(dve, c, free[a], i + (1 + second * turns))
                            col = i * (2 * half) + a * half
                            ch.add(dve.tensor_copy(pay_s[:, a, :, :], pay[:, bass.ds(col, half), :]))
                            ch.add(dve.tensor_copy(pos_s[:, a, :], pos_i[:, bass.ds(col, half)]))
                            ch.join()
                            dve.sem_inc(staged[a], 1)
                    ch.restart()

                positions(LO)
                ch(dve.tensor_copy(pos_i[:, :], pos[:, :]))
                stage_out(0)
                dve.wait_ge(reloaded, 32)
                ch(dve.tensor_scalar(dst_i[:, :], pay[:, :, 0], NODE_BITS, LO - 1, ALU.logical_shift_right, ALU.bitwise_and))
                ch(dve.tensor_scalar(src_i[:, :], prev[:, :, 0], NODE_BITS, LO - 1, ALU.logical_shift_right, ALU.bitwise_and))
                ch(dve.tensor_copy(other[:, :], dst_i[:, :]))
                ch(dve.tensor_copy(eq[:, :], src_i[:, :]))
                ch(dve.tensor_tensor(keep[:, :], other[:, :], eq[:, :], ALU.is_equal))
                ch(dve.tensor_scalar(tmp_i[:, :], pay[:, :, 0], NODE_BITS + LO_BITS, None, ALU.logical_shift_right))
                ch(dve.tensor_copy(digit[:, :], tmp_i[:, :]))
                ch(dve.memset(last[:, :], 0.0))
                ch(dve.tensor_reduce(cum[:, 0:1], keep[:, :], AX, ALU.min))
                ch(dve.tensor_copy(allsame[:, :], cum[:, 0:1].broadcast_to([P, LO])))
                with dve.Fori(0, HI) as b:
                    ch.restart()
                    ch(dve.tensor_scalar(eq[:, :], digit[:, :], c.iota[:, bass.ds(b, 1)], None, ALU.is_equal))
                    ch(dve.tensor_tensor_scan(run[:, :], keep[:, :], eq[:, :], 0.0, ALU.mult, ALU.add))
                    ch(dve.tensor_copy(last[:, bass.ds(b, 1)], run[:, F - 1:F]))
                ch.restart()
                dve.sem_inc(counted, 1)
                dve.wait_ge(mm, 2)
                ch.add(dve.tensor_copy(last_t[:, :], ps[0:LO, 0, 0:P]))
                ch.add(dve.tensor_copy(same_t[:, :], ps[0:LO, 1, 0:P]))
                ch(dve.memset(carry_t[:, 0:1], 0.0))
                ch(dve.tensor_tensor_scan(carry_t[:, 1:P], same_t[:, 0:P - 1], last_t[:, 0:P - 1], 0.0, ALU.mult, ALU.add))
                dve.sem_inc(counted, 1)
                dve.wait_ge(mm, 3)
                ch(dve.tensor_copy(base[:, :], ps[:, 2, 0:LO]))
                ch(dve.memset(pos[:, :], 1.0))
                ch(dve.memset(cnt[:, :], 0.0))
                positions(HI)
                dve.sem_inc(counted, 1)
                dve.wait_ge(mm, 4)
                ch(dve.tensor_copy(peak_t[:, :], ps[0:LO, 3, 0:P]))
                ch(dve.tensor_reduce(peak[:, 0:1], peak_t[:, :], AX, ALU.max))
                dve.sem_inc(counted, 1)
                dve.wait_ge(mm, 5)
                ch(dve.tensor_copy(row[:, :], ps[0:1, 4, 0:LO]))
                pairs = row[:, 0:HI].rearrange("a (t two) -> a t two", two=2)
                ch(dve.tensor_tensor(row2[:, 0:NT], pairs[:, :, 0], pairs[:, :, 1], ALU.max))
                ch(dve.tensor_scalar(row2[:, 0:NT], row2[:, 0:NT], 1.0, float(SLOTS - 1), ALU.max, ALU.add))
                ch(dve.tensor_copy(row_i[:, 0:NT], row2[:, 0:NT]))
                ch(dve.tensor_scalar(row_i[:, 0:NT], row_i[:, 0:NT], SLOTS.bit_length() - 1, None, ALU.logical_shift_right))
                ch(dve.tensor_copy(row2[:, 0:NT], row_i[:, 0:NT]))
                ch(dve.memset(row3[:, 0:1], 0.0))
                ch(dve.memset(row[:, :], 1.0))
                ch(dve.tensor_tensor_scan(row3[:, 1:NT + 1], row[:, 0:NT], row2[:, 0:NT], 0.0, ALU.mult, ALU.add))
                ch(dve.tensor_copy(base_row[:, 0:NT + 1], row3[:, 0:NT + 1]))
                dve.sem_inc(counted, 1)
                dve.sem_inc(based, 1)
                dve.wait_ge(mm, 6)
                ch(dve.tensor_copy(bases[:, :], ps[:, 5, 0:NT + 1]))
                ch(dve.tensor_scalar(pos[:, :], pos[:, :], -1.0, None, ALU.add))
                ch(dve.tensor_copy(pos_i[:, :], pos[:, :]))
                ch(dve.tensor_scalar(tmp_i[:, :], pos_i[:, :], SLOTS - 1, None, ALU.bitwise_and))
                ch(dve.tensor_copy(run[:, :], tmp_i[:, :]))
                ch(dve.tensor_tensor(pos[:, :], pos[:, :], run[:, :], ALU.subtract))
                ch(dve.scalar_tensor_tensor(pos[:, :], pos[:, :], float(P), run[:, :], ALU.mult, ALU.add))
                ch(dve.tensor_scalar(tmp_i[:, :], pay[:, :, 0], NODE_BITS, P - 1, ALU.logical_shift_right, ALU.bitwise_and))
                ch(dve.tensor_copy(run[:, :], tmp_i[:, :]))
                ch(dve.scalar_tensor_tensor(pos[:, :], run[:, :], float(SLOTS), pos[:, :], ALU.mult, ALU.add))
                ch(dve.tensor_scalar(tmp_i[:, :], pay[:, :, 0], NODE_BITS + 7, None, ALU.logical_shift_right))
                ch(dve.tensor_copy(digit[:, :], tmp_i[:, :]))
                ch(dve.tensor_scalar(run[:, :], digit[:, :], float(NT), float(rows), ALU.is_ge, ALU.mult))
                ch(dve.tensor_tensor(pos[:, :], pos[:, :], run[:, :], ALU.add))
                with dve.Fori(0, NT) as b:
                    ch.restart()
                    ch(dve.tensor_scalar(run[:, :], digit[:, :], c.iota[:, bass.ds(b, 1)], bases[:, bass.ds(b, 1)], ALU.is_equal, ALU.mult))
                    ch(dve.scalar_tensor_tensor(pos[:, :], run[:, :], float(P * SLOTS), pos[:, :], ALU.mult, ALU.add))
                ch.restart()
                ch(dve.tensor_copy(pos_i[:, :], pos[:, :]))
                ch(dve.tensor_scalar(tmp_i[:, :], pay[:, :, 0], (1 << NODE_BITS) - 1, None, ALU.bitwise_and))
                ch(dve.tensor_copy(pay[:, :, 0], tmp_i[:, :]))
                stage_out(1)

            @block.tensor
            def _(pe):
                pe.wait_ge(counted, 1)
                pe.matmul(ps[:, 0, 0:LO], c.before[:, :], cnt[:, :], start=True, stop=True)
                pe.matmul(ps[:, 1, 0:LO], c.ones[:, :], cnt[:, :], start=True, stop=True).then_inc(mm, 1)
                pe.wait_ge(counted, 2)
                pe.transpose(ps[0:LO, 0, 0:P], last[:, :], c.ident[:, :])
                pe.transpose(ps[0:LO, 1, 0:P], allsame[:, :], c.ident[:, :]).then_inc(mm, 1)
                pe.wait_ge(counted, 3)
                pe.transpose(ps[:, 2, 0:LO], carry_t[:, :], c.ident[0:LO, 0:LO]).then_inc(mm, 1)
                pe.wait_ge(counted, 4)
                pe.transpose(ps[0:LO, 3, 0:P], cnt[:, :], c.ident[:, :]).then_inc(mm, 1)
                pe.wait_ge(counted, 5)
                pe.transpose(ps[0:1, 4, 0:LO], peak[:, 0:1], c.ident[0:LO, 0:LO]).then_inc(mm, 1)
                pe.wait_ge(counted, 6)
                pe.matmul(ps[:, 5, 0:NT + 1], c.ones[0:1, :], row3[:, 0:NT + 1], start=True, stop=True).then_inc(mm, 1)

            @block.gpsimd
            def _(pool):
                for second in range(2):
                    if second:
                        pool.wait_ge(emptied, 1)
                    with pool.Fori(0, turns) as i:
                        for a in range(2):
                            when(pool, c, staged[a], i + (1 + second * turns))
                            for k in range(half):
                                pool.indirect_dma_start(
                                    out=(table[:, :] if second else sorted_lo[:, :]),
                                    out_offset=bass.IndirectOffsetOnAxis(ap=pos_s[:, a, k:k + 1].bitcast(U32), axis=0),
                                    in_=pay_s[:, a, k, :], in_offset=None,
                                    bounds_check=rows - 1 if second else P * F, oob_is_err=False).then_inc(sent[a], 16)
                pool.wait_ge(sent[0], 16 * half * (2 * turns))
                pool.wait_ge(sent[1], 16 * half * (2 * turns))
                pool.sem_inc(c.passed, 1)



def normalise(dve, ch, c, src, i, stats, moments, rstd, xn, varied, rooted):
    for j in range(U):
        ch.add(dve.bn_stats(stats[:, j, :], src[:, bass.ds((i * U + j) * D, D)]))
    ch.join()
    for j in range(U):
        ch.add(dve.bn_aggr(moments[:, j, :], stats[:, j, :]))
    ch.join()
    ch(dve.tensor_scalar(rstd[:, :], moments[:, :, 1], LN_EPS, None, ALU.add))
    dve.sem_inc(varied, 1)
    when(dve, c, rooted, i + 1)
    ch(dve.reciprocal(rstd[:, :], rstd[:, :]))
    for j in range(U):
        ch.add(dve.tensor_scalar(xn[:, j, :], src[:, bass.ds((i * U + j) * D, D)], moments[:, j, 0:1], rstd[:, j:j + 1],
                                 ALU.subtract, ALU.mult))
    ch.join()


def prepare(nc, c, name, src, weights, width, norm=True, bias=None, attend=None, transposed=False,
            hidden=None, rows=None, xn_rows=False, scores=None, neighbours=None, keep_xt=False, add=False, ready=None, add_xn=False):
    NB = c.NT // U
    H = attend[0] if attend else 0
    N = width + 2 * H
    row_width = (width + H) if not xn_rows else 2 * D
    with stage(nc, name) as st:
        sb, sem = st.sb, st.sem
        w = ready if ready is not None else sb("w", [P, KT, N])
        stats, moments, rstd = sb("stats", [P, U, 6]), sb("moments", [P, U, 2]), sb("rstd", [P, U])
        xn, xt = sb("xn", [P, U, D]), sb("xt", [P, U, D])
        out_rows = sb("rows", [P, U, row_width]) if rows is not None else None
        if attend:
            vec = sb("vec", [P, 2, width])
            prod = sb("prod", [P, width])
        if transposed:
            raw = sb("raw", [P, 2, KT, D])
        bias_row = sb("bias", [1, N]) if bias is not None else None
        if hidden:
            w1 = sb("w1", [P, KT, P])
            b1 = sb("b1", [P, 1])
            hid = sb("hid", [P, U, P])
        chain_sem, loaded, weighed, flipped_w = (sem(n) for n in ("chain", "loaded", "weighed", "flipped_w"))
        normed = sem("normed")
        flipped = sem("flipped")
        turned = sem("turned")
        kept = sem("kept")
        multiplied = sem("multiplied")
        taken = sem("taken")
        evacuated = sem("evacuated")
        filled = sem("filled")
        sent = sem("sent")
        stored = sem("stored")
        hidden_in, hidden_out = sem("hidden_in"), sem("hidden_out")
        varied, rooted = sem("varied"), sem("rooted")
        ps = c.psum
        loads = []
        if ready is None and not transposed:
            if hidden:
                loads.append((w[:, 0, 0:width], weights))
            else:
                loads += [(w[:, k, 0:width], weights[:, k, :]) for k in range(KT)]
        if transposed:
            for a in range(2):
                loads.append((raw[:, a, :, :], weights[a].rearrange("(k p) n -> p k n", p=P)))
        if attend:
            for a in range(2):
                loads.append((vec[:, a, :], attend[1 + a].rearrange("(o n) -> o n", o=1).broadcast_to([P, width])))
        if bias is not None:
            for off, b in bias:
                loads.append((bias_row[:, off:off + b.shape[0]], b.rearrange("(o n) -> o n", o=1)))
        if hidden:
            loads.append((w1[:, :, :], hidden[0].rearrange("(k p) n -> p k n", p=P)))
            loads.append((b1[:, :], hidden[1].rearrange("(p o) -> p o", o=1)))

        with nc.Block() as block:

            @block.sync
            def _(sp):
                with nc.allow_non_contiguous_dma(reason="small weights, loaded once"):
                    for tile, source in loads:
                        sp.dma_start(tile, source).then_inc(loaded, 16)
                if rows is not None:
                    sp.sem_inc(stored, 1)
                    with sp.Fori(0, NB) as i:
                        if xn_rows:
                            when(sp, c, filled, i + 1)
                        when(sp, c, evacuated, (i + 2) * U)
                        sp.dma_start(rows[bass.ds(i * (U * P), U * P), 0:row_width].rearrange("(j p) w -> p j w", p=P),
                                     out_rows[:, :, :]).then_inc(sent, 16)
                        when(sp, c, sent, (i + 1) * 16)
                        sp.sem_inc(stored, 1)

            @block.vector
            def _(dve):
                ch = Chain(dve, chain_sem)
                dve.sem_inc(taken, U)
                if loads:
                    dve.wait_ge(loaded, 16 * len(loads))
                if attend:
                    for a in range(2):
                        for k in range(KT):
                            ch(dve.tensor_tensor(prod[:, :], w[:, k, 0:width], vec[:, a, :], ALU.mult))
                            ch(dve.tensor_reduce(w[:, k, width + a * H:width + (a + 1) * H],
                                                 prod[:, :].rearrange("p (h d) -> p h d", h=H), AX, ALU.add))
                if transposed:
                    for a in range(2):
                        dve.wait_ge(flipped_w, a + 1)
                        for k in range(KT):
                            ch(dve.tensor_copy(w[:, k, a * D:(a + 1) * D], ps[:, 2 * a + k, 0:D]))
                dve.sem_inc(weighed, 1)
                ch.restart()
                with dve.Fori(0, NB) as i:
                    ch.restart()
                    when(dve, c, flipped, i + 1)
                    if norm:
                        normalise(dve, ch, c, src, i, stats, moments, rstd, xn, varied, rooted)
                    else:
                        ch(dve.tensor_copy(xn[:, :, :].rearrange("p u d -> p (u d)"), src[:, bass.ds(i * (U * D), U * D)]))
                    dve.sem_inc(normed, 1)
                    if add_xn:
                        whole = c.x[:, bass.ds(i * (U * D), U * D)]
                        ch(dve.tensor_tensor(whole, whole, xn[:, :, :].rearrange("p u d -> p (u d)"), ALU.add))
                    if xn_rows:
                        when(dve, c, stored, i + 1)
                        ch(dve.tensor_copy(out_rows[:, :, D:2 * D], xn[:, :, :]))
                        dve.sem_inc(filled, 1)
                    for j in range(U):
                        t = i * U + j
                        when(dve, c, evacuated, t + U + 1) if rows is not None else when(dve, c, multiplied, t + 1)
                        if attend:
                            ch(dve.tensor_copy(c.er[:, bass.ds(t * 8, H)], ps[:, 3 + j, width + H:width + 2 * H]))
                        if neighbours is not None:
                            ch(dve.tensor_copy(neighbours[:, bass.ds(t * D, D)], ps[:, 3 + j, D:2 * D]))
                        if scores is not None:
                            ch(dve.tensor_copy(scores[:, bass.ds(t * 8, width)], ps[:, 3 + j, 0:width]))
                        if add:
                            ch(dve.tensor_tensor(c.x[:, bass.ds(t * D, D)], ps[:, 3 + j, 0:D], c.x[:, bass.ds(t * D, D)], ALU.add))
                        dve.sem_inc(taken, 1)
                ch.restart()

            @block.tensor
            def _(pe):
                pe.sem_inc(flipped, 1)
                if transposed:
                    pe.wait_ge(loaded, 16 * len(loads))
                    for a in range(2):
                        for k in range(KT):
                            for n in range(KT):
                                ins = pe.transpose(ps[:, 2 * a + k, n * P:(n + 1) * P], raw[:, a, n, k * P:(k + 1) * P], c.ident[:, :])
                        ins.then_inc(flipped_w, 1)
                pe.wait_ge(weighed, 1)
                with pe.Fori(0, NB) as i:
                    when(pe, c, normed, i + 1)
                    when(pe, c, turned, i + 1)
                    for j in range(U):
                        for k in range(KT):
                            ins = pe.transpose(ps[:, j // 2, (j % 2) * D + k * P:(j % 2) * D + (k + 1) * P],
                                               xn[:, j, k * P:(k + 1) * P], c.ident[:, :])
                    ins.then_inc(flipped, 1)
                    when(pe, c, turned, i + 2)
                    if hidden:
                        for j in range(U):
                            when(pe, c, taken, i * U + j + 1)
                            for k in range(KT):
                                ins = pe.matmul(ps[:, 3 + j, 0:P], w1[:, k, :], xt[:, j, k * P:(k + 1) * P],
                                                start=(k == 0), stop=(k == KT - 1))
                            ins.then_inc(hidden_in, 1)
                    for j in range(U):
                        t = i * U + j
                        if hidden:
                            when(pe, c, hidden_out, t + 1)
                            pe.matmul(ps[:, 3 + j, 0:N], hid[:, j, :], w[:, 0, 0:N], start=True, stop=False)
                        else:
                            when(pe, c, taken, t + 1)
                            if rows is not None:
                                when(pe, c, evacuated, t + 1)
                            for k in range(KT):
                                ins = pe.matmul(ps[:, 3 + j, 0:N], xt[:, j, k * P:(k + 1) * P], w[:, k, 0:N],
                                                start=(k == 0), stop=(k == KT - 1 and bias is None))
                        if bias is not None:
                            ins = pe.matmul(ps[:, 3 + j, 0:N], c.ones[0:1, :], bias_row[:, :], start=False, stop=True)
                        ins.then_inc(multiplied, 1)

            @block.scalar
            def _(act):
                act.sem_inc(turned, 1)
                if rows is not None:
                    act.sem_inc(evacuated, U)
                with act.Fori(0, NB) as i:
                    if norm:
                        when(act, c, varied, i + 1)
                        act.activation(rstd[:, :], rstd[:, :], ACT.Sqrt).then_inc(rooted, 1)
                    when(act, c, flipped, i + 2)
                    if keep_xt:
                        when(act, c, kept, i + 1)
                    for q in range(3):
                        n = min(2, U - 2 * q)
                        ins = act.activation(xt[:, 2 * q:2 * q + n, :].rearrange("p u d -> p (u d)"), ps[:, q, 0:n * D], ACT.Copy)
                    ins.then_inc(turned, 1)
                    if hidden:
                        for j in range(U):
                            when(act, c, hidden_in, i * U + j + 1)
                            act.activation(hid[:, j, :], ps[:, 3 + j, 0:P], ACT.Relu, bias=b1[:, :]).then_inc(hidden_out, 1)
                    if rows is not None:
                        when(act, c, stored, i + 1)
                        for j in range(U):
                            when(act, c, multiplied, i * U + j + 1)
                            n = D if xn_rows else width + H
                            act.activation(out_rows[:, j, 0:n], ps[:, 3 + j, 0:n], ACT.Copy).then_inc(evacuated, 1)

            @block.gpsimd
            def _(pool):
                if keep_xt:
                    pool.sem_inc(kept, 1)
                    with pool.Fori(0, NB) as i:
                        when(pool, c, turned, i + 2)
                        pool.tensor_copy(c.xt[:, bass.ds(i * (U * D), U * D)], xt[:, :, :].rearrange("p u d -> p (u d)")).then_inc(kept, 1)


def attend_edges(nc, c, name, table, base_row, rows, H, DH, loops=False, tiny=0.0, bias=None, relu=False,
                 out=None, add=False, neighbours=None, fallback=False):
    VW = H * DH
    by_feature = neighbours is not None
    SC = 0 if by_feature else VW
    V0 = D if by_feature else 0
    RW = VW + H
    blocks = table.shape[0] // (P * SLOTS)
    with stage(nc, name) as st:
        sb, sem = st.sb, st.sem
        idx = sb("idx", [P, 2, SLOTS, 2], I32)
        got = sb("got", [P, 2 * SLOTS * RW])
        self_row = sb("self_row", [P, RW])
        e = sb("e", [P, SLOTS + 1, H]) if not by_feature else None
        d = sb("d", [P, SLOTS + 1, H])
        p = sb("p", [P, SLOTS + 1, H]) if not by_feature else None
        v = sb("v", [P, SLOTS, VW]) if not by_feature else None
        PV = (SLOTS + 1) * 2 * D
        pv = sb("pv", [P, 2 * PV]) if by_feature else None
        zeros = sb("zeros", [P, 2 * D]) if by_feature else None
        later = sb("later", [P, 1])
        top, new, rden = sb("top", [P, H]), sb("new", [P, H]), sb("rden", [P, H])
        both = sb("both", [P, H + VW])
        den, acc = both[:, 0:H], both[:, H:H + VW]
        part = sb("part", [P, VW])
        bias_all = sb("bias", [P, VW]) if bias is not None else None
        chain_sem, loaded = sem("chain"), sem("loaded")
        self_in, self_free = sem("self_in"), sem("self_free")
        idx_in = [sem("idx_in_a"), sem("idx_in_b")]
        gathered = [sem("got_a"), sem("got_b")]
        arrived = sem("arrived")
        freed = sem("freed")
        shifted, weighed = sem("shifted"), sem("weighed")
        valued, summed = sem("valued"), sem("summed")
        reset = sem("reset")
        need_self = loops or fallback
        ps = c.psum

        def tiles(eng, body, before=None, after=None):
            with eng.Fori(0, c.NT) as t:
                if before:
                    before(t)
                b0 = eng.value_load(base_row[0:1, bass.ds(t, 1)], min_val=0, max_val=blocks - 2)
                b1 = eng.value_load(base_row[0:1, bass.ds(t + 1, 1)], min_val=1, max_val=blocks - 1)
                with eng.Fori(b0, b1) as b:
                    body(t, b)
                if after:
                    after(t, b1)

        def buffer(b, lo, hi):
            rows_b = got[:, bass.ds((b % 2) * (SLOTS * RW), SLOTS * RW)].rearrange("p (s w) -> p s w", w=RW)
            return rows_b[:, :, lo:hi]

        def weights_of(b):
            return pv[:, bass.ds((b % 2) * PV, PV)].rearrange("p (s two d) -> p s two d", two=2, d=D)

        with nc.Block() as block:

            @block.sync
            def _(sp):
                if bias is not None:
                    sp.dma_start(bias_all[:, :], bias.rearrange("(o n) -> o n", o=1).broadcast_to([P, VW])).then_inc(loaded, 16)
                total = sp.value_load(base_row[0:1, c.NT:c.NT + 1], min_val=1, max_val=blocks - 4)

                def load(b, a):
                    sp.dma_start(idx[:, a, :, :], table[bass.ds(b * (P * SLOTS), P * SLOTS), :].rearrange(
                        "(p s) w -> p s w", s=SLOTS)).then_inc(idx_in[a], 16)

                for a in range(2):
                    load(a, a)
                with sp.Fori(0, (total + 1) // 2) as q:
                    for a in range(2):
                        when(sp, c, gathered[a], (q + 1) * (16 * SLOTS))
                        sp.sem_inc(arrived, 1)
                        load(q * 2 + (2 + a), a)
                for a in range(2):
                    when(sp, c, idx_in[a], ((total + 1) // 2 + 1) * 16)

            @block.gpsimd
            def _(pool):
                total = pool.value_load(base_row[0:1, c.NT:c.NT + 1], min_val=1, max_val=blocks - 4)
                with pool.Fori(0, (total + 1) // 2) as q:
                    for a in range(2):
                        when(pool, c, idx_in[a], (q + 1) * 16)
                        when(pool, c, freed, q * 2 + (a + 1))
                        if by_feature:
                            when(pool, c, reset, q * 2 + (a + 1))
                        for k in range(SLOTS):
                            at = (a * SLOTS + k) * RW
                            pool.indirect_dma_start(
                                out=got[:, at:at + RW], out_offset=None, in_=rows[:, :],
                                in_offset=bass.IndirectOffsetOnAxis(ap=idx[:, a, k, 0:1].bitcast(U32), axis=0),
                                bounds_check=c.N - 1, oob_is_err=False).then_inc(gathered[a], 16)

            @block.scalar
            def _(act):
                if by_feature:
                    act.sem_inc(reset, 2)

                def load_self(t):
                    when(act, c, self_free, t + 1)
                    act.dma_start(self_row[:, :], rows[bass.ds(t * P, P), 0:RW]).then_inc(self_in, 16)

                def exponentials(t, b):
                    when(act, c, shifted, b + 1)
                    act.activation(weights_of(b)[:, :, 0, :] if by_feature else p[:, :, :], d[:, :, :], ACT.Exp).then_inc(weighed, 1)
                    if by_feature:
                        scores = buffer(b, 0, D)
                        act.activation(scores, scores, ACT.Copy, bias=FLOOR, scale=0.0).then_inc(reset, 1)

                tiles(act, exponentials, before=load_self if need_self else None)

            if by_feature:
                @block.tensor
                def _(pe):
                    pe.wait_ge(loaded, 1)
                    pe.matmul(ps[:, 1, :], c.ident[:, :], zeros[:, :], start=True, stop=True).then_inc(summed, 1)

                    def sums(t, b):
                        when(pe, c, valued, b + 1)
                        bank = (b % 2) * 512
                        for k in range(SLOTS):
                            ins = pe.matmul(ps[:, :, :].rearrange("p b n -> p (b n)")[:, bass.ds(bank, 512)], c.ident[:, :],
                                            pv[:, bass.ds((b % 2) * PV + k * (2 * D), 2 * D)],
                                            start=(k == 0), stop=(k == SLOTS - 1))
                        ins.then_inc(summed, 1)

                    tiles(pe, sums)

            @block.vector
            def _(dve):
                ch = Chain(dve, chain_sem)
                ch(dve.memset(got[:, :], FLOOR))
                if by_feature:
                    ch(dve.memset(zeros[:, :], 0.0))
                    ch(dve.memset(pv[:, :], 0.0))
                    dve.sem_inc(loaded, 1)
                dve.sem_inc(self_free, 1)
                dve.sem_inc(freed, 2)
                if bias is not None:
                    dve.wait_ge(loaded, 16)
                ch.restart()
                by_head = lambda ap: ap.rearrange("p (h d) -> p h d", h=H)
                spread = lambda ap: ap.unsqueeze(2).broadcast_to([P, H, DH])

                def begin(t):
                    ch.restart()
                    if need_self:
                        when(dve, c, self_in, (t + 1) * 16)
                    if loops:
                        ch(dve.tensor_tensor(top[:, :], self_row[:, SC:SC + H], c.er[:, bass.ds(t * 8, H)], ALU.add))
                        ch.add(dve.scalar_tensor_tensor(e[:, SLOTS, :], top[:, :], SLOPE, top[:, :], ALU.mult, ALU.max))
                        ch.add(dve.memset(den, 1.0))
                        ch.add(dve.tensor_copy(acc, self_row[:, 0:VW]))
                    else:
                        ch.add(dve.memset(top[:, :] if by_feature else e[:, SLOTS, :], START))
                        ch.add(dve.memset(both[:, :], 0.0))
                        ch.add(dve.memset(later[:, :], 0.0))
                    ch.join()

                def by_heads(t, b):
                    ch.restart()
                    when(dve, c, arrived, b + 1)
                    er = c.er[:, bass.ds(t * 8, H)].unsqueeze(1).broadcast_to([P, SLOTS, H])
                    ch(dve.tensor_tensor(e[:, 0:SLOTS, :], buffer(b, SC, SC + H), er, ALU.add))
                    ch(dve.scalar_tensor_tensor(e[:, 0:SLOTS, :], e[:, 0:SLOTS, :], SLOPE, e[:, 0:SLOTS, :], ALU.mult, ALU.max))
                    ch(dve.tensor_reduce(top[:, :], e[:, :, :].rearrange("p s h -> p h s"), AX, ALU.max))
                    ch(dve.tensor_tensor(d[:, :, :], e[:, :, :], top[:, :].unsqueeze(1).broadcast_to([P, SLOTS + 1, H]), ALU.subtract))
                    dve.sem_inc(shifted, 1)
                    ch.add(dve.tensor_copy(e[:, SLOTS, :], top[:, :]))
                    ch.add(dve.tensor_scalar(buffer(b, SC, SC + H), d[:, 0:SLOTS, :], 0.0, FLOOR, ALU.mult, ALU.add))
                    ch.join()
                    when(dve, c, weighed, b + 1)
                    ch.add(dve.tensor_tensor(
                        v[:, :, :].rearrange("p s (h d) -> p s h d", h=H),
                        buffer(b, V0, V0 + VW).rearrange("p s (h d) -> p s h d", h=H),
                        p[:, 0:SLOTS, :].unsqueeze(3).broadcast_to([P, SLOTS, H, DH]), ALU.mult))
                    ch.add(dve.tensor_tensor(by_head(acc), by_head(acc), spread(p[:, SLOTS, :]), ALU.mult))
                    ch.join()
                    dve.sem_inc(freed, 1)
                    ch.add(dve.tensor_tensor(p[:, SLOTS, :], p[:, SLOTS, :], den, ALU.mult))
                    ch.add(dve.tensor_reduce(part[:, :], v[:, :, :].rearrange("p s w -> p w s"), AX, ALU.add))
                    ch.join()
                    ch.add(dve.tensor_reduce(den, p[:, :, :].rearrange("p s h -> p h s"), AX, ALU.add))
                    ch.add(dve.tensor_tensor(acc, acc, part[:, :], ALU.add))
                    ch.join()

                def rescale(b_next):
                    two = both[:, :].rearrange("p (two d) -> p two d", two=2)
                    ch(dve.tensor_tensor(two, two, weights_of(b_next + 1)[:, SLOTS, 0, :].unsqueeze(1).broadcast_to([P, 2, D]), ALU.mult))

                def add_sums(b_next):
                    when(dve, c, summed, b_next + 1)
                    bank = ps[:, :, :].rearrange("p b n -> p (b n)")[:, bass.ds(((b_next + 1) % 2) * 512, 512)]
                    ch(dve.scalar_tensor_tensor(both[:, :], bank, later[:, :], both[:, :], ALU.mult, ALU.add))

                def by_features(t, b):
                    ch.restart()
                    when(dve, c, arrived, b + 1)
                    near = neighbours[:, bass.ds(t * D, D)]
                    ch(dve.tensor_reduce(new[:, :], buffer(b, 0, D).rearrange("p s w -> p w s"), AX, ALU.max))
                    ch(dve.tensor_tensor(new[:, :], new[:, :], near, ALU.add))
                    ch(dve.tensor_tensor(new[:, :], new[:, :], top[:, :], ALU.max))
                    ch.add(dve.tensor_tensor(d[:, SLOTS, :], top[:, :], new[:, :], ALU.subtract))
                    ch.add(dve.tensor_tensor(part[:, :], new[:, :], near, ALU.subtract))
                    ch.join()
                    ch.add(dve.tensor_tensor(d[:, 0:SLOTS, :], buffer(b, 0, D), part[:, :].unsqueeze(1).broadcast_to([P, SLOTS, D]), ALU.subtract))
                    ch.add(dve.tensor_copy(top[:, :], new[:, :]))
                    ch.join()
                    dve.sem_inc(shifted, 1)
                    rescale(b)
                    when(dve, c, weighed, b + 1)
                    w_b = weights_of(b)
                    ch.add(dve.tensor_tensor(w_b[:, 0:SLOTS, 1, :], buffer(b, D, 2 * D), w_b[:, 0:SLOTS, 0, :], ALU.mult))
                    ch.join()
                    dve.sem_inc(valued, 1)
                    dve.sem_inc(freed, 1)
                    add_sums(b)
                    ch(dve.memset(later[:, :], 1.0))

                def finish(t, b1):
                    ch.restart()
                    if by_feature:
                        rescale(b1)
                        add_sums(b1)
                    if fallback:
                        ch(dve.tensor_scalar(top[:, :], den, 0.0, None, ALU.is_equal))
                        ch(dve.tensor_tensor(den, den, top[:, :], ALU.add))
                        ch(dve.tensor_tensor(part[:, :], top[:, :], self_row[:, V0:V0 + VW], ALU.mult))
                        ch(dve.reciprocal(rden[:, :], den))
                        ch(dve.tensor_tensor(acc, acc, rden[:, :], ALU.mult))
                        ch(dve.tensor_tensor(acc, acc, part[:, :], ALU.add))
                    else:
                        if tiny:
                            ch(dve.tensor_scalar(den, den, tiny, None, ALU.add))
                        ch(dve.reciprocal(rden[:, :], den))
                        ch(dve.tensor_tensor(by_head(acc), by_head(acc), spread(rden[:, :]), ALU.mult))
                    if need_self:
                        dve.sem_inc(self_free, 1)
                    if bias is not None:
                        ch(dve.tensor_tensor(acc, acc, bias_all[:, :], ALU.add))
                    if relu:
                        ch(dve.tensor_scalar(acc, acc, 0.0, None, ALU.max))
                    target = out[:, bass.ds(t * VW, VW)]
                    if add:
                        ch(dve.tensor_tensor(target, target, acc, ALU.add))
                    else:
                        ch(dve.tensor_copy(target, acc))

                tiles(dve, by_features if by_feature else by_heads, before=begin, after=finish)
                ch.restart()


def set_weights(nc, c, name, edge_table, base_row, wmat):
    blocks = edge_table.shape[0] // (P * SLOTS)
    with stage(nc, name) as st:
        sb, sem = st.sb, st.sem
        blk = sb("blk", [P, SLOTS, 2], I32)
        src = sb("src", [P, SLOTS])
        mask = sb("mask", [P, D])
        wt = sb("wt", [P, KT, D])
        chain_sem, loaded, freed, filled, flipped = (sem(n) for n in ("chain", "loaded", "freed", "filled", "flipped"))
        ps = c.psum
        with nc.Block() as block:

            @block.sync
            def _(sp):
                with sp.Fori(0, KT) as t:
                    b0 = sp.value_load(base_row[0:1, bass.ds(t, 1)], min_val=0, max_val=blocks - 1)
                    b1 = sp.value_load(base_row[0:1, bass.ds(t + 1, 1)], min_val=1, max_val=blocks)
                    with sp.Fori(b0, b1) as b:
                        when(sp, c, freed, b + 1)
                        sp.dma_start(blk[:, :, :], edge_table[bass.ds(b * (P * SLOTS), P * SLOTS), :].rearrange(
                            "(p s) w -> p s w", s=SLOTS)).then_inc(loaded, 16)

            @block.vector
            def _(dve):
                ch = Chain(dve, chain_sem)
                dve.sem_inc(freed, 1)
                ch(dve.memset(wt[:, :, :], 0.0))
                ch.restart()
                for t in range(KT):
                    b0 = dve.value_load(base_row[0:1, t:t + 1], min_val=0, max_val=blocks - 1)
                    b1 = dve.value_load(base_row[0:1, t + 1:t + 2], min_val=1, max_val=blocks)
                    with dve.Fori(b0, b1) as b:
                        ch.restart()
                        when(dve, c, loaded, (b + 1) * 16)
                        ch(dve.tensor_copy(src[:, :], blk[:, :, 0]))
                        for k in range(SLOTS):
                            ch(dve.tensor_scalar(mask[:, :], c.iota[:, 0:D], src[:, k:k + 1], None, ALU.is_equal))
                            ch(dve.copy_predicated(wt[:, t, :], mask[:, :].bitcast(I32), blk[:, k, 1:2].bitcast(F32).broadcast_to([P, D])))
                        dve.sem_inc(freed, 1)
                    ch.restart()
                dve.sem_inc(filled, 1)
                dve.wait_ge(flipped, 1)
                for k in range(KT):
                    ch(dve.tensor_copy(wmat[:, k, :], ps[:, k, 0:D]))

            @block.tensor
            def _(pe):
                pe.wait_ge(filled, 1)
                for k in range(KT):
                    for n in range(KT):
                        ins = pe.transpose(ps[:, k, n * P:(n + 1) * P], wt[:, n, k * P:(k + 1) * P], c.ident[:, :])
                ins.then_inc(flipped, 1)


def gate(nc, c, name, E, mode, agg=None, gamma=None, beta=None):
    NT = c.NT
    with stage(nc, name) as st:
        sb, sem = st.sb, st.sem
        s, t1, oh1, oh2 = (sb(n, [P, NT, E]) for n in ("s", "t1", "oh1", "oh2"))
        m1, m2, i1, u, z, w1, w2 = (sb(n, [P, NT]) for n in ("m1", "m2", "i1", "u", "z", "w1", "w2"))
        chain_sem, shifted, exped, loaded = sem("chain"), sem("shifted"), sem("exped"), sem("loaded")
        if agg is not None:
            W = 16
            cen, sq = sb("cen", [P, NT, W]), sb("sq", [P, NT, W])
            gam, bet = sb("gam", [P, W]), sb("bet", [P, W])
        lg = c.lg[:, :].rearrange("p (t e) -> p t e", e=8)[:, :, 0:E]
        g = c.g[:, :].rearrange("p (t e) -> p t e", e=8)[:, :, 0:E]
        io = c.iota[:, 0:E].unsqueeze(1).broadcast_to([P, NT, E])
        sp3 = lambda ap: ap.unsqueeze(2).broadcast_to([P, NT, E])

        with nc.Block() as block:

            @block.sync
            def _(sp):
                if agg is not None:
                    for tile, v in ((gam, gamma), (bet, beta)):
                        sp.dma_start(tile[:, :], v.rearrange("(o n) -> o n", o=1).broadcast_to([P, 16])).then_inc(loaded, 16)

            @block.vector
            def _(dve):
                ch = Chain(dve, chain_sem)
                if agg is not None:
                    a3 = agg[:, :].rearrange("p (t w) -> p t w", w=16)
                    sp16 = lambda ap: ap.unsqueeze(2).broadcast_to([P, NT, 16])
                    across = lambda ap: ap.unsqueeze(1).broadcast_to([P, NT, 16])
                    ch(dve.tensor_reduce(u[:, :], a3, AX, ALU.add))
                    ch(dve.tensor_scalar(u[:, :], u[:, :], 1.0 / 16, None, ALU.mult))
                    ch(dve.tensor_tensor(cen[:, :, :], a3, sp16(u[:, :]), ALU.subtract))
                    ch(dve.tensor_tensor(sq[:, :, :], cen[:, :, :], cen[:, :, :], ALU.mult))
                    ch(dve.tensor_reduce(z[:, :], sq[:, :, :], AX, ALU.add))
                    ch(dve.tensor_scalar(z[:, :], z[:, :], 1.0 / 16, LN_EPS, ALU.mult, ALU.add))
                    dve.sem_inc(shifted, 1)
                    dve.wait_ge(exped, 1)
                    ch(dve.reciprocal(z[:, :], z[:, :]))
                    ch(dve.tensor_tensor(cen[:, :, :], cen[:, :, :], sp16(z[:, :]), ALU.mult))
                    dve.wait_ge(loaded, 32)
                    ch(dve.tensor_tensor(cen[:, :, :], cen[:, :, :], across(gam[:, :]), ALU.mult))
                    ch(dve.tensor_tensor(cen[:, :, :], cen[:, :, :], across(bet[:, :]), ALU.add))
                    v4 = cen[:, :, :].rearrange("p t (h e) -> p t e h", e=E)
                    ch(dve.tensor_reduce(s[:, :, :], v4, AX, ALU.add))
                    ch(dve.tensor_scalar(s[:, :, :], s[:, :, :], 0.25, None, ALU.mult))
                else:
                    ch(dve.tensor_copy(s[:, :, :], lg))
                if mode in ("softmax2", "normalised"):
                    ch(dve.tensor_reduce(m1[:, :], s[:, :, :], AX, ALU.max))
                    ch(dve.tensor_tensor(t1[:, :, :], s[:, :, :], sp3(m1[:, :]), ALU.subtract))
                    dve.sem_inc(shifted, 1)
                    dve.wait_ge(exped, 1)
                    ch(dve.tensor_reduce(u[:, :], t1[:, :, :], AX, ALU.add))
                    ch(dve.reciprocal(z[:, :], u[:, :]))
                    ch(dve.tensor_tensor(s[:, :, :], t1[:, :, :], sp3(z[:, :]), ALU.mult))

                def best(m, oh):
                    ch(dve.tensor_reduce(m[:, :], s[:, :, :], AX, ALU.max))
                    ch(dve.tensor_tensor(t1[:, :, :], s[:, :, :], sp3(m[:, :]), ALU.is_lt))
                    ch(dve.tensor_scalar(t1[:, :, :], t1[:, :, :], float(E), None, ALU.mult))
                    ch(dve.tensor_tensor(t1[:, :, :], t1[:, :, :], io, ALU.add))
                    ch(dve.tensor_reduce(i1[:, :], t1[:, :, :], AX, ALU.min))
                    ch(dve.tensor_tensor(oh[:, :, :], io, sp3(i1[:, :]), ALU.is_equal))

                best(m1, oh1)
                ch(dve.scalar_tensor_tensor(s[:, :, :].rearrange("p t e -> p (t e)"), oh1[:, :, :].rearrange("p t e -> p (t e)"), FLOOR,
                                            s[:, :, :].rearrange("p t e -> p (t e)"), ALU.mult, ALU.add))
                best(m2, oh2)
                if mode == "mask":
                    ch(dve.tensor_tensor(g, oh1[:, :, :], oh2[:, :, :], ALU.add))
                    return
                if mode in ("softmax", "softmax2"):
                    ch(dve.tensor_tensor(u[:, :], m2[:, :], m1[:, :], ALU.subtract))
                    dve.sem_inc(shifted, 1)
                    dve.wait_ge(exped, 2)
                    ch(dve.tensor_scalar(z[:, :], u[:, :], 1.0, None, ALU.add))
                    ch(dve.reciprocal(w1[:, :], z[:, :]))
                    ch(dve.tensor_tensor(w2[:, :], u[:, :], w1[:, :], ALU.mult))
                else:
                    ch(dve.tensor_tensor(u[:, :], m2[:, :], m1[:, :], ALU.add))
                    ch(dve.tensor_scalar(u[:, :], u[:, :], 1e-12, None, ALU.max))
                    ch(dve.reciprocal(z[:, :], u[:, :]))
                    ch(dve.tensor_tensor(w1[:, :], m1[:, :], z[:, :], ALU.mult))
                    ch(dve.tensor_tensor(w2[:, :], m2[:, :], z[:, :], ALU.mult))
                ch(dve.tensor_tensor(oh1[:, :, :], oh1[:, :, :], sp3(w1[:, :]), ALU.mult))
                ch(dve.tensor_tensor(oh2[:, :, :], oh2[:, :, :], sp3(w2[:, :]), ALU.mult))
                ch(dve.tensor_tensor(g, oh1[:, :, :], oh2[:, :, :], ALU.add))

            @block.scalar
            def _(act):
                n = 0
                if agg is not None:
                    n += 1
                    act.wait_ge(shifted, n)
                    act.activation(z[:, :], z[:, :], ACT.Sqrt).then_inc(exped, 1)
                if mode in ("softmax2", "normalised"):
                    n += 1
                    act.wait_ge(shifted, n)
                    act.activation(t1[:, :, :], t1[:, :, :], ACT.Exp).then_inc(exped, 1)
                if mode in ("softmax", "softmax2"):
                    n += 1
                    act.wait_ge(shifted, n)
                    act.activation(u[:, :], u[:, :], ACT.Exp).then_inc(exped, 1)


def experts(nc, c, name, E, func, layers):
    inner, (w_last, b_last) = layers[:-1], layers[-1]
    C = U
    HALVES = ((0, 3), (3, 5))
    turns = c.NT // C
    NL = len(inner)
    sizes = [w.shape[2] // P for w, _ in inner]
    HT = sizes[-1]
    with stage(nc, name) as st:
        sb, sem = st.sb, st.sem
        w = [sb(f"w{l}", [P, 2, wl.shape[1] // P, wl.shape[2]]) for l, (wl, _) in enumerate(inner)]
        wl_sb = sb("w_last", [P, 2, HT, D])
        b = [sb(f"b{l}", [P, 2, sizes[l]]) for l in range(NL)]
        b_sb = sb("b_last", [1, 2, 2, D])
        h = [sb(f"h{l}", [P, sizes[l] if l < NL - 1 else 2, C * P]) for l in range(NL)]
        loaded = [sem("loaded_a"), sem("loaded_b")]
        product = sem("product")
        hidden = sem("hidden")
        added = sem("added")
        used = sem("used")
        chain_sem = sem("chain")
        ps = c.psum
        per_turn = sum(sizes)
        credits = 2 * turns * HT
        n_loads = 2 * NL + 3
        xt = c.xt[:, :].rearrange("p (t k n) -> p t k n", k=KT, n=P)

        with nc.Block() as block:

            @block.sync
            def _(sp):
                with nc.allow_non_contiguous_dma(reason="biases, one column per block"), sp.Fori(0, E // 2) as pair:
                    for a in range(2):
                        e = pair * 2 + a
                        when(sp, c, used, (e + 1) * (turns * HT))
                        for l, (wl, bl) in enumerate(inner):
                            sp.dma_start(w[l][:, a, :, :], wl[bass.ds(e, 1), :, :].rearrange("o (k p) n -> p (o k) n", p=P)).then_inc(loaded[a], 16)
                            sp.dma_start(b[l][:, a, :], bl[bass.ds(e, 1), :].rearrange("o (k p) -> p (o k)", p=P)).then_inc(loaded[a], 16)
                        sp.dma_start(wl_sb[:, a, :, :], w_last[bass.ds(e, 1), :, :].rearrange("o (k p) n -> p (o k) n", p=P)).then_inc(loaded[a], 16)
                        for r in range(2):
                            sp.dma_start(b_sb[:, a, r, :], b_last[bass.ds(e, 1), :]).then_inc(loaded[a], 16)

            @block.tensor
            def _(pe):
                pe.sem_inc(used, credits)
                with pe.Fori(0, E // 2) as pair:
                    for a in range(2):
                        e = pair * 2 + a
                        when(pe, c, loaded[a], (pair + 1) * (16 * n_loads))
                        with pe.Fori(0, turns) as i:
                            turn = e * turns + i
                            q = 0

                            def outputs(m):
                                when(pe, c, hidden, turn * per_turn + (2 + per_turn - HT + m + 1))
                                if m == 0:
                                    when(pe, c, added, turn + 1)
                                    for y in range(3):
                                        n = min(2, C - 2 * y)
                                        pe.matmul(ps[:, 4 + y, 0:n * D], c.ones[0:1, :],
                                                  b_sb[:, a, 0:n, :].rearrange("o r d -> o (r d)"), start=True, stop=False,
                                                  skip_group_check=True)
                                for j in range(C):
                                    ins = pe.matmul(ps[:, 4 + j // 2, (j % 2) * D:(j % 2 + 1) * D],
                                                    h[-1][:, m % 2, j * P:(j + 1) * P], wl_sb[:, a, m, :],
                                                    start=False, stop=(m == HT - 1), skip_group_check=True)
                                ins.then_inc(used, 1)

                            for l in range(NL):
                                for m in range(sizes[l]):
                                    when(pe, c, hidden, turn * per_turn + (q + 1))
                                    if l:
                                        when(pe, c, hidden, turn * per_turn + (2 + sizes[0]) )
                                    kn = w[l].shape[2]
                                    for y, (lo, hi) in enumerate(HALVES):
                                        for k in range(kn):
                                            rhs = (xt[:, bass.ds(i * C + lo, hi - lo), k, :] if l == 0
                                                   else h[l - 1][:, k, lo * P:hi * P])
                                            ins = pe.matmul(ps[:, 2 * (q % 2) + y, 0:(hi - lo) * P], w[l][:, a, k, m * P:(m + 1) * P],
                                                            rhs, start=(k == 0), stop=(k == kn - 1))
                                    ins.then_inc(product, 1)
                                    q += 1
                                    if l == NL - 1 and m >= 1:
                                        outputs(m - 1)
                            outputs(HT - 1)

            @block.scalar
            def _(act):
                act.sem_inc(hidden, 2)
                with act.Fori(0, E // 2) as pair:
                    for a in range(2):
                        e = pair * 2 + a
                        with act.Fori(0, turns) as i:
                            turn = e * turns + i
                            q = 0
                            for l in range(NL):
                                for m in range(sizes[l]):
                                    when(act, c, product, turn * per_turn + (q + 1))
                                    if l == NL - 1:
                                        when(act, c, used, turn * HT + (credits + m - 1))
                                    for y, (lo, hi) in enumerate(HALVES):
                                        ins = act.activation(h[l][:, m % 2 if l == NL - 1 else m, lo * P:hi * P],
                                                             ps[:, 2 * (q % 2) + y, 0:(hi - lo) * P], func,
                                                             bias=b[l][:, a, m:m + 1])
                                    ins.then_inc(hidden, 1)
                                    q += 1

            @block.vector
            def _(dve):
                ch = Chain(dve, chain_sem)
                dve.sem_inc(added, 1)
                with dve.Fori(0, E // 2) as pair:
                    for a in range(2):
                        e = pair * 2 + a
                        with dve.Fori(0, turns) as i:
                            ch.restart()
                            when(dve, c, used, (e * turns + i + 1) * HT + credits)
                            for j in range(C):
                                t = i * C + j
                                target = c.x[:, bass.ds(t * D, D)]
                                ch.add(dve.scalar_tensor_tensor(target, ps[:, 4 + j // 2, (j % 2) * D:(j % 2 + 1) * D],
                                                                c.g[:, bass.ds(t * 8 + e, 1)], target, ALU.mult, ALU.add))
                            ch.join()
                            dve.sem_inc(added, 1)
                ch.restart()


def gnn_transformer_kernel(nc, a, out):
    c = Core()
    c.N = a["x"].shape[0]
    c.NT = -(-c.N // P)
    NT = c.NT
    tail = c.N - (NT - 1) * P
    rows_of = lambda w: nc.dram_tensor(f"rows_{w}_{nc.next_id()}", (NT * P, w), F32, kind="Internal").ap()

    def blocks_of(edges):
        return -(-edges // SLOTS) + NT + 4

    with ExitStack() as ctx:
        def sb(name, shape, dt=F32):
            return ctx.enter_context(nc.sbuf_tensor(name, shape, dt))

        c.x = sb("x", [P, NT * D])
        c.xt = sb("xt", [P, NT * D])
        c.er = sb("er", [P, NT * 8])
        c.lg = sb("lg", [P, NT * 8])
        c.g = sb("g", [P, NT * 8])
        agg = sb("agg", [P, NT * 16])
        wmat = sb("wmat", [P, KT, D])
        c.ident, c.before, c.ones = sb("ident", [P, P]), sb("before", [P, P]), sb("ones", [P, P])
        c.iota, iota_i = sb("iota", [P, D]), sb("iota_i", [P, D], I32)
        base_main, base_gate = sb("base_main", [1, NT + 1], I32), sb("base_gate", [1, NT + 1], I32)
        c.psum = ctx.enter_context(nc.psum_tensor("ps", [P, 8, 512], F32))
        c.passed = nc.alloc_semaphore("passed")
        E_main, E_gate = a["src"].shape[0], a["L1_ffn_edge_index"].shape[1]
        table_main = nc.dram_tensor("table_main", (blocks_of(E_main) * P * SLOTS, 2), I32, kind="Internal").ap()
        table_gate = nc.dram_tensor("table_gate", (blocks_of(E_gate) * P * SLOTS, 2), I32, kind="Internal").ap()

        with stage(nc, "begin") as st:
            loaded, counted, cleared, filled = (st.sem(n) for n in ("loaded", "counted", "cleared", "filled"))
            with nc.Block() as block:

                @block.sync
                def _(sp):
                    sp.dma_start(c.x[:, 0:(NT - 1) * D].rearrange("p (t d) -> p t d", d=D),
                                 a["x"][0:(NT - 1) * P, :].rearrange("(t p) d -> p t d", p=P)).then_inc(loaded, 16)
                    sp.wait_ge(cleared, 1)
                    sp.dma_start(c.x[0:tail, (NT - 1) * D:NT * D], a["x"][(NT - 1) * P:c.N, :]).then_inc(loaded, 16)
                    sp.wait_ge(loaded, 32)
                    sp.sem_inc(c.passed, 1)

                @block.vector
                def _(dve):
                    dve.memset(c.x[:, (NT - 1) * D:NT * D], 0.0).then_inc(cleared, 1)
                    dve.memset(c.ones[:, :], 1.0)
                    dve.wait_ge(counted, 1)
                    dve.tensor_copy(c.iota[:, :], iota_i[:, :])

                @block.gpsimd
                def _(pool):
                    pool.iota(iota_i[:, :], pattern=[[1, D]], base=0, channel_multiplier=0).then_inc(counted, 1)
                    pool.memset(c.ident[:, :], 0.0).then_inc(filled, 1)
                    pool.memset(c.before[:, :], 1.0).then_inc(filled, 1)
                    pool.wait_ge(filled, 2)
                    pool.affine_select(out=c.ident[:, :], in_=c.ident[:, :], compare_op=ALU.not_equal, fill=1.0,
                                       base=0, pattern=[[-1, P]], channel_multiplier=1)
                    pool.affine_select(out=c.before[:, :], in_=c.before[:, :], compare_op=ALU.is_gt, fill=0.0,
                                       base=0, pattern=[[1, P]], channel_multiplier=-1)

        build_edge_table(nc, c, "main", a["dst"], a["src"], a["edge_weight"].bitcast(I32), E_main, 17, table_main, base_main)
        gate_src, gate_dst = a["L1_ffn_edge_index"][0, :], a["L1_ffn_edge_index"][1, :]
        build_edge_table(nc, c, "gate", gate_dst, gate_src, gate_src, E_gate, 16, table_gate, base_gate)

        by_block = lambda w: w.rearrange("(k p) n -> p k n", p=P)

        for l in range(2):
            rows = rows_of(D + 1)
            prepare(nc, c, f"l0p{l}", c.xt if l else c.x, by_block(a["L0_gnn_W"][l]), D, norm=(l == 0),
                    attend=(1, a["L0_gnn_attn_l"][l], a["L0_gnn_attn_r"][l]), rows=rows)
            attend_edges(nc, c, f"l0a{l}", table_main, base_main, rows, 1, D, loops=True, bias=a["L0_gnn_bias"][l],
                         relu=(l == 0), out=c.x if l else c.xt, add=(l == 1))
        prepare(nc, c, "l0f", c.x, by_block(a["L0_ffn_Wg"]), 8, bias=[(0, a["L0_ffn_bg"])], scores=c.lg, keep_xt=True)
        gate(nc, c, "l0g", 8, "mask")
        experts(nc, c, "l0e", 8, ACT.Gelu, [(a["L0_ffn_W1"], a["L0_ffn_b1"]), (a["L0_ffn_W2"], a["L0_ffn_b2"])])

        set_weights(nc, c, "l1w", table_main, base_main, wmat)
        prepare(nc, c, "l1p", c.x, None, D, ready=wmat, add=True)
        rows = rows_of(16 + 4)
        flat = lambda v: v.rearrange("h d -> (h d)")
        prepare(nc, c, "l1f", c.x, by_block(a["L1_ffn_W_gat"]), 16,
                attend=(4, flat(a["L1_ffn_att_src"]), flat(a["L1_ffn_att_dst"])), rows=rows, keep_xt=True)
        attend_edges(nc, c, "l1a", table_gate, base_gate, rows, 4, 4, loops=True, tiny=1e-16, bias=a["L1_ffn_b_gat"], out=agg)
        gate(nc, c, "l1g", 4, "softmax", agg=agg, gamma=a["L1_ffn_ln_gamma"], beta=a["L1_ffn_ln_beta"])
        experts(nc, c, "l1e", 4, ACT.Gelu, [(a["L1_ffn_W1"], a["L1_ffn_b1"]), (a["L1_ffn_W2"], a["L1_ffn_b2"])])

        rows = rows_of(2 * D)
        prepare(nc, c, "l2p", c.x, (a["L2_gnn_W_self"], a["L2_gnn_W_nb"]), 2 * D, transposed=True,
                bias=[(0, a["L2_gnn_b_self"]), (D, a["L2_gnn_b_nb"])], rows=rows, xn_rows=True, neighbours=c.xt)
        attend_edges(nc, c, "l2a", table_main, base_main, rows, D, 1, neighbours=c.xt, fallback=True, out=c.x, add=True)
        prepare(nc, c, "l2f", c.x, a["L2_ffn_router_w2"], 6, bias=[(0, a["L2_ffn_router_b2"])],
                hidden=(a["L2_ffn_router_w1"], a["L2_ffn_router_b1"]), scores=c.lg, keep_xt=True)
        gate(nc, c, "l2g", 6, "softmax2")
        experts(nc, c, "l2e", 6, ACT.Relu, [(a["L2_ffn_expert_w1"], a["L2_ffn_expert_b1"]),
                                            (a["L2_ffn_expert_w2"], a["L2_ffn_expert_b2"]),
                                            (a["L2_ffn_expert_w3"], a["L2_ffn_expert_b3"])])

        rows = rows_of(D + 8)
        prepare(nc, c, "l3p", c.x, a["L3_gnn_W"].rearrange("(k p) h d -> p k (h d)", p=P), D,
                attend=(8, flat(a["L3_gnn_att_src"]), flat(a["L3_gnn_att_dst"])), rows=rows)
        attend_edges(nc, c, "l3a", table_main, base_main, rows, 8, D // 8, tiny=1e-16, bias=a["L3_gnn_bias"], relu=True,
                     out=c.x, add=True)
        prepare(nc, c, "l3f", c.x, a["L3_ffn_router_w"].rearrange("e (k p) -> p k e", p=P), 8, scores=c.lg, keep_xt=True,
                add_xn=True)
        gate(nc, c, "l3g", 8, "normalised")
        experts(nc, c, "l3e", 8, ACT.Gelu, [(a["L3_ffn_w1"], a["L3_ffn_b1"]), (a["L3_ffn_w2"], a["L3_ffn_b2"])])

        with stage(nc, "end") as st:
            stored = st.sem("stored")
            with nc.Block() as block:

                @block.sync
                def _(sp):
                    sp.dma_start(out[0:(NT - 1) * P, :].rearrange("(t p) d -> p t d", p=P),
                                 c.x[:, 0:(NT - 1) * D].rearrange("p (t d) -> p t d", d=D)).then_inc(stored, 16)
                    sp.dma_start(out[(NT - 1) * P:c.N, :], c.x[0:tail, (NT - 1) * D:NT * D]).then_inc(stored, 16)
                    sp.wait_ge(stored, 32)


def kernel(**inputs):
    import numpy as _np
    import concourse.bacc as _bacc
    from concourse import mybir as _mybir
    from concourse.bass_utils import run_bass_kernel_spmd as _run

    nc = _bacc.Bacc("TRN2", target_bir_lowering=False, num_devices=1)
    arrays, args = {}, {}
    for name, value in inputs.items():
        v = _np.ascontiguousarray(value)
        arrays[f"in_{name}_dram"] = v
        args[name] = nc.dram_tensor(f"in_{name}_dram", v.shape, _mybir.dt.from_np(v.dtype), kind="ExternalInput").ap()
    out = nc.dram_tensor("out_0_dram", tuple(inputs["x"].shape), _mybir.dt.float32, kind="ExternalOutput").ap()
    gnn_transformer_kernel(nc, args, out)
    r = _run(nc, [arrays], core_ids=[0])
    return r.results[0]["out_0_dram"]
```

```python
from contextlib import ExitStack, contextmanager

import concourse.bass as bass
from concourse import mybir

ALU = mybir.AluOpType
ACT = mybir.ActivationFunctionType
F32 = mybir.dt.float32
I32 = mybir.dt.int32
U32 = mybir.dt.uint32
AX = mybir.AxisListType.X

P = 128
D = 256
KT = D // P
LN_EPS = 1e-5
SLOPE = 0.2
U = 5
SLOTS = 8
DIGITS = 4
BUFFERS = 4
AT_ONCE = 8
NODE_BITS = 12
LO_BITS = 6
LO = 1 << LO_BITS
DROPPED = 4095
NOBODY = 8191
FLOOR = -1e30
START = -1e25


class Core:
    pass


class Stage:

    def __init__(self, nc, name):
        self.nc, self.name = nc, name
        self.stack = ExitStack()
        self.sems = []

    def sb(self, name, shape, dt=F32):
        return self.stack.enter_context(self.nc.sbuf_tensor(f"{self.name}_{name}", shape, dt))

    def sem(self, name):
        s = self.nc.alloc_semaphore(f"{self.name}_{name}")
        self.sems.append(s)
        return s


@contextmanager
def stage(nc, name):
    st = Stage(nc, name)
    yield st
    st.stack.close()
    nc.clear_and_free_semaphores(st.sems)
    nc.all_engine_barrier()


class Chain:

    def __init__(self, eng, sem):
        self.eng, self.sem, self.n = eng, sem, 0

    def __call__(self, ins):
        self.n += 1
        ins.then_inc(self.sem, 1)
        self.eng.wait_ge(self.sem, self.n)

    def add(self, ins):
        self.n += 1
        ins.then_inc(self.sem, 1)

    def join(self):
        self.eng.wait_ge(self.sem, self.n)

    def restart(self):
        self.eng.sem_clear(self.sem)
        self.n = 0


def when(eng, c, sem, value):
    eng.wait_ge(sem, value)
    eng.sem_inc(c.passed, 1)



def build_edge_table(nc, c, name, dst, src, weight, edges, half, table, base_row):
    NT = c.NT
    F = -(-edges // P)
    whole = edges // F
    rest = edges - whole * F
    turns = F // (2 * half)
    assert turns * 2 * half == F
    HI = 2 * NT
    rows = table.shape[0]
    sorted_lo = nc.dram_tensor(f"{name}_sorted_lo", (1 + P * F, 2), I32, kind="Internal").ap()

    with stage(nc, name) as st:
        sb, sem = st.sb, st.sem
        dst_i, src_i = sb("dst_i", [P, F], I32), sb("src_i", [P, F], I32)
        pay = sb("pay", [P, F, 2], I32)
        prev = sb("prev", [P, F, 2], I32)
        digit, other = sb("digit", [P, F]), sb("other", [P, F])
        eq, run, pos, keep = sb("eq", [P, F]), sb("run", [P, F]), sb("pos", [P, F]), sb("keep", [P, F])
        pos_i = sb("pos_i", [P, F], I32)
        tmp_i = sb("tmp_i", [P, F], I32)
        eqs, runs = sb("eqs", [P, DIGITS, F]), sb("runs", [P, U, F])
        pay_s, pos_s = sb("pay_s", [P, 2, half, 2], I32), sb("pos_s", [P, 2, half], I32)
        cnt, base = sb("cnt", [P, LO]), sb("base", [P, LO])
        tot, cum = sb("tot", [P, LO]), sb("cum", [P, LO])
        last, allsame = sb("last", [P, LO]), sb("allsame", [P, LO])
        last_t, same_t, carry_t, peak_t = (sb(n, [LO, P]) for n in ("last_t", "same_t", "carry_t", "peak_t"))
        peak = sb("peak", [LO, 2])
        before_i, before_f = sb("before_i", [P, 1], I32), sb("before_f", [P, 1])
        ordered, step, apart, descents = (sb(n, [P, 1]) for n in ("ordered", "step", "apart", "descents"))
        turns_f, turns_i = sb("turns_f", [1, 4]), sb("turns_i", [1, 4], I32)
        row, row2, row3 = sb("row", [1, LO]), sb("row2", [1, LO]), sb("row3", [1, LO])
        row_i = sb("row_i", [1, LO], I32)
        bases = sb("bases", [P, NT + 1])
        empty = sb("empty", [P, AT_ONCE * SLOTS, 2], I32)
        zrow = sb("zrow", [1, 2], I32)
        loaded, chain_sem, stored, counted = (sem(n) for n in ("loaded", "chain", "stored", "counted"))
        staged, sent, free = ([[sem(f"{n}_{second}{a}") for a in "ab"] for second in range(2)] for n in ("staged", "sent", "free"))
        packed, checked, judged, known = sem("packed"), sem("checked"), sem("judged"), sem("known")
        reloaded, based, emptied, cleared, mm = sem("reloaded"), sem("based"), sem("emptied"), sem("cleared"), sem("mm")
        ps = c.psum

        with nc.Block() as block:

            @block.sync
            def _(sp):
                def rows_of(tile, ap):
                    sp.wait_ge(cleared, 2)
                    sp.dma_start(tile[0:whole, :], ap[0:whole * F].rearrange("(p f) -> p f", f=F)).then_inc(loaded, 16)
                    if rest:
                        sp.dma_start(tile[whole:whole + 1, 0:rest],
                                     ap[whole * F:edges].rearrange("(a f) -> a f", a=1)).then_inc(loaded, 16)

                rows_of(dst_i, dst)
                rows_of(src_i, src)
                rows_of(tmp_i, weight)
                held = min(whole, P - 1)
                sp.dma_start(before_i[1:1 + held, :],
                             dst[0:held * F].rearrange("(p f) -> p f", f=F)[:, F - 1:F], allow_slow_non_contiguous=True).then_inc(loaded, 16)
                sp.dma_start(sorted_lo[0:1, :], zrow[:, :]).then_inc(stored, 16)

                def relay(second, n):
                    for a in range(2):
                        sp.sem_inc(free[second][a], 1)
                    with sp.Fori(0, n) as i:
                        for a in range(2):
                            when(sp, c, sent[second][a], (i + 1) * (16 * half))
                            sp.sem_inc(free[second][a], 1)

                sp.wait_ge(packed, 1)
                sp.dma_start(sorted_lo[1:1 + P * F, :].rearrange("(p f) w -> p f w", f=F), pay[:, :, :]).then_inc(stored, 16)
                sp.wait_ge(stored, 32)
                sp.wait_ge(known, 1)
                relay(0, sp.value_load(turns_i[0:1, 2:3], min_val=1, max_val=turns))
                sp.dma_start(pay[:, :, :], sorted_lo[1:1 + P * F, :].rearrange("(p f) w -> p f w", f=F)).then_inc(reloaded, 16)
                sp.dma_start(prev[:, :, :], sorted_lo[0:P * F, :].rearrange("(p f) w -> p f w", f=F)).then_inc(reloaded, 16)
                sp.wait_ge(based, 1)
                n = sp.value_load(base_row[0:1, NT:NT + 1], min_val=1, max_val=rows // (P * SLOTS) - (2 * BUFFERS + AT_ONCE))
                with sp.Fori(0, (n + (2 * BUFFERS - 1 + AT_ONCE)) // AT_ONCE) as b:
                    sp.dma_start(table[bass.ds(b * (AT_ONCE * P * SLOTS), AT_ONCE * P * SLOTS), :].rearrange(
                        "(p s) w -> p s w", s=AT_ONCE * SLOTS), empty[:, :, :]).then_inc(stored, 16)
                sp.wait_ge(stored, (n + (2 * BUFFERS - 1 + AT_ONCE)) // AT_ONCE * 16 + 32)
                sp.sem_inc(emptied, 1)
                relay(1, turns)

            @block.vector
            def _(dve):
                ch = Chain(dve, chain_sem)
                dve.memset(dst_i[:, :], DROPPED).then_inc(cleared, 1)
                dve.memset(src_i[:, :], 0)
                dve.memset(zrow[:, :], 0)
                dve.memset(before_i[:, :], 0)
                dve.memset(cnt[:, :], 0.0)
                dve.memset(empty[:, :, :], NOBODY)
                dve.memset(pos[:, :], 0.0)
                ch(dve.memset(tmp_i[:, :], 0))
                dve.sem_inc(cleared, 1)
                dve.wait_ge(loaded, (112 if rest else 64))
                ch(dve.tensor_scalar(other[:, :], src_i[:, :], float(c.N - 1), None, ALU.min))
                ch(dve.tensor_scalar(digit[:, :], dst_i[:, :], float(DROPPED), float(1 << NODE_BITS), ALU.min, ALU.mult))
                ch(dve.tensor_tensor(other[:, :], digit[:, :], other[:, :], ALU.add))
                ch.add(dve.tensor_copy(pay[:, :, 0], other[:, :]))
                ch.add(dve.tensor_copy(pay[:, :, 1], tmp_i[:, :]))
                ch(dve.tensor_scalar(digit[:, :], dst_i[:, :], float(DROPPED), None, ALU.min))
                dve.sem_inc(packed, 1)
                ch(dve.tensor_scalar(before_f[:, :], before_i[:, :], float(DROPPED), None, ALU.min))
                ch.add(dve.tensor_tensor(eq[:, 0:1], before_f[:, :], digit[:, 0:1], ALU.is_gt))
                ch(dve.tensor_tensor(eq[:, 1:F], digit[:, 0:F - 1], digit[:, 1:F], ALU.is_gt))
                ch(dve.tensor_reduce(descents[:, :], eq[:, :], AX, ALU.max))
                dve.sem_inc(checked, 1)
                dve.wait_ge(judged, 1)
                ch(dve.tensor_scalar(ordered[:, :], ps[:, 6, 0:1], 0.0, None, ALU.is_equal))
                ch.add(dve.tensor_scalar(step[:, :], ordered[:, :], float(LO), None, ALU.mult))
                ch.add(dve.tensor_scalar(apart[:, :], ordered[:, :], float(1 << 20), None, ALU.mult))
                for k, n in enumerate((LO // DIGITS, -(-HI // DIGITS), turns)):
                    ch.add(dve.tensor_scalar(turns_f[:, k:k + 1], ordered[0:1, :], float(1 - n), float(n), ALU.mult, ALU.add))
                ch.join()
                ch(dve.tensor_copy(turns_i[:, 0:3], turns_f[:, 0:3]))
                dve.sem_inc(known, 3)
                n_lo = dve.value_load(turns_i[0:1, 0:1], min_val=1, max_val=LO // DIGITS)
                n_hi = dve.value_load(turns_i[0:1, 1:2], min_val=1, max_val=-(-HI // DIGITS))
                n_turns = dve.value_load(turns_i[0:1, 2:3], min_val=1, max_val=turns)
                ch(dve.tensor_copy(dst_i[:, :], digit[:, :]))
                ch(dve.tensor_scalar(src_i[:, :], dst_i[:, :], LO - 1, None, ALU.bitwise_and))
                ch(dve.tensor_copy(digit[:, :], src_i[:, :]))
                ch(dve.memset(keep[:, :], 1.0))
                spans = lambda ap: ap.unsqueeze(1).broadcast_to([P, DIGITS, F])

                def mark(b):
                    ch(dve.tensor_tensor(eqs[:, :, :], spans(digit[:, :]), c.iota[:, bass.ds(b * DIGITS, DIGITS)].unsqueeze(
                        2).broadcast_to([P, DIGITS, F]), ALU.is_equal))

                with dve.Fori(0, n_lo) as b:
                    ch.restart()
                    mark(b)
                    ch(dve.tensor_reduce(cnt[:, bass.ds(b * DIGITS, DIGITS)], eqs[:, :, :], AX, ALU.add))
                ch.restart()
                dve.sem_inc(counted, 1)
                dve.wait_ge(mm, 1)
                ch(dve.tensor_copy(tot[:, :], ps[:, 1, 0:LO]))
                ch(dve.tensor_tensor_scan(cum[:, :], keep[:, 0:LO], tot[:, :], 0.0, ALU.mult, ALU.add))
                ch(dve.tensor_tensor(cum[:, :], cum[:, :], tot[:, :], ALU.subtract))
                ch(dve.tensor_tensor(base[:, :], cum[:, :], ps[:, 0, 0:LO], ALU.add))

                def positions(n):
                    with dve.Fori(0, n) as b:
                        ch.restart()
                        mark(b)
                        for k in range(DIGITS):
                            ch.add(dve.tensor_tensor_scan(runs[:, k, :], keep[:, :], eqs[:, k, :],
                                                          base[:, bass.ds(b * DIGITS + k, 1)], ALU.mult, ALU.add))
                        ch.join()
                        for k in range(DIGITS):
                            ch(dve.copy_predicated(pos[:, :], eqs[:, k, :].bitcast(I32), runs[:, k, :]))
                    ch.restart()

                def stage_out(second, n):
                    with dve.Fori(0, n) as i:
                        ch.restart()
                        for a in range(2):
                            when(dve, c, free[second][a], i + 1)
                            col = i * (2 * half) + a * half
                            ch.add(dve.tensor_copy(pay_s[:, a, :, :], pay[:, bass.ds(col, half), :]))
                            ch.add(dve.tensor_copy(pos_s[:, a, :], pos_i[:, bass.ds(col, half)]))
                            ch.join()
                            dve.sem_inc(staged[second][a], 1)
                    ch.restart()

                positions(n_lo)
                ch(dve.tensor_scalar(pos[:, :], pos[:, :], apart[:, :], None, ALU.add))
                ch(dve.tensor_copy(pos_i[:, :], pos[:, :]))
                stage_out(0, n_turns)
                dve.wait_ge(reloaded, 32)
                ch(dve.tensor_scalar(dst_i[:, :], pay[:, :, 0], NODE_BITS, LO - 1, ALU.logical_shift_right, ALU.bitwise_and))
                ch(dve.tensor_scalar(src_i[:, :], prev[:, :, 0], NODE_BITS, LO - 1, ALU.logical_shift_right, ALU.bitwise_and))
                ch.add(dve.tensor_copy(other[:, :], dst_i[:, :]))
                ch.add(dve.tensor_copy(eq[:, :], src_i[:, :]))
                ch.join()
                ch.add(dve.tensor_scalar(tmp_i[:, :], pay[:, :, 0], NODE_BITS + LO_BITS, None, ALU.logical_shift_right))
                ch.add(dve.tensor_scalar(dst_i[:, :], prev[:, :, 0], NODE_BITS + LO_BITS, None, ALU.logical_shift_right))
                ch.join()
                ch.add(dve.tensor_copy(digit[:, :], tmp_i[:, :]))
                ch.add(dve.tensor_copy(run[:, :], dst_i[:, :]))
                ch.join()
                ch.add(dve.scalar_tensor_tensor(other[:, :], digit[:, :], step[:, :], other[:, :], ALU.mult, ALU.add))
                ch.add(dve.scalar_tensor_tensor(eq[:, :], run[:, :], step[:, :], eq[:, :], ALU.mult, ALU.add))
                ch.join()
                ch(dve.tensor_tensor(keep[:, :], other[:, :], eq[:, :], ALU.is_equal))
                ch(dve.tensor_scalar(before_f[:, :], ordered[:, :], -1.0, 1.0, ALU.mult, ALU.add))
                ch(dve.tensor_scalar(digit[:, :], digit[:, :], before_f[:, :], None, ALU.mult))
                ch(dve.memset(last[:, :], 0.0))
                ch(dve.tensor_reduce(cum[:, 0:1], keep[:, :], AX, ALU.min))
                ch(dve.tensor_copy(allsame[:, :], cum[:, 0:1].broadcast_to([P, LO])))
                with dve.Fori(0, n_hi) as b:
                    ch.restart()
                    mark(b)
                    for k in range(DIGITS):
                        ch.add(dve.tensor_tensor_scan(runs[:, k, :], keep[:, :], eqs[:, k, :], 0.0, ALU.mult, ALU.add))
                    ch.join()
                    ch(dve.tensor_copy(last[:, bass.ds(b * DIGITS, DIGITS)], runs[:, 0:DIGITS, F - 1]))
                ch.restart()
                dve.sem_inc(counted, 1)
                dve.wait_ge(mm, 2)
                ch.add(dve.tensor_copy(last_t[:, :], ps[0:LO, 0, 0:P]))
                ch.add(dve.tensor_copy(same_t[:, :], ps[0:LO, 1, 0:P]))
                ch(dve.memset(carry_t[:, 0:1], 0.0))
                ch(dve.tensor_tensor_scan(carry_t[:, 1:P], same_t[:, 0:P - 1], last_t[:, 0:P - 1], 0.0, ALU.mult, ALU.add))
                dve.sem_inc(counted, 1)
                dve.wait_ge(mm, 3)
                ch(dve.tensor_copy(base[:, :], ps[:, 2, 0:LO]))
                ch(dve.memset(pos[:, :], 1.0))
                ch(dve.memset(cnt[:, :], 0.0))
                positions(n_hi)
                ch(dve.tensor_scalar(tmp_i[:, :], pay[:, :, 0], NODE_BITS + 7, None, ALU.logical_shift_right))
                ch(dve.tensor_copy(digit[:, :], tmp_i[:, :]))
                with dve.Fori(0, NT // U) as b:
                    ch.restart()
                    for k in range(U):
                        ch.add(dve.scalar_tensor_tensor(runs[:, k, :], digit[:, :], c.iota[:, bass.ds(b * U + k, 1)], pos[:, :],
                                                        ALU.is_equal, ALU.mult))
                    ch.join()
                    ch(dve.tensor_reduce(cnt[:, bass.ds(b * U, U)], runs[:, :, :], AX, ALU.max))
                ch.restart()
                dve.sem_inc(counted, 1)
                dve.wait_ge(mm, 4)
                ch(dve.tensor_copy(peak_t[:, :], ps[0:LO, 3, 0:P]))
                ch(dve.tensor_reduce(peak[:, 0:1], peak_t[:, :], AX, ALU.max))
                dve.sem_inc(counted, 1)
                dve.wait_ge(mm, 5)
                ch(dve.tensor_copy(row2[:, 0:NT], ps[0:1, 4, 0:NT]))
                ch(dve.tensor_scalar(row2[:, 0:NT], row2[:, 0:NT], float(SLOTS + 1), float(SLOTS - 1), ALU.max, ALU.add))
                ch(dve.tensor_copy(row_i[:, 0:NT], row2[:, 0:NT]))
                ch(dve.tensor_scalar(row_i[:, 0:NT], row_i[:, 0:NT], SLOTS.bit_length() - 1, None, ALU.logical_shift_right))
                ch(dve.tensor_copy(row2[:, 0:NT], row_i[:, 0:NT]))
                ch(dve.memset(row3[:, 0:1], 0.0))
                ch(dve.memset(row[:, :], 1.0))
                ch(dve.tensor_tensor_scan(row3[:, 1:NT + 1], row[:, 0:NT], row2[:, 0:NT], 0.0, ALU.mult, ALU.add))
                ch(dve.tensor_copy(base_row[:, 0:NT + 1], row3[:, 0:NT + 1]))
                dve.sem_inc(counted, 1)
                dve.sem_inc(based, 1)
                dve.wait_ge(mm, 6)
                ch(dve.tensor_copy(bases[:, :], ps[:, 5, 0:NT + 1]))
                ch(dve.tensor_scalar(pos[:, :], pos[:, :], -1.0, None, ALU.add))
                ch(dve.tensor_copy(pos_i[:, :], pos[:, :]))
                ch(dve.tensor_scalar(tmp_i[:, :], pos_i[:, :], SLOTS - 1, None, ALU.bitwise_and))
                ch(dve.tensor_copy(run[:, :], tmp_i[:, :]))
                ch(dve.tensor_tensor(pos[:, :], pos[:, :], run[:, :], ALU.subtract))
                ch(dve.scalar_tensor_tensor(pos[:, :], pos[:, :], float(P), run[:, :], ALU.mult, ALU.add))
                ch(dve.tensor_scalar(tmp_i[:, :], pay[:, :, 0], NODE_BITS, P - 1, ALU.logical_shift_right, ALU.bitwise_and))
                ch(dve.tensor_copy(run[:, :], tmp_i[:, :]))
                ch(dve.scalar_tensor_tensor(pos[:, :], run[:, :], float(SLOTS), pos[:, :], ALU.mult, ALU.add))
                ch(dve.tensor_scalar(run[:, :], digit[:, :], float(NT), float(rows), ALU.is_ge, ALU.mult))
                ch(dve.tensor_tensor(pos[:, :], pos[:, :], run[:, :], ALU.add))
                with dve.Fori(0, NT // U) as b:
                    ch.restart()
                    for k in range(U):
                        t = b * U + k
                        ch.add(dve.tensor_scalar(runs[:, k, :], digit[:, :], c.iota[:, bass.ds(t, 1)], bases[:, bass.ds(t, 1)],
                                                 ALU.is_equal, ALU.mult))
                    ch.join()
                    for k in range(U):
                        ch(dve.scalar_tensor_tensor(pos[:, :], runs[:, k, :], float(P * SLOTS), pos[:, :], ALU.mult, ALU.add))
                ch.restart()
                ch(dve.tensor_copy(pos_i[:, :], pos[:, :]))
                ch(dve.tensor_scalar(tmp_i[:, :], pay[:, :, 0], (1 << NODE_BITS) - 1, None, ALU.bitwise_and))
                ch(dve.tensor_copy(pay[:, :, 0], tmp_i[:, :]))
                stage_out(1, turns)

            @block.tensor
            def _(pe):
                pe.wait_ge(checked, 1)
                pe.matmul(ps[:, 6, 0:1], c.ones[:, :], descents[:, :], start=True, stop=True).then_inc(judged, 1)
                pe.wait_ge(counted, 1)
                pe.matmul(ps[:, 0, 0:LO], c.before[:, :], cnt[:, :], start=True, stop=True)
                pe.matmul(ps[:, 1, 0:LO], c.ones[:, :], cnt[:, :], start=True, stop=True).then_inc(mm, 1)
                pe.wait_ge(counted, 2)
                pe.transpose(ps[0:LO, 0, 0:P], last[:, :], c.ident[:, :])
                pe.transpose(ps[0:LO, 1, 0:P], allsame[:, :], c.ident[:, :]).then_inc(mm, 1)
                pe.wait_ge(counted, 3)
                pe.transpose(ps[:, 2, 0:LO], carry_t[:, :], c.ident[0:LO, 0:LO]).then_inc(mm, 1)
                pe.wait_ge(counted, 4)
                pe.transpose(ps[0:LO, 3, 0:P], cnt[:, :], c.ident[:, :]).then_inc(mm, 1)
                pe.wait_ge(counted, 5)
                pe.transpose(ps[0:1, 4, 0:LO], peak[:, 0:1], c.ident[0:LO, 0:LO]).then_inc(mm, 1)
                pe.wait_ge(counted, 6)
                pe.matmul(ps[:, 5, 0:NT + 1], c.ones[0:1, :], row3[:, 0:NT + 1], start=True, stop=True).then_inc(mm, 1)

            @block.gpsimd
            def _(pool):
                pool.wait_ge(known, 1)
                n_turns = pool.value_load(turns_i[0:1, 2:3], min_val=1, max_val=turns)
                for second in range(2):
                    if second:
                        pool.wait_ge(emptied, 1)
                    with pool.Fori(0, turns if second else n_turns) as i:
                        for a in range(2):
                            when(pool, c, staged[second][a], i + 1)
                            for k in range(half):
                                pool.indirect_dma_start(
                                    out=(table[:, :] if second else sorted_lo[:, :]),
                                    out_offset=bass.IndirectOffsetOnAxis(ap=pos_s[:, a, k:k + 1].bitcast(U32), axis=0),
                                    in_=pay_s[:, a, k, :], in_offset=None,
                                    bounds_check=rows - 1 if second else P * F, oob_is_err=False).then_inc(sent[second][a], 16)
                pool.wait_ge(sent[1][0], 16 * half * turns)
                pool.wait_ge(sent[1][1], 16 * half * turns)
                pool.sem_inc(c.passed, 1)



def normalise(dve, ch, c, src, i, stats, moments, rstd, xn, varied, rooted):
    for j in range(U):
        ch.add(dve.bn_stats(stats[:, j, :], src[:, bass.ds((i * U + j) * D, D)]))
    ch.join()
    for j in range(U):
        ch.add(dve.bn_aggr(moments[:, j, :], stats[:, j, :]))
    ch.join()
    ch(dve.tensor_scalar(rstd[:, :], moments[:, :, 1], LN_EPS, None, ALU.add))
    dve.sem_inc(varied, 1)
    when(dve, c, rooted, i + 1)
    ch(dve.reciprocal(rstd[:, :], rstd[:, :]))
    for j in range(U):
        ch.add(dve.tensor_scalar(xn[:, j, :], src[:, bass.ds((i * U + j) * D, D)], moments[:, j, 0:1], rstd[:, j:j + 1],
                                 ALU.subtract, ALU.mult))
    ch.join()


def prepare(nc, c, name, src, weights, width, norm=True, bias=None, attend=None, transposed=False,
            hidden=None, rows=None, xn_rows=False, scores=None, neighbours=None, keep_xt=False, add=False, ready=None, add_xn=False):
    NB = c.NT // U
    H = attend[0] if attend else 0
    N = width + 2 * H
    row_width = (width + H) if not xn_rows else 2 * D
    with stage(nc, name) as st:
        sb, sem = st.sb, st.sem
        w = ready if ready is not None else sb("w", [P, KT, N])
        stats, moments, rstd = sb("stats", [P, U, 6]), sb("moments", [P, U, 2]), sb("rstd", [P, U])
        xn, xt = sb("xn", [P, U, D]), sb("xt", [P, U, D])
        out_rows = sb("rows", [P, U, row_width]) if rows is not None else None
        if attend:
            vec = sb("vec", [P, 2, width])
            prod = sb("prod", [P, width])
        if transposed:
            raw = sb("raw", [P, 2, KT, D])
        bias_row = sb("bias", [1, N]) if bias is not None else None
        if hidden:
            w1 = sb("w1", [P, KT, P])
            b1 = sb("b1", [P, 1])
            hid = sb("hid", [P, U, P])
        chain_sem, loaded, weighed, flipped_w = (sem(n) for n in ("chain", "loaded", "weighed", "flipped_w"))
        normed = sem("normed")
        flipped = sem("flipped")
        turned = sem("turned")
        kept = sem("kept")
        multiplied = sem("multiplied")
        taken = sem("taken")
        evacuated = sem("evacuated")
        filled = sem("filled")
        sent = sem("sent")
        stored = sem("stored")
        hidden_in, hidden_out = sem("hidden_in"), sem("hidden_out")
        varied, rooted = sem("varied"), sem("rooted")
        warmed, warm = sb("warmed", [P, 1]), sem("warm")
        ps = c.psum
        loads = []
        if ready is None and not transposed:
            if hidden:
                loads.append((w[:, 0, 0:width], weights))
            else:
                loads += [(w[:, k, 0:width], weights[:, k, :]) for k in range(KT)]
        if transposed:
            for a in range(2):
                loads.append((raw[:, a, :, :], weights[a].rearrange("(k p) n -> p k n", p=P)))
        if attend:
            for a in range(2):
                loads.append((vec[:, a, :], attend[1 + a].rearrange("(o n) -> o n", o=1).broadcast_to([P, width])))
        if bias is not None:
            for off, b in bias:
                loads.append((bias_row[:, off:off + b.shape[0]], b.rearrange("(o n) -> o n", o=1)))
        if hidden:
            loads.append((w1[:, :, :], hidden[0].rearrange("(k p) n -> p k n", p=P)))
            loads.append((b1[:, :], hidden[1].rearrange("(p o) -> p o", o=1)))

        with nc.Block() as block:

            @block.sync
            def _(sp):
                with nc.allow_non_contiguous_dma(reason="small weights, loaded once"):
                    for tile, source in loads:
                        sp.dma_start(tile, source).then_inc(loaded, 16)
                if rows is not None:
                    sp.sem_inc(stored, 1)
                    with sp.Fori(0, NB) as i:
                        if xn_rows:
                            when(sp, c, filled, i + 1)
                        when(sp, c, evacuated, (i + 2) * U)
                        sp.dma_start(rows[bass.ds(i * (U * P), U * P), 0:row_width].rearrange("(j p) w -> p j w", p=P),
                                     out_rows[:, :, :]).then_inc(sent, 16)
                        when(sp, c, sent, (i + 1) * 16)
                        sp.sem_inc(stored, 1)

            @block.vector
            def _(dve):
                ch = Chain(dve, chain_sem)
                dve.sem_inc(taken, U)
                if norm:
                    dve.memset(warmed[:, :], 0.0).then_inc(warm, 1)
                if loads:
                    dve.wait_ge(loaded, 16 * len(loads))
                if attend:
                    for a in range(2):
                        for k in range(KT):
                            ch(dve.tensor_tensor(prod[:, :], w[:, k, 0:width], vec[:, a, :], ALU.mult))
                            ch(dve.tensor_reduce(w[:, k, width + a * H:width + (a + 1) * H],
                                                 prod[:, :].rearrange("p (h d) -> p h d", h=H), AX, ALU.add))
                if transposed:
                    for a in range(2):
                        dve.wait_ge(flipped_w, a + 1)
                        for k in range(KT):
                            ch(dve.tensor_copy(w[:, k, a * D:(a + 1) * D], ps[:, 2 * a + k, 0:D]))
                dve.sem_inc(weighed, 1)
                ch.restart()

                def normed_turn(i):
                    when(dve, c, flipped, i + 1)
                    if norm:
                        normalise(dve, ch, c, src, i, stats, moments, rstd, xn, varied, rooted)
                    else:
                        ch(dve.tensor_copy(xn[:, :, :].rearrange("p u d -> p (u d)"), src[:, bass.ds(i * (U * D), U * D)]))
                    dve.sem_inc(normed, 1)
                    if add_xn:
                        whole = c.x[:, bass.ds(i * (U * D), U * D)]
                        ch(dve.tensor_tensor(whole, whole, xn[:, :, :].rearrange("p u d -> p (u d)"), ALU.add))
                    if xn_rows:
                        when(dve, c, stored, i + 1)
                        ch(dve.tensor_copy(out_rows[:, :, D:2 * D], xn[:, :, :]))
                        dve.sem_inc(filled, 1)

                def taken_turn(i):
                    for j in range(U):
                        t = i * U + j
                        when(dve, c, evacuated, t + U + 1) if rows is not None else when(dve, c, multiplied, t + 1)
                        if attend:
                            ch(dve.tensor_copy(c.er[:, bass.ds(t * 8, H)], ps[:, 3 + j, width + H:width + 2 * H]))
                        if neighbours is not None:
                            ch(dve.tensor_copy(neighbours[:, bass.ds(t * D, D)], ps[:, 3 + j, D:2 * D]))
                        if scores is not None:
                            ch(dve.tensor_copy(scores[:, bass.ds(t * 8, width)], ps[:, 3 + j, 0:width]))
                        if add:
                            ch(dve.tensor_tensor(c.x[:, bass.ds(t * D, D)], ps[:, 3 + j, 0:D], c.x[:, bass.ds(t * D, D)], ALU.add))
                        dve.sem_inc(taken, 1)

                normed_turn(0)
                with dve.Fori(0, NB - 1) as i:
                    ch.restart()
                    normed_turn(i + 1)
                    taken_turn(i)
                ch.restart()
                taken_turn(NB - 1)
                ch.restart()

            @block.tensor
            def _(pe):
                pe.sem_inc(flipped, 1)
                if transposed:
                    pe.wait_ge(loaded, 16 * len(loads))
                    for a in range(2):
                        for k in range(KT):
                            for n in range(KT):
                                ins = pe.transpose(ps[:, 2 * a + k, n * P:(n + 1) * P], raw[:, a, n, k * P:(k + 1) * P], c.ident[:, :])
                        ins.then_inc(flipped_w, 1)
                pe.wait_ge(weighed, 1)

                def transposes(i):
                    when(pe, c, normed, i + 1)
                    when(pe, c, turned, i + 1)
                    for j in range(U):
                        for k in range(KT):
                            ins = pe.transpose(ps[:, j // 2, (j % 2) * D + k * P:(j % 2) * D + (k + 1) * P],
                                               xn[:, j, k * P:(k + 1) * P], c.ident[:, :])
                    ins.then_inc(flipped, 1)

                def products(i):
                    when(pe, c, turned, i + 2)
                    if hidden:
                        for j in range(U):
                            when(pe, c, taken, i * U + j + 1)
                            for k in range(KT):
                                ins = pe.matmul(ps[:, 3 + j, 0:P], w1[:, k, :], xt[:, j, k * P:(k + 1) * P],
                                                start=(k == 0), stop=(k == KT - 1))
                            ins.then_inc(hidden_in, 1)
                    for j in range(U):
                        t = i * U + j
                        if hidden:
                            when(pe, c, hidden_out, t + 1)
                            pe.matmul(ps[:, 3 + j, 0:N], hid[:, j, :], w[:, 0, 0:N], start=True, stop=False)
                        else:
                            when(pe, c, taken, t + 1)
                            if rows is not None:
                                when(pe, c, evacuated, t + 1)
                            for k in range(KT):
                                ins = pe.matmul(ps[:, 3 + j, 0:N], xt[:, j, k * P:(k + 1) * P], w[:, k, 0:N],
                                                start=(k == 0), stop=(k == KT - 1 and bias is None))
                        if bias is not None:
                            ins = pe.matmul(ps[:, 3 + j, 0:N], c.ones[0:1, :], bias_row[:, :], start=False, stop=True)
                        ins.then_inc(multiplied, 1)

                transposes(0)
                with pe.Fori(0, NB - 1) as i:
                    transposes(i + 1)
                    products(i)
                products(NB - 1)

            @block.scalar
            def _(act):
                act.sem_inc(turned, 1)
                if norm:
                    act.wait_ge(warm, 1)
                    act.activation(warmed[:, :], warmed[:, :], ACT.Sqrt)
                if rows is not None:
                    act.sem_inc(evacuated, U)

                def roots(i):
                    if norm:
                        when(act, c, varied, i + 1)
                        act.activation(rstd[:, :], rstd[:, :], ACT.Sqrt).then_inc(rooted, 1)

                def copies(i):
                    when(act, c, flipped, i + 2)
                    if keep_xt:
                        when(act, c, kept, i + 1)
                    for q in range(3):
                        n = min(2, U - 2 * q)
                        ins = act.activation(xt[:, 2 * q:2 * q + n, :].rearrange("p u d -> p (u d)"), ps[:, q, 0:n * D], ACT.Copy)
                    ins.then_inc(turned, 1)

                def products_out(i):
                    if hidden:
                        for j in range(U):
                            when(act, c, hidden_in, i * U + j + 1)
                            act.activation(hid[:, j, :], ps[:, 3 + j, 0:P], ACT.Relu, bias=b1[:, :]).then_inc(hidden_out, 1)
                    if rows is not None:
                        when(act, c, stored, i + 1)
                        for j in range(U):
                            when(act, c, multiplied, i * U + j + 1)
                            n = D if xn_rows else width + H
                            act.activation(out_rows[:, j, 0:n], ps[:, 3 + j, 0:n], ACT.Copy).then_inc(evacuated, 1)

                roots(0)
                copies(0)
                with act.Fori(0, NB - 1) as i:
                    roots(i + 1)
                    products_out(i)
                    when(act, c, multiplied, (i + 1) * U)
                    copies(i + 1)
                products_out(NB - 1)

            @block.gpsimd
            def _(pool):
                if keep_xt:
                    pool.sem_inc(kept, 1)
                    with pool.Fori(0, NB) as i:
                        when(pool, c, turned, i + 2)
                        pool.tensor_copy(c.xt[:, bass.ds(i * (U * D), U * D)], xt[:, :, :].rearrange("p u d -> p (u d)")).then_inc(kept, 1)


def attend_edges(nc, c, name, table, base_row, rows, H, DH, loops=False, tiny=0.0, bias=None, relu=False,
                 out=None, add=False, neighbours=None, fallback=False):
    VW = H * DH
    by_feature = neighbours is not None
    SC = 0 if by_feature else VW
    V0 = D if by_feature else 0
    RW = VW + H
    blocks = table.shape[0] // (P * SLOTS)
    with stage(nc, name) as st:
        sb, sem = st.sb, st.sem
        idx = sb("idx", [P, BUFFERS, SLOTS, 2], I32)
        got = sb("got", [P, BUFFERS * SLOTS * RW])
        self_rows = sb("self_rows", [P, 2 * RW]) if loops or fallback else None
        e = sb("e", [P, SLOTS + 1, H]) if not by_feature else None
        d = sb("d", [P, SLOTS + 1, H])
        p = sb("p", [P, SLOTS + 1, H]) if not by_feature else None
        v = sb("v", [P, SLOTS, VW]) if not by_feature else None
        PV = (SLOTS + 1) * 2 * D
        pv = sb("pv", [P, 2 * PV]) if by_feature else None
        warmed, warm = sb("warmed", [P, 1]), sem("warm")
        top, new, rden = sb("top", [P, H]), sb("new", [P, H]), sb("rden", [P, H])
        both = sb("both", [P, H + VW])
        den, acc = both[:, 0:H], both[:, H:H + VW]
        part = sb("part", [P, VW])
        peak = sb("peak", [P, H]) if by_feature else None
        bias_all = sb("bias", [P, VW]) if bias is not None else None
        chain_sem, loaded = sem("chain"), sem("loaded")
        self_in, self_free = sem("self_in"), sem("self_free")
        idx_in = [sem(f"idx_in_{a}") for a in range(BUFFERS)]
        gathered = [sem(f"got_{a}") for a in range(BUFFERS)]
        arrived = sem("arrived")
        freed = sem("freed")
        shifted, weighed = sem("shifted"), sem("weighed")
        valued, summed = sem("valued"), sem("summed")
        reset = sem("reset")
        need_self = loops or fallback
        ps = c.psum

        def tiles(eng, body, before=None, after=None):
            with eng.Fori(0, c.NT) as t:
                if before:
                    before(t)
                b0 = eng.value_load(base_row[0:1, bass.ds(t, 1)], min_val=0, max_val=blocks - 2)
                b1 = eng.value_load(base_row[0:1, bass.ds(t + 1, 1)], min_val=1, max_val=blocks - 1)
                with eng.Fori(b0, b1) as b:
                    body(t, b)
                if after:
                    after(t, b1)

        def buffer(b, lo, hi):
            rows_b = got[:, bass.ds((b % BUFFERS) * (SLOTS * RW), SLOTS * RW)].rearrange("p (s w) -> p s w", w=RW)
            return rows_b[:, :, lo:hi]

        def weights_of(b):
            return pv[:, bass.ds((b % 2) * PV, PV)].rearrange("p (s two d) -> p s two d", two=2, d=D)

        with nc.Block() as block:

            @block.sync
            def _(sp):
                if bias is not None:
                    sp.dma_start(bias_all[:, :], bias.rearrange("(o n) -> o n", o=1).broadcast_to([P, VW])).then_inc(loaded, 16)
                total = sp.value_load(base_row[0:1, c.NT:c.NT + 1], min_val=1, max_val=blocks - 2 * BUFFERS)

                def load(b, a):
                    sp.dma_start(idx[:, a, :, :], table[bass.ds(b * (P * SLOTS), P * SLOTS), :].rearrange(
                        "(p s) w -> p s w", s=SLOTS)).then_inc(idx_in[a], 16)

                for a in range(BUFFERS):
                    load(a, a)
                with sp.Fori(0, (total + BUFFERS) // BUFFERS) as q:
                    for a in range(BUFFERS):
                        when(sp, c, gathered[a], (q + 1) * (16 * SLOTS))
                        sp.sem_inc(arrived, 1)
                        load(q * BUFFERS + (BUFFERS + a), a)
                for a in range(BUFFERS):
                    when(sp, c, idx_in[a], ((total + BUFFERS) // BUFFERS + 1) * 16)

            @block.gpsimd
            def _(pool):
                total = pool.value_load(base_row[0:1, c.NT:c.NT + 1], min_val=1, max_val=blocks - 2 * BUFFERS)
                with pool.Fori(0, (total + BUFFERS) // BUFFERS) as q:
                    for a in range(BUFFERS):
                        when(pool, c, idx_in[a], (q + 1) * 16)
                        when(pool, c, freed, q * BUFFERS + (a + 1))
                        if by_feature:
                            when(pool, c, reset, q * BUFFERS + (a + 1))
                        for k in range(SLOTS):
                            at = (a * SLOTS + k) * RW
                            pool.indirect_dma_start(
                                out=got[:, at:at + RW], out_offset=None, in_=rows[:, :],
                                in_offset=bass.IndirectOffsetOnAxis(ap=idx[:, a, k, 0:1].bitcast(U32), axis=0),
                                bounds_check=c.N - 1, oob_is_err=False).then_inc(gathered[a], 16)

            @block.scalar
            def _(act):
                act.wait_ge(warm, 1)
                act.activation(warmed[:, :], warmed[:, :], ACT.Exp)
                if by_feature:
                    act.sem_inc(reset, BUFFERS)

                def load_self(t):
                    when(act, c, self_free, t + 1)
                    act.dma_start(self_rows[:, bass.ds((t % 2) * RW, RW)], rows[bass.ds(t * P, P), 0:RW]).then_inc(self_in, 16)

                def exponentials(t, b):
                    when(act, c, shifted, b + 1)
                    act.activation(weights_of(b)[:, :, 0, :] if by_feature else p[:, :, :], d[:, :, :], ACT.Exp).then_inc(weighed, 1)
                    if by_feature:
                        scores = buffer(b, 0, D)
                        act.activation(scores, scores, ACT.Copy, bias=FLOOR, scale=0.0).then_inc(reset, 1)

                def self_landed(t, b1):
                    when(act, c, self_in, (t + 1) * 16)

                tiles(act, exponentials, before=load_self if need_self else None, after=self_landed if need_self else None)

            if by_feature:
                @block.tensor
                def _(pe):
                    pe.wait_ge(loaded, 1)
                    pe.matmul(ps[:, 1, :], c.ident[:, :], pv[:, PV:PV + 2 * D], start=True, stop=True).then_inc(summed, 1)

                    def sums(t, b):
                        for part_of, ready in enumerate((weighed, valued)):
                            when(pe, c, ready, b + 1)
                            bank = (b % 2) * 512 + part_of * D
                            for k in range(SLOTS):
                                ins = pe.matmul(ps[:, :, :].rearrange("p b n -> p (b n)")[:, bass.ds(bank, D)], c.ident[:, :],
                                                pv[:, bass.ds((b % 2) * PV + (k * (2 * D) + part_of * D), D)],
                                                start=(k == 0), stop=(k == SLOTS - 1))
                        ins.then_inc(summed, 1)

                    tiles(pe, sums)

            @block.vector
            def _(dve):
                ch = Chain(dve, chain_sem)
                dve.memset(warmed[:, :], 0.0).then_inc(warm, 1)
                ch(dve.memset(got[:, :], FLOOR))
                if by_feature:
                    ch(dve.memset(pv[:, :], 0.0))
                    dve.sem_inc(loaded, 1)
                dve.sem_inc(self_free, 2)
                dve.sem_inc(freed, BUFFERS)
                if bias is not None:
                    dve.wait_ge(loaded, 16)
                ch.restart()
                by_head = lambda ap: ap.rearrange("p (h d) -> p h d", h=H)
                spread = lambda ap: ap.unsqueeze(2).broadcast_to([P, H, DH])

                own = lambda t, lo, hi: self_rows[:, bass.ds((t % 2) * RW + lo, hi - lo)]

                def largest(b):
                    when(dve, c, arrived, b + 1)
                    ch(dve.tensor_reduce(peak[:, :], buffer(b, 0, D).rearrange("p s w -> p w s"), AX, ALU.max))

                if by_feature:
                    total = dve.value_load(base_row[0:1, c.NT:c.NT + 1], min_val=1, max_val=blocks - 2 * BUFFERS)
                    dve.wait_ge(arrived, 1)
                    ch(dve.tensor_reduce(peak[:, :], got[:, 0:SLOTS * RW].rearrange("p (s w) -> p w s", w=RW)[:, 0:D, :], AX, ALU.max))

                def begin(t):
                    ch.restart()
                    if loops:
                        when(dve, c, self_in, (t + 1) * 16)
                    if loops:
                        ch(dve.tensor_tensor(top[:, :], own(t, SC, SC + H), c.er[:, bass.ds(t * 8, H)], ALU.add))
                        ch.add(dve.scalar_tensor_tensor(e[:, SLOTS, :], top[:, :], SLOPE, top[:, :], ALU.mult, ALU.max))
                        ch.add(dve.memset(den, 1.0))
                        ch.add(dve.tensor_copy(acc, own(t, 0, VW)))
                    else:
                        ch.add(dve.memset(e[:, SLOTS, :], START))
                        ch.add(dve.memset(both[:, :], 0.0))
                    ch.join()

                def by_heads(t, b):
                    ch.restart()
                    when(dve, c, arrived, b + 1)
                    er = c.er[:, bass.ds(t * 8, H)].unsqueeze(1).broadcast_to([P, SLOTS, H])
                    ch(dve.tensor_tensor(e[:, 0:SLOTS, :], buffer(b, SC, SC + H), er, ALU.add))
                    ch(dve.scalar_tensor_tensor(e[:, 0:SLOTS, :], e[:, 0:SLOTS, :], SLOPE, e[:, 0:SLOTS, :], ALU.mult, ALU.max))
                    ch(dve.tensor_reduce(top[:, :], e[:, :, :].rearrange("p s h -> p h s"), AX, ALU.max))
                    ch(dve.tensor_tensor(d[:, :, :], e[:, :, :], top[:, :].unsqueeze(1).broadcast_to([P, SLOTS + 1, H]), ALU.subtract))
                    dve.sem_inc(shifted, 1)
                    ch.add(dve.tensor_copy(e[:, SLOTS, :], top[:, :]))
                    ch.add(dve.tensor_scalar(buffer(b, SC, SC + H), d[:, 0:SLOTS, :], 0.0, FLOOR, ALU.mult, ALU.add))
                    ch.join()
                    when(dve, c, weighed, b + 1)
                    ch.add(dve.tensor_tensor(
                        v[:, :, :].rearrange("p s (h d) -> p s h d", h=H),
                        buffer(b, V0, V0 + VW).rearrange("p s (h d) -> p s h d", h=H),
                        p[:, 0:SLOTS, :].unsqueeze(3).broadcast_to([P, SLOTS, H, DH]), ALU.mult))
                    ch.add(dve.tensor_tensor(by_head(acc), by_head(acc), spread(p[:, SLOTS, :]), ALU.mult))
                    ch.join()
                    dve.sem_inc(freed, 1)
                    ch.add(dve.tensor_tensor(p[:, SLOTS, :], p[:, SLOTS, :], den, ALU.mult))
                    ch.add(dve.tensor_reduce(part[:, :], v[:, :, :].rearrange("p s w -> p w s"), AX, ALU.add))
                    ch.join()
                    ch.add(dve.tensor_reduce(den, p[:, :, :].rearrange("p s h -> p h s"), AX, ALU.add))
                    ch.add(dve.tensor_tensor(acc, acc, part[:, :], ALU.add))
                    ch.join()

                def rescale(b_next):
                    two = both[:, :].rearrange("p (two d) -> p two d", two=2)
                    ch(dve.tensor_tensor(two, two, weights_of(b_next + 1)[:, SLOTS, 0, :].unsqueeze(1).broadcast_to([P, 2, D]), ALU.mult))

                def add_sums(b_next):
                    when(dve, c, summed, b_next + 1)
                    bank = ps[:, :, :].rearrange("p b n -> p (b n)")[:, bass.ds(((b_next + 1) % 2) * 512, 512)]
                    ch(dve.tensor_tensor(both[:, :], bank, both[:, :], ALU.add))

                def by_features(t, b):
                    near = neighbours[:, bass.ds(t * D, D)]
                    ch(dve.tensor_tensor(new[:, :], peak[:, :], near, ALU.add))
                    ch(dve.tensor_tensor(new[:, :], new[:, :], top[:, :], ALU.max))
                    ch.add(dve.tensor_tensor(d[:, SLOTS, :], top[:, :], new[:, :], ALU.subtract))
                    ch.add(dve.tensor_tensor(part[:, :], new[:, :], near, ALU.subtract))
                    ch.join()
                    ch.add(dve.tensor_tensor(d[:, 0:SLOTS, :], buffer(b, 0, D), part[:, :].unsqueeze(1).broadcast_to([P, SLOTS, D]), ALU.subtract))
                    ch.add(dve.tensor_copy(top[:, :], new[:, :]))
                    ch.join()
                    dve.sem_inc(shifted, 1)
                    rescale(b)
                    largest(b + 1)
                    when(dve, c, weighed, b + 1)
                    w_b = weights_of(b)
                    ch.add(dve.tensor_tensor(w_b[:, 0:SLOTS, 1, :], buffer(b, D, 2 * D), w_b[:, 0:SLOTS, 0, :], ALU.mult))
                    ch.join()
                    dve.sem_inc(valued, 1)
                    dve.sem_inc(freed, 1)
                    add_sums(b)

                def finish(t):
                    if by_feature:
                        when(dve, c, self_in, (t + 1) * 16)
                    if fallback:
                        ch(dve.tensor_scalar(new[:, :], den, 0.0, None, ALU.is_equal))
                        ch(dve.tensor_tensor(den, den, new[:, :], ALU.add))
                        ch(dve.tensor_tensor(part[:, :], new[:, :], own(t, V0, V0 + VW), ALU.mult))
                        ch(dve.reciprocal(rden[:, :], den))
                        ch(dve.tensor_tensor(acc, acc, rden[:, :], ALU.mult))
                        ch(dve.tensor_tensor(acc, acc, part[:, :], ALU.add))
                    else:
                        if tiny:
                            ch(dve.tensor_scalar(den, den, tiny, None, ALU.add))
                        ch(dve.reciprocal(rden[:, :], den))
                        ch(dve.tensor_tensor(by_head(acc), by_head(acc), spread(rden[:, :]), ALU.mult))
                    if need_self:
                        dve.sem_inc(self_free, 1)
                    if bias is not None:
                        ch(dve.tensor_tensor(acc, acc, bias_all[:, :], ALU.add))
                    if relu:
                        ch(dve.tensor_scalar(acc, acc, 0.0, None, ALU.max))
                    target = out[:, bass.ds(t * VW, VW)]
                    if add:
                        ch(dve.tensor_tensor(target, target, acc, ALU.add))
                    else:
                        ch(dve.tensor_copy(target, acc))

                def feature_tile(t, tile_before):
                    ch.restart()
                    b0 = dve.value_load(base_row[0:1, bass.ds(t, 1)], min_val=0, max_val=blocks - 2)
                    b1 = dve.value_load(base_row[0:1, bass.ds(t + 1, 1)], min_val=2, max_val=blocks - 1)
                    ch(dve.memset(top[:, :], START))
                    by_features(t, b0)
                    if tile_before is not None:
                        finish(tile_before)
                    ch(dve.memset(both[:, :], 0.0))
                    with dve.Fori(b0 + 1, b1) as b:
                        ch.restart()
                        by_features(t, b)
                    ch.restart()

                def after(t, b1):
                    ch.restart()
                    finish(t)

                if by_feature:
                    ch(dve.memset(both[:, :], 0.0))
                    feature_tile(0, None)
                    with dve.Fori(1, c.NT) as t:
                        feature_tile(t, t - 1)
                    rescale(total)
                    add_sums(total)
                    finish(c.NT - 1)
                else:
                    tiles(dve, by_heads, before=begin, after=after)
                ch.restart()


def set_weights(nc, c, name, edge_table, base_row, wmat):
    blocks = edge_table.shape[0] // (P * SLOTS)
    with stage(nc, name) as st:
        sb, sem = st.sb, st.sem
        blk = sb("blk", [P, SLOTS, 2], I32)
        src = sb("src", [P, SLOTS])
        mask = sb("mask", [P, D])
        wt = sb("wt", [P, KT, D])
        chain_sem, loaded, freed, filled, flipped = (sem(n) for n in ("chain", "loaded", "freed", "filled", "flipped"))
        ps = c.psum
        with nc.Block() as block:

            @block.sync
            def _(sp):
                with sp.Fori(0, KT) as t:
                    b0 = sp.value_load(base_row[0:1, bass.ds(t, 1)], min_val=0, max_val=blocks - 1)
                    b1 = sp.value_load(base_row[0:1, bass.ds(t + 1, 1)], min_val=1, max_val=blocks)
                    with sp.Fori(b0, b1) as b:
                        when(sp, c, freed, b + 1)
                        sp.dma_start(blk[:, :, :], edge_table[bass.ds(b * (P * SLOTS), P * SLOTS), :].rearrange(
                            "(p s) w -> p s w", s=SLOTS)).then_inc(loaded, 16)

            @block.vector
            def _(dve):
                ch = Chain(dve, chain_sem)
                dve.sem_inc(freed, 1)
                ch(dve.memset(wt[:, :, :], 0.0))
                ch.restart()
                for t in range(KT):
                    b0 = dve.value_load(base_row[0:1, t:t + 1], min_val=0, max_val=blocks - 1)
                    b1 = dve.value_load(base_row[0:1, t + 1:t + 2], min_val=1, max_val=blocks)
                    with dve.Fori(b0, b1) as b:
                        ch.restart()
                        when(dve, c, loaded, (b + 1) * 16)
                        ch(dve.tensor_copy(src[:, :], blk[:, :, 0]))
                        for k in range(SLOTS):
                            ch(dve.tensor_scalar(mask[:, :], c.iota[:, 0:D], src[:, k:k + 1], None, ALU.is_equal))
                            ch(dve.copy_predicated(wt[:, t, :], mask[:, :].bitcast(I32), blk[:, k, 1:2].bitcast(F32).broadcast_to([P, D])))
                        dve.sem_inc(freed, 1)
                    ch.restart()
                dve.sem_inc(filled, 1)
                dve.wait_ge(flipped, 1)
                for k in range(KT):
                    ch(dve.tensor_copy(wmat[:, k, :], ps[:, k, 0:D]))

            @block.tensor
            def _(pe):
                pe.wait_ge(filled, 1)
                for k in range(KT):
                    for n in range(KT):
                        ins = pe.transpose(ps[:, k, n * P:(n + 1) * P], wt[:, n, k * P:(k + 1) * P], c.ident[:, :])
                ins.then_inc(flipped, 1)


def gate(nc, c, name, E, mode, agg=None, gamma=None, beta=None):
    NT = c.NT
    with stage(nc, name) as st:
        sb, sem = st.sb, st.sem
        s, t1, oh1, oh2 = (sb(n, [P, NT, E]) for n in ("s", "t1", "oh1", "oh2"))
        m1, m2, i1, u, z, w1, w2 = (sb(n, [P, NT]) for n in ("m1", "m2", "i1", "u", "z", "w1", "w2"))
        chain_sem, shifted, exped, loaded = sem("chain"), sem("shifted"), sem("exped"), sem("loaded")
        if agg is not None:
            W = 16
            cen, sq = sb("cen", [P, NT, W]), sb("sq", [P, NT, W])
            gam, bet = sb("gam", [P, W]), sb("bet", [P, W])
        lg = c.lg[:, :].rearrange("p (t e) -> p t e", e=8)[:, :, 0:E]
        g = c.g[:, :].rearrange("p (t e) -> p t e", e=8)[:, :, 0:E]
        io = c.iota[:, 0:E].unsqueeze(1).broadcast_to([P, NT, E])
        sp3 = lambda ap: ap.unsqueeze(2).broadcast_to([P, NT, E])

        with nc.Block() as block:

            @block.sync
            def _(sp):
                if agg is not None:
                    for tile, v in ((gam, gamma), (bet, beta)):
                        sp.dma_start(tile[:, :], v.rearrange("(o n) -> o n", o=1).broadcast_to([P, 16])).then_inc(loaded, 16)

            @block.vector
            def _(dve):
                ch = Chain(dve, chain_sem)
                if agg is not None:
                    a3 = agg[:, :].rearrange("p (t w) -> p t w", w=16)
                    sp16 = lambda ap: ap.unsqueeze(2).broadcast_to([P, NT, 16])
                    across = lambda ap: ap.unsqueeze(1).broadcast_to([P, NT, 16])
                    ch(dve.tensor_reduce(u[:, :], a3, AX, ALU.add))
                    ch(dve.tensor_scalar(u[:, :], u[:, :], 1.0 / 16, None, ALU.mult))
                    ch(dve.tensor_tensor(cen[:, :, :], a3, sp16(u[:, :]), ALU.subtract))
                    ch(dve.tensor_tensor(sq[:, :, :], cen[:, :, :], cen[:, :, :], ALU.mult))
                    ch(dve.tensor_reduce(z[:, :], sq[:, :, :], AX, ALU.add))
                    ch(dve.tensor_scalar(z[:, :], z[:, :], 1.0 / 16, LN_EPS, ALU.mult, ALU.add))
                    dve.sem_inc(shifted, 1)
                    dve.wait_ge(exped, 1)
                    ch(dve.reciprocal(z[:, :], z[:, :]))
                    ch(dve.tensor_tensor(cen[:, :, :], cen[:, :, :], sp16(z[:, :]), ALU.mult))
                    dve.wait_ge(loaded, 32)
                    ch(dve.tensor_tensor(cen[:, :, :], cen[:, :, :], across(gam[:, :]), ALU.mult))
                    ch(dve.tensor_tensor(cen[:, :, :], cen[:, :, :], across(bet[:, :]), ALU.add))
                    v4 = cen[:, :, :].rearrange("p t (h e) -> p t e h", e=E)
                    ch(dve.tensor_reduce(s[:, :, :], v4, AX, ALU.add))
                    ch(dve.tensor_scalar(s[:, :, :], s[:, :, :], 0.25, None, ALU.mult))
                else:
                    ch(dve.tensor_copy(s[:, :, :], lg))
                if mode in ("softmax2", "normalised"):
                    ch(dve.tensor_reduce(m1[:, :], s[:, :, :], AX, ALU.max))
                    ch(dve.tensor_tensor(t1[:, :, :], s[:, :, :], sp3(m1[:, :]), ALU.subtract))
                    dve.sem_inc(shifted, 1)
                    dve.wait_ge(exped, 1)
                    ch(dve.tensor_reduce(u[:, :], t1[:, :, :], AX, ALU.add))
                    ch(dve.reciprocal(z[:, :], u[:, :]))
                    ch(dve.tensor_tensor(s[:, :, :], t1[:, :, :], sp3(z[:, :]), ALU.mult))

                def best(m, oh):
                    ch(dve.tensor_reduce(m[:, :], s[:, :, :], AX, ALU.max))
                    ch(dve.tensor_tensor(t1[:, :, :], s[:, :, :], sp3(m[:, :]), ALU.is_lt))
                    ch(dve.tensor_scalar(t1[:, :, :], t1[:, :, :], float(E), None, ALU.mult))
                    ch(dve.tensor_tensor(t1[:, :, :], t1[:, :, :], io, ALU.add))
                    ch(dve.tensor_reduce(i1[:, :], t1[:, :, :], AX, ALU.min))
                    ch(dve.tensor_tensor(oh[:, :, :], io, sp3(i1[:, :]), ALU.is_equal))

                best(m1, oh1)
                ch(dve.scalar_tensor_tensor(s[:, :, :].rearrange("p t e -> p (t e)"), oh1[:, :, :].rearrange("p t e -> p (t e)"), FLOOR,
                                            s[:, :, :].rearrange("p t e -> p (t e)"), ALU.mult, ALU.add))
                best(m2, oh2)
                if mode == "mask":
                    ch(dve.tensor_tensor(g, oh1[:, :, :], oh2[:, :, :], ALU.add))
                    return
                if mode in ("softmax", "softmax2"):
                    ch(dve.tensor_tensor(u[:, :], m2[:, :], m1[:, :], ALU.subtract))
                    dve.sem_inc(shifted, 1)
                    dve.wait_ge(exped, 2)
                    ch(dve.tensor_scalar(z[:, :], u[:, :], 1.0, None, ALU.add))
                    ch(dve.reciprocal(w1[:, :], z[:, :]))
                    ch(dve.tensor_tensor(w2[:, :], u[:, :], w1[:, :], ALU.mult))
                else:
                    ch(dve.tensor_tensor(u[:, :], m2[:, :], m1[:, :], ALU.add))
                    ch(dve.tensor_scalar(u[:, :], u[:, :], 1e-12, None, ALU.max))
                    ch(dve.reciprocal(z[:, :], u[:, :]))
                    ch(dve.tensor_tensor(w1[:, :], m1[:, :], z[:, :], ALU.mult))
                    ch(dve.tensor_tensor(w2[:, :], m2[:, :], z[:, :], ALU.mult))
                ch(dve.tensor_tensor(oh1[:, :, :], oh1[:, :, :], sp3(w1[:, :]), ALU.mult))
                ch(dve.tensor_tensor(oh2[:, :, :], oh2[:, :, :], sp3(w2[:, :]), ALU.mult))
                ch(dve.tensor_tensor(g, oh1[:, :, :], oh2[:, :, :], ALU.add))

            @block.scalar
            def _(act):
                n = 0
                if agg is not None:
                    n += 1
                    act.wait_ge(shifted, n)
                    act.activation(z[:, :], z[:, :], ACT.Sqrt).then_inc(exped, 1)
                if mode in ("softmax2", "normalised"):
                    n += 1
                    act.wait_ge(shifted, n)
                    act.activation(t1[:, :, :], t1[:, :, :], ACT.Exp).then_inc(exped, 1)
                if mode in ("softmax", "softmax2"):
                    n += 1
                    act.wait_ge(shifted, n)
                    act.activation(u[:, :], u[:, :], ACT.Exp).then_inc(exped, 1)


def experts(nc, c, name, E, func, layers):
    inner, (w_last, b_last) = layers[:-1], layers[-1]
    C = U
    HALVES = ((0, 3), (3, 5))
    turns = c.NT // C
    NL = len(inner)
    sizes = [w.shape[2] // P for w, _ in inner]
    HT = sizes[-1]
    with stage(nc, name) as st:
        sb, sem = st.sb, st.sem
        w = [sb(f"w{l}", [P, 2, wl.shape[1] // P, wl.shape[2]]) for l, (wl, _) in enumerate(inner)]
        wl_sb = sb("w_last", [P, 2, HT, D])
        b = [sb(f"b{l}", [P, 2, sizes[l]]) for l in range(NL)]
        b_sb = sb("b_last", [1, 2, 2, D])
        h = [sb(f"h{l}", [P, sizes[l] if l < NL - 1 else 2, C * P]) for l in range(NL)]
        loaded = [sem("loaded_a"), sem("loaded_b")]
        product = sem("product")
        hidden = sem("hidden")
        added = sem("added")
        used = sem("used")
        chain_sem = sem("chain")
        ps = c.psum
        per_turn = sum(sizes)
        credits = 2 * turns * HT
        n_loads = 2 * NL + 3
        xt = c.xt[:, :].rearrange("p (t k n) -> p t k n", k=KT, n=P)

        with nc.Block() as block:

            @block.sync
            def _(sp):
                with nc.allow_non_contiguous_dma(reason="biases, one column per block"), sp.Fori(0, E // 2) as pair:
                    for a in range(2):
                        e = pair * 2 + a
                        when(sp, c, used, (e + 1) * (turns * HT))
                        for l, (wl, bl) in enumerate(inner):
                            sp.dma_start(w[l][:, a, :, :], wl[bass.ds(e, 1), :, :].rearrange("o (k p) n -> p (o k) n", p=P)).then_inc(loaded[a], 16)
                            sp.dma_start(b[l][:, a, :], bl[bass.ds(e, 1), :].rearrange("o (k p) -> p (o k)", p=P)).then_inc(loaded[a], 16)
                        sp.dma_start(wl_sb[:, a, :, :], w_last[bass.ds(e, 1), :, :].rearrange("o (k p) n -> p (o k) n", p=P)).then_inc(loaded[a], 16)
                        for r in range(2):
                            sp.dma_start(b_sb[:, a, r, :], b_last[bass.ds(e, 1), :]).then_inc(loaded[a], 16)

            @block.tensor
            def _(pe):
                pe.sem_inc(used, credits)
                with pe.Fori(0, E // 2) as pair:
                    for a in range(2):
                        e = pair * 2 + a
                        when(pe, c, loaded[a], (pair + 1) * (16 * n_loads))
                        with pe.Fori(0, turns) as i:
                            turn = e * turns + i
                            q = 0

                            def outputs(m):
                                when(pe, c, hidden, turn * per_turn + (2 + per_turn - HT + m + 1))
                                if m == 0:
                                    when(pe, c, added, turn + 1)
                                    for y in range(3):
                                        n = min(2, C - 2 * y)
                                        pe.matmul(ps[:, 4 + y, 0:n * D], c.ones[0:1, :],
                                                  b_sb[:, a, 0:n, :].rearrange("o r d -> o (r d)"), start=True, stop=False,
                                                  skip_group_check=True)
                                for j in range(C):
                                    ins = pe.matmul(ps[:, 4 + j // 2, (j % 2) * D:(j % 2 + 1) * D],
                                                    h[-1][:, m % 2, j * P:(j + 1) * P], wl_sb[:, a, m, :],
                                                    start=False, stop=(m == HT - 1), skip_group_check=True)
                                ins.then_inc(used, 1)

                            for l in range(NL):
                                for m in range(sizes[l]):
                                    when(pe, c, hidden, turn * per_turn + (q + 1))
                                    if l:
                                        when(pe, c, hidden, turn * per_turn + (2 + sizes[0]) )
                                    kn = w[l].shape[2]
                                    for y, (lo, hi) in enumerate(HALVES):
                                        for k in range(kn):
                                            rhs = (xt[:, bass.ds(i * C + lo, hi - lo), k, :] if l == 0
                                                   else h[l - 1][:, k, lo * P:hi * P])
                                            ins = pe.matmul(ps[:, 2 * (q % 2) + y, 0:(hi - lo) * P], w[l][:, a, k, m * P:(m + 1) * P],
                                                            rhs, start=(k == 0), stop=(k == kn - 1))
                                    ins.then_inc(product, 1)
                                    q += 1
                                    if l == NL - 1 and m >= 1:
                                        outputs(m - 1)
                            outputs(HT - 1)

            @block.scalar
            def _(act):
                act.sem_inc(hidden, 2)
                with act.Fori(0, E // 2) as pair:
                    for a in range(2):
                        e = pair * 2 + a
                        with act.Fori(0, turns) as i:
                            turn = e * turns + i
                            q = 0
                            for l in range(NL):
                                for m in range(sizes[l]):
                                    when(act, c, product, turn * per_turn + (q + 1))
                                    if l == NL - 1:
                                        when(act, c, used, turn * HT + (credits + m - 1))
                                    for y, (lo, hi) in enumerate(HALVES):
                                        ins = act.activation(h[l][:, m % 2 if l == NL - 1 else m, lo * P:hi * P],
                                                             ps[:, 2 * (q % 2) + y, 0:(hi - lo) * P], func,
                                                             bias=b[l][:, a, m:m + 1])
                                    ins.then_inc(hidden, 1)
                                    q += 1

            @block.vector
            def _(dve):
                ch = Chain(dve, chain_sem)
                dve.sem_inc(added, 1)
                with dve.Fori(0, E // 2) as pair:
                    for a in range(2):
                        e = pair * 2 + a
                        with dve.Fori(0, turns) as i:
                            ch.restart()
                            when(dve, c, used, (e * turns + i + 1) * HT + credits)
                            for j in range(C):
                                t = i * C + j
                                target = c.x[:, bass.ds(t * D, D)]
                                ch.add(dve.scalar_tensor_tensor(target, ps[:, 4 + j // 2, (j % 2) * D:(j % 2 + 1) * D],
                                                                c.g[:, bass.ds(t * 8 + e, 1)], target, ALU.mult, ALU.add))
                            ch.join()
                            dve.sem_inc(added, 1)
                ch.restart()


def gnn_transformer_kernel(nc, a, out):
    c = Core()
    c.N = a["x"].shape[0]
    c.NT = -(-c.N // P)
    NT = c.NT
    tail = c.N - (NT - 1) * P
    rows_of = lambda w: nc.dram_tensor(f"rows_{w}_{nc.next_id()}", (NT * P, w), F32, kind="Internal").ap()

    def blocks_of(edges):
        return -(-edges // SLOTS) + 2 * NT + 2 * BUFFERS + AT_ONCE

    with ExitStack() as ctx:
        def sb(name, shape, dt=F32):
            return ctx.enter_context(nc.sbuf_tensor(name, shape, dt))

        c.x = sb("x", [P, NT * D])
        c.xt = sb("xt", [P, NT * D])
        c.er = sb("er", [P, NT * 8])
        c.lg = sb("lg", [P, NT * 8])
        c.g = sb("g", [P, NT * 8])
        agg = sb("agg", [P, NT * 16])
        wmat = sb("wmat", [P, KT, D])
        c.ident, c.before, c.ones = sb("ident", [P, P]), sb("before", [P, P]), sb("ones", [P, P])
        c.iota, iota_i = sb("iota", [P, D]), sb("iota_i", [P, D], I32)
        base_main, base_gate = sb("base_main", [1, NT + 1], I32), sb("base_gate", [1, NT + 1], I32)
        c.psum = ctx.enter_context(nc.psum_tensor("ps", [P, 8, 512], F32))
        c.passed = nc.alloc_semaphore("passed")
        E_main, E_gate = a["src"].shape[0], a["L1_ffn_edge_index"].shape[1]
        table_main = nc.dram_tensor("table_main", (blocks_of(E_main) * P * SLOTS, 2), I32, kind="Internal").ap()
        table_gate = nc.dram_tensor("table_gate", (blocks_of(E_gate) * P * SLOTS, 2), I32, kind="Internal").ap()

        with stage(nc, "begin") as st:
            loaded, counted, cleared, filled = (st.sem(n) for n in ("loaded", "counted", "cleared", "filled"))
            with nc.Block() as block:

                @block.sync
                def _(sp):
                    sp.dma_start(c.x[:, 0:(NT - 1) * D].rearrange("p (t d) -> p t d", d=D),
                                 a["x"][0:(NT - 1) * P, :].rearrange("(t p) d -> p t d", p=P)).then_inc(loaded, 16)
                    sp.wait_ge(cleared, 1)
                    sp.dma_start(c.x[0:tail, (NT - 1) * D:NT * D], a["x"][(NT - 1) * P:c.N, :]).then_inc(loaded, 16)
                    sp.wait_ge(loaded, 32)
                    sp.sem_inc(c.passed, 1)

                @block.vector
                def _(dve):
                    dve.memset(c.x[:, (NT - 1) * D:NT * D], 0.0).then_inc(cleared, 1)
                    dve.memset(c.ones[:, :], 1.0)
                    dve.wait_ge(counted, 1)
                    dve.tensor_copy(c.iota[:, :], iota_i[:, :])

                @block.gpsimd
                def _(pool):
                    pool.iota(iota_i[:, :], pattern=[[1, D]], base=0, channel_multiplier=0).then_inc(counted, 1)
                    pool.memset(c.ident[:, :], 0.0).then_inc(filled, 1)
                    pool.memset(c.before[:, :], 1.0).then_inc(filled, 1)
                    pool.wait_ge(filled, 2)
                    pool.affine_select(out=c.ident[:, :], in_=c.ident[:, :], compare_op=ALU.not_equal, fill=1.0,
                                       base=0, pattern=[[-1, P]], channel_multiplier=1)
                    pool.affine_select(out=c.before[:, :], in_=c.before[:, :], compare_op=ALU.is_gt, fill=0.0,
                                       base=0, pattern=[[1, P]], channel_multiplier=-1)

        build_edge_table(nc, c, "main", a["dst"], a["src"], a["edge_weight"].bitcast(I32), E_main, 17, table_main, base_main)
        gate_src, gate_dst = a["L1_ffn_edge_index"][0, :], a["L1_ffn_edge_index"][1, :]
        build_edge_table(nc, c, "gate", gate_dst, gate_src, gate_src, E_gate, 16, table_gate, base_gate)

        by_block = lambda w: w.rearrange("(k p) n -> p k n", p=P)

        for l in range(2):
            rows = rows_of(D + 1)
            prepare(nc, c, f"l0p{l}", c.xt if l else c.x, by_block(a["L0_gnn_W"][l]), D, norm=(l == 0),
                    attend=(1, a["L0_gnn_attn_l"][l], a["L0_gnn_attn_r"][l]), rows=rows)
            attend_edges(nc, c, f"l0a{l}", table_main, base_main, rows, 1, D, loops=True, bias=a["L0_gnn_bias"][l],
                         relu=(l == 0), out=c.x if l else c.xt, add=(l == 1))
        prepare(nc, c, "l0f", c.x, by_block(a["L0_ffn_Wg"]), 8, bias=[(0, a["L0_ffn_bg"])], scores=c.lg, keep_xt=True)
        gate(nc, c, "l0g", 8, "mask")
        experts(nc, c, "l0e", 8, ACT.Gelu, [(a["L0_ffn_W1"], a["L0_ffn_b1"]), (a["L0_ffn_W2"], a["L0_ffn_b2"])])

        set_weights(nc, c, "l1w", table_main, base_main, wmat)
        prepare(nc, c, "l1p", c.x, None, D, ready=wmat, add=True)
        rows = rows_of(16 + 4)
        flat = lambda v: v.rearrange("h d -> (h d)")
        prepare(nc, c, "l1f", c.x, by_block(a["L1_ffn_W_gat"]), 16,
                attend=(4, flat(a["L1_ffn_att_src"]), flat(a["L1_ffn_att_dst"])), rows=rows, keep_xt=True)
        attend_edges(nc, c, "l1a", table_gate, base_gate, rows, 4, 4, loops=True, tiny=1e-16, bias=a["L1_ffn_b_gat"], out=agg)
        gate(nc, c, "l1g", 4, "softmax", agg=agg, gamma=a["L1_ffn_ln_gamma"], beta=a["L1_ffn_ln_beta"])
        experts(nc, c, "l1e", 4, ACT.Gelu, [(a["L1_ffn_W1"], a["L1_ffn_b1"]), (a["L1_ffn_W2"], a["L1_ffn_b2"])])

        rows = rows_of(2 * D)
        prepare(nc, c, "l2p", c.x, (a["L2_gnn_W_self"], a["L2_gnn_W_nb"]), 2 * D, transposed=True,
                bias=[(0, a["L2_gnn_b_self"]), (D, a["L2_gnn_b_nb"])], rows=rows, xn_rows=True, neighbours=c.xt)
        attend_edges(nc, c, "l2a", table_main, base_main, rows, D, 1, neighbours=c.xt, fallback=True, out=c.x, add=True)
        prepare(nc, c, "l2f", c.x, a["L2_ffn_router_w2"], 6, bias=[(0, a["L2_ffn_router_b2"])],
                hidden=(a["L2_ffn_router_w1"], a["L2_ffn_router_b1"]), scores=c.lg, keep_xt=True)
        gate(nc, c, "l2g", 6, "softmax2")
        experts(nc, c, "l2e", 6, ACT.Relu, [(a["L2_ffn_expert_w1"], a["L2_ffn_expert_b1"]),
                                            (a["L2_ffn_expert_w2"], a["L2_ffn_expert_b2"]),
                                            (a["L2_ffn_expert_w3"], a["L2_ffn_expert_b3"])])

        rows = rows_of(D + 8)
        prepare(nc, c, "l3p", c.x, a["L3_gnn_W"].rearrange("(k p) h d -> p k (h d)", p=P), D,
                attend=(8, flat(a["L3_gnn_att_src"]), flat(a["L3_gnn_att_dst"])), rows=rows)
        attend_edges(nc, c, "l3a", table_main, base_main, rows, 8, D // 8, tiny=1e-16, bias=a["L3_gnn_bias"], relu=True,
                     out=c.x, add=True)
        prepare(nc, c, "l3f", c.x, a["L3_ffn_router_w"].rearrange("e (k p) -> p k e", p=P), 8, scores=c.lg, keep_xt=True,
                add_xn=True)
        gate(nc, c, "l3g", 8, "normalised")
        experts(nc, c, "l3e", 8, ACT.Gelu, [(a["L3_ffn_w1"], a["L3_ffn_b1"]), (a["L3_ffn_w2"], a["L3_ffn_b2"])])

        with stage(nc, "end") as st:
            stored = st.sem("stored")
            with nc.Block() as block:

                @block.sync
                def _(sp):
                    sp.dma_start(out[0:(NT - 1) * P, :].rearrange("(t p) d -> p t d", p=P),
                                 c.x[:, 0:(NT - 1) * D].rearrange("p (t d) -> p t d", d=D)).then_inc(stored, 16)
                    sp.dma_start(out[(NT - 1) * P:c.N, :], c.x[0:tail, (NT - 1) * D:NT * D]).then_inc(stored, 16)
                    sp.wait_ge(stored, 32)


def kernel(**inputs):
    import numpy as _np
    import concourse.bacc as _bacc
    from concourse import mybir as _mybir
    from concourse.bass_utils import run_bass_kernel_spmd as _run

    nc = _bacc.Bacc("TRN2", target_bir_lowering=False, num_devices=1)
    arrays, args = {}, {}
    for name, value in inputs.items():
        v = _np.ascontiguousarray(value)
        arrays[f"in_{name}_dram"] = v
        args[name] = nc.dram_tensor(f"in_{name}_dram", v.shape, _mybir.dt.from_np(v.dtype), kind="ExternalInput").ap()
    out = nc.dram_tensor("out_0_dram", tuple(inputs["x"].shape), _mybir.dt.float32, kind="ExternalOutput").ap()
    gnn_transformer_kernel(nc, args, out)
    r = _run(nc, [arrays], core_ids=[0])
    return r.results[0]["out_0_dram"]
```
